# Optimizing a Trainium2 kernel written in Bass

```python
import numpy as np
import jax
import jax.numpy as jnp

def _softmax(x, axis=-1):
    return jax.nn.softmax(x, axis=axis)

def _gelu(x):
    return jax.nn.gelu(x, approximate=True)

def _silu(x):
    return jax.nn.silu(x)

def _sigmoid(x):
    return jax.nn.sigmoid(x)

def _layernorm(x, axis=-1, eps=1e-05):
    m = jnp.mean(x, axis=axis, keepdims=True)
    v = jnp.var(x, axis=axis, keepdims=True)
    return (x - m) / jnp.sqrt(v + eps)

def _scatter_add(tgt, idx, src, axis=0):
    return tgt.at[idx].add(src)

def _segment_sum(src, seg, n):
    return jax.ops.segment_sum(src, seg, n)
kernel_name = 'mk_gnn_resnorm_d4_gnn_r64_0a89d3'

def setup_inputs(seed: int=0):
    np.random.seed(seed)
    _w = jnp.asarray

    def _rec_inputs():
        import jax
        import jax.numpy as jnp
        _gk = jax.random.key(seed)
        x = -0.0001006 + 1 * jax.random.normal(jax.random.fold_in(_gk, 1), (100000, 48), jnp.float32)
        src = jax.random.randint(jax.random.fold_in(_gk, 2), (25000,), 0, 100000, jnp.int32)
        dst = jax.random.randint(jax.random.fold_in(_gk, 3), (25000,), 0, 100000, jnp.int32)
        _o = jnp.argsort(dst, stable=True)
        src = src[_o]
        dst = dst[_o]
        edge_attr_40 = jax.random.uniform(jax.random.fold_in(_gk, 13), (25000, 40), jnp.float32, 0.0, 1)
        edge_attr_48 = -4.21973e-05 + 0.999841 * jax.random.normal(jax.random.fold_in(_gk, 14), (25000, 48), jnp.float32)
        edge_weight = jax.random.uniform(jax.random.fold_in(_gk, 16), (25000,), jnp.float32, 0.0, 6.99999)
        node_type_119 = jax.random.randint(jax.random.fold_in(_gk, 17), (100000,), 0, 119, jnp.int32)
        node_vec = jax.random.uniform(jax.random.fold_in(_gk, 18), (100000,), jnp.float32, 0.0, 1.49999)
        return (x, src, dst, edge_attr_40, edge_attr_48, edge_weight, node_type_119, node_vec)
    x, src, dst, edge_attr_40, edge_attr_48, edge_weight, node_type_119, node_vec = _rec_inputs()

    def _L0_gnn_setup():
        import jax, jax.numpy as jnp
        import numpy as np
        N_NODES = 100000
        N_EDGES = 25000
        D_FEAT = 48
        key = jax.random.key(seed)
        k1, k2, k3, k4 = jax.random.split(key, 4)
        node_feat = jax.random.normal(k1, (N_NODES, D_FEAT), dtype=jnp.float32)
        edge_feat = jax.random.normal(k2, (N_EDGES, D_FEAT), dtype=jnp.float32)
        src = jax.random.randint(k3, (N_EDGES,), 0, N_NODES, dtype=jnp.int32)
        dst = jax.random.randint(k4, (N_EDGES,), 0, N_NODES, dtype=jnp.int32)
        eps = jnp.zeros((1,), dtype=jnp.float32)
        return {'node_feat': node_feat, 'edge_feat': edge_feat, 'src': src, 'dst': dst, 'eps': eps}
    _L0_gnn_all = _L0_gnn_setup()
    _L0_gnn_in = {k: v for k, v in _L0_gnn_all.items() if k in ('eps',)}
    del _L0_gnn_all

    def _L1_gnn_setup():
        import jax, jax.numpy as jnp
        import numpy as np
        N_NODES = 50000
        N_EDGES = 25000
        D_IN = 48
        D_OUT = 48
        key = jax.random.key(seed)
        k1, k2, k3, k4 = jax.random.split(key, 4)
        features = jax.random.normal(k1, (N_NODES, D_IN), dtype=jnp.float32)
        src = jax.random.randint(k2, (N_EDGES,), 0, N_NODES, dtype=jnp.int64)
        dst = jax.random.randint(k3, (N_EDGES,), 0, N_NODES, dtype=jnp.int64)
        std = np.sqrt(2.0 / (D_IN + D_OUT))
        W = jax.random.normal(k4, (D_OUT, D_IN), dtype=jnp.float32) * std
        b = jnp.zeros((D_OUT,), dtype=jnp.float32)
        return {'features': features, 'src': src, 'dst': dst, 'W': W, 'b': b}
    _L1_gnn_all = _L1_gnn_setup()
    _L1_gnn_in = {k: v for k, v in _L1_gnn_all.items() if k in ('W', 'b')}
    del _L1_gnn_all

    def _L2_gnn_setup():
        import jax, jax.numpy as jnp
        import numpy as np
        N_NODES = 100000
        N_EDGES = 25000
        IN_F = 48
        OUT_F = 48
        key = jax.random.key(seed)
        k1, k2, k3, k4 = jax.random.split(key, 4)
        x = jax.random.normal(k1, (N_NODES, IN_F), dtype=jnp.float32)
        edge_index = jax.random.randint(k2, (2, N_EDGES), 0, N_NODES, dtype=jnp.int32)
        bound = 1.0 / np.sqrt(IN_F)
        W = jax.random.uniform(k3, (OUT_F, IN_F), minval=-bound, maxval=bound, dtype=jnp.float32)
        b = jax.random.uniform(k4, (OUT_F,), minval=-bound, maxval=bound, dtype=jnp.float32)
        return {'x': x, 'edge_index': edge_index, 'W': W, 'b': b}
    _L2_gnn_all = _L2_gnn_setup()
    _L2_gnn_in = {k: v for k, v in _L2_gnn_all.items() if k in ('W', 'b')}
    del _L2_gnn_all

    def _L3_gnn_setup():
        import jax, jax.numpy as jnp
        import numpy as np
        CUTOFF = 6.0
        LN_EPS = 1e-05
        key = jax.random.key(seed)
        ks = jax.random.split(key, 16)
        N, E, H, R, NEL, G = (50000, 12500, 48, 40, 119, 32)
        inp = {'h': jax.random.normal(ks[0], (N, H), jnp.float32), 'edge_index': jax.random.randint(ks[1], (2, E), 0, N, jnp.int64), 'edge_attr': jax.random.uniform(ks[2], (E, R), jnp.float32), 'distances': jax.random.uniform(ks[3], (E,), jnp.float32) * 7.0, 'atom_z': jax.random.randint(ks[4], (N,), 0, NEL, jnp.int64), 'node_mult': jax.random.uniform(ks[5], (N,), jnp.float32) + 0.5, 'batch': jnp.zeros((N,), jnp.int64), 'W1': jax.random.normal(ks[6], (H, R), jnp.float32) / np.sqrt(R), 'b1': jax.random.normal(ks[7], (H,), jnp.float32) * 0.01, 'W2': jax.random.normal(ks[8], (H, H), jnp.float32) / np.sqrt(H), 'b2': jax.random.normal(ks[9], (H,), jnp.float32) * 0.01, 'emb': jax.random.normal(ks[10], (NEL, G), jnp.float32) * 0.01, 'adaptW': jax.random.normal(ks[11], (G, G), jnp.float32) * 0.01, 'gamma': jnp.ones((H,), jnp.float32), 'beta': jnp.zeros((H,), jnp.float32)}
        return inp
    _L3_gnn_all = _L3_gnn_setup()
    _L3_gnn_in = {k: v for k, v in _L3_gnn_all.items() if k in ('W1', 'b1', 'W2', 'b2', 'emb', 'adaptW', 'gamma', 'beta')}
    del _L3_gnn_all
    return {'x': x, 'src': src, 'dst': dst, 'edge_attr_40': edge_attr_40, 'edge_attr_48': edge_attr_48, 'edge_weight': edge_weight, 'node_type_119': node_type_119, 'node_vec': node_vec, 'L0_gnn_eps': _L0_gnn_in['eps'], 'L1_gnn_W': _L1_gnn_in['W'], 'L1_gnn_b': _L1_gnn_in['b'], 'L2_gnn_W': _L2_gnn_in['W'], 'L2_gnn_b': _L2_gnn_in['b'], 'L3_gnn_W1': _L3_gnn_in['W1'], 'L3_gnn_b1': _L3_gnn_in['b1'], 'L3_gnn_W2': _L3_gnn_in['W2'], 'L3_gnn_b2': _L3_gnn_in['b2'], 'L3_gnn_emb': _L3_gnn_in['emb'], 'L3_gnn_adaptW': _L3_gnn_in['adaptW'], 'L3_gnn_gamma': _L3_gnn_in['gamma'], 'L3_gnn_beta': _L3_gnn_in['beta']}

def reference(x, src, dst, edge_attr_40, edge_attr_48, edge_weight, node_type_119, node_vec, L0_gnn_eps, L1_gnn_W, L1_gnn_b, L2_gnn_W, L2_gnn_b, L3_gnn_W1, L3_gnn_b1, L3_gnn_W2, L3_gnn_b2, L3_gnn_emb, L3_gnn_adaptW, L3_gnn_gamma, L3_gnn_beta):
    import jax
    import jax.numpy as jnp

    def _L0_gnn_ref(node_feat, edge_feat, src, dst, eps):
        import jax, jax.numpy as jnp
        import numpy as np
        N_NODES = 100000
        N_EDGES = 25000
        D_FEAT = 48
        m = jax.nn.relu(node_feat[src] + edge_feat)
        neigh = jax.ops.segment_sum(m, dst, num_segments=N_NODES)
        return (1.0 + eps[0]) * node_feat + neigh

    def _L1_gnn_ref(features, src, dst, W, b):
        import jax, jax.numpy as jnp
        import numpy as np
        N_NODES = 50000
        N_EDGES = 25000
        D_IN = 48
        D_OUT = 48
        n = features.shape[0]
        ones = jnp.ones(src.shape[0], dtype=features.dtype)
        out_deg = jax.ops.segment_sum(ones, src, num_segments=n)
        in_deg = jax.ops.segment_sum(ones, dst, num_segments=n)
        ci = jax.lax.rsqrt(jnp.maximum(out_deg, 1.0))
        cj = jax.lax.rsqrt(jnp.maximum(in_deg, 1.0))
        msg = features[src] * ci[src][:, None]
        agg = jax.ops.segment_sum(msg, dst, num_segments=n) * cj[:, None]
        h = jnp.where(in_deg[:, None] > 0, agg, features)
        out = jax.nn.relu(h @ W.T + b)
        return out

    def _L2_gnn_ref(x, edge_index, W, b):
        import jax, jax.numpy as jnp
        import numpy as np
        N_NODES = 100000
        N_EDGES = 25000
        IN_F = 48
        OUT_F = 48
        row, col = (edge_index[0], edge_index[1])
        n = x.shape[0]
        deg = jnp.bincount(row, length=n).astype(x.dtype)
        deg_inv_sqrt = jnp.where(deg > 0, jax.lax.rsqrt(jnp.where(deg > 0, deg, 1.0)), 0.0)
        norm = deg_inv_sqrt[row] * deg_inv_sqrt[col]
        msg = norm[:, None] * x[col]
        agg = jax.ops.segment_sum(msg, row, num_segments=n)
        out = agg @ W.T + b
        return jax.nn.relu(out)

    def _L3_gnn_ref(h, edge_index, edge_attr, distances, atom_z, node_mult, batch, W1, b1, W2, b2, emb, adaptW, gamma, beta):
        import jax, jax.numpy as jnp
        import numpy as np
        CUTOFF = 6.0
        LN_EPS = 1e-05
        src, dst = (edge_index[0], edge_index[1])
        N = h.shape[0]
        gate = jax.nn.silu(edge_attr @ W1.T + b1) @ W2.T + b2
        ei = emb[atom_z[src]]
        ej = emb[atom_z[dst]]
        adapt_logit = jnp.sum(ei * (ej @ adaptW.T), axis=-1, keepdims=True)
        gate = gate + adapt_logit
        cw = jnp.where(distances < CUTOFF, 0.5 * (jnp.cos(jnp.pi * distances / CUTOFF) + 1.0), 0.0)
        mj = node_mult[dst]
        msg = gate * h[dst] * (cw * mj)[:, None]
        agg = jax.ops.segment_sum(msg, src, num_segments=N)
        tot = jax.ops.segment_sum(mj, src, num_segments=N)
        agg = agg / jnp.clip(tot, 1e-08, None)[:, None]
        x = h + agg
        mu = jnp.mean(x, axis=-1, keepdims=True)
        var = jnp.mean(jnp.square(x - mu), axis=-1, keepdims=True)
        return (x - mu) / jnp.sqrt(var + LN_EPS) * gamma + beta
    edge_index = jnp.stack([src, dst])
    batch0 = jnp.zeros((100000,), jnp.int32)
    x = _layernorm(x + _L0_gnn_ref(x, edge_attr_48, src, dst, L0_gnn_eps), axis=-1)
    x = _layernorm(x + _L1_gnn_ref(x, src, dst, L1_gnn_W, L1_gnn_b), axis=-1)
    x = _layernorm(x + _L2_gnn_ref(x, edge_index, L2_gnn_W, L2_gnn_b), axis=-1)
    x = _layernorm(x + _L3_gnn_ref(x, edge_index, edge_attr_40, edge_weight, node_type_119, node_vec, batch0, L3_gnn_W1, L3_gnn_b1, L3_gnn_W2, L3_gnn_b2, L3_gnn_emb, L3_gnn_adaptW, L3_gnn_gamma, L3_gnn_beta), axis=-1)
    return x

_drawn_inputs = setup_inputs


def setup_inputs(seed=0):
    import zlib

    import numpy as np

    out = dict(_drawn_inputs(seed))
    spreads = {'L1_gnn_b': (0.0, 0.1), 'L3_gnn_gamma': (1.0, 0.2), 'L3_gnn_beta': (0.0, 0.1)}
    factors = {'edge_attr_40': 2.785,
     'node_vec': 36.723,
     'L3_gnn_b1': 64.0,
     'L3_gnn_b2': 54.036,
     'L3_gnn_emb': 64.0,
     'L3_gnn_adaptW': 64.0}
    for name, (base, spread) in spreads.items():
        noise = np.random.default_rng([zlib.crc32(name.encode()), seed]).standard_normal(out[name].shape)
        drawn = base * np.exp(spread * noise) if base else spread * noise
        out[name] = jnp.asarray(drawn.astype(out[name].dtype))
    for name, factor in factors.items():
        out[name] = (out[name] * factor).astype(out[name].dtype)
    return out
```

```python
from contextlib import ExitStack, contextmanager

import concourse.bass as bass
from concourse import mybir

P = 128
D = 48
N = 100000
CN = 784
NP = P * CN
E = 25000
CE = 196
EP = P * CE
R = 28
H = 14
NBLK = CE // R
DBLK = CN // R
PER = DBLK // NBLK
XW = 52
RW = 98
A_DIM = 40
Z = 120
G = 32
EPS = 1e-5
SORT_C = 256
SORT_P = EP // SORT_C
SKIP = float(1 << 20)
HALF_NODES = NP // 2
F32 = mybir.dt.float32
I32 = mybir.dt.int32
I16 = mybir.dt.int16
BF16 = mybir.dt.bfloat16


class Count:

    def __init__(self, sem, step=1):
        self.sem, self.step, self.n, self.turn = sem, step, 0, 0

    def add(self):
        self.n += self.step
        return self.step

    def up(self, times=1):
        self.n += self.step * times
        return self.now()

    def now(self):
        return self.turn + self.n


def sort_turns():
    now, turns = 0, []
    for m in range(1, 16):
        if m > 8:
            turns.append(now)
            now = (now + 1 + m - 8) % 2
            turns.append(now)
            now = (now + 1) % 2
        now = (now + min(m, 8)) % 2
    return turns, now


@contextmanager
def loop(eng, times, per):
    with eng.Fori(0, times) as i:
        before = {c: c.n for c in per}
        for c, k in per.items():
            c.turn = i * (k * c.step)
        yield i
        for c, k in per.items():
            assert c.n - before[c] == k * c.step, (c.sem, c.n - before[c], k * c.step)
            c.turn = 0
    for c, k in per.items():
        c.n = before[c] + times * k * c.step


def bass_gnn(nc, A, OUT):
    ALU, ACT, X = mybir.AluOpType, mybir.ActivationFunctionType, mybir.AxisListType.X
    ctx = ExitStack()
    with ctx:
        def sb(name, shape, dt=F32):
            return ctx.enter_context(nc.sbuf_tensor(name, shape, dt))

        def ps(name):
            return ctx.enter_context(nc.psum_tensor(name, [P, 512], F32))

        def sem(name):
            return ctx.enter_context(nc.semaphore(name))

        def dram(name, shape, dt=F32):
            return nc.dram_tensor(name, shape, dt, kind="Internal").ap()

        XA = dram("xa_table", [NP, XW])
        X1 = dram("x1_table", [NP, D])
        Y1 = dram("y1_table", [NP, D])
        X2 = dram("x2_table", [NP, D])
        X3 = dram("x3_table", [NP, D])
        X3C = dram("x3_copy", [NP, D])
        REC = dram("edge_records", [EP, RW])
        SRT = dram("sorted_src", [P * SORT_C + 2], I32)

        def blk(table, k, w=D):
            return table.rearrange("(p c) d -> p c d", p=P)[:, bass.ds(k * R, R), 0:w]

        MG = sb("MG", [P, 1 + CE, D])
        M = MG[:, 1:1 + CE, :]
        XS = sb("XS", [P, CE, D])
        GX = sb("GX", [P, CE, D + 2])
        ring = sb("ring", [P, 2, H, RW])
        idx = sb("idx", [P, 2, H], I32)
        stage = sb("stage", [P, 2, H, D])
        din = sb("din", [P, 2, R * XW])
        du = sb("du", [P, 2, R, D])
        sq = sb("sq", [P, 2, R, D])
        do = sb("do", [P, 2, R, D])
        su = sb("su", [P, R, D])
        hT = sb("hT", [97, 2, 512])
        mu = sb("mu", [P, 2, R])
        var = sb("var", [P, 2, R])
        srs = sb("srs", [P, 2, R])
        deg = sb("deg", [P, CN])
        srcI = sb("srcI", [P, CE], I32)
        dstI = sb("dstI", [P, CE], I32)
        dstS = sb("dstS", [P, CE], I32)
        key = sb("key", [P, CE])
        keyn = sb("keyn", [P, CE])
        cont = sb("cont", [P, CE])
        pre = sb("pre", [P, CE])
        suf = sb("suf", [P, CE])
        end = sb("end", [P, CE])
        cnt = sb("cnt", [P, CE])
        put = sb("put", [P, CE], I32)
        zs = sb("zs", [P, CE])
        zd = sb("zd", [P, CE])
        nv = sb("nv", [P, CE])
        dg = sb("dg", [P, CE])
        t0 = sb("t0", [P, CE])
        t1 = sb("t1", [P, CE])
        tail = sb("tail", [P, D + 1])
        carry = sb("carry", [P, D + 1])
        ident = sb("ident", [P, P])
        identb = sb("identb", [P, P], BF16)
        fullT = sb("fullT", [D + 1, P])
        tailT = sb("tailT", [D + 1, P])
        shT = sb("shT", [D + 1, P + 1])
        w1b = sb("w1b", [97, 96])
        w2b = sb("w2b", [97, 96])
        wm1 = sb("wm1", [A_DIM, D])
        bm1 = sb("bm1", [D, 1])
        wm2 = sb("wm2", [D + 1, D])
        embw = sb("embw", [Z, G])
        embT = sb("embT", [G, Z])
        adT = sb("adT", [G, G])
        eaw = sb("eaw", [Z, G])
        rows = sb("rows", [P, 3, D])
        c2e = sb("c2e", [P, 1])
        lneps = sb("lneps", [P, 1])
        psgn = sb("psgn", [P, 8])
        pos = sb("pos", [P, SORT_C], I32)
        va = sb("va", [P, SORT_C])
        vb = sb("vb", [P, SORT_C])
        zero1 = sb("zero1", [P, 1])
        gflat = GX[:, :, :].rearrange("p c w -> p (c w)")
        iota = gflat[:, 0:CN // 2].bitcast(I16)
        ohc = gflat[:, 400:400 + CN].bitcast(BF16).rearrange("p (h c) -> p h c", h=2)
        ohp = gflat[:, 1200:1200 + P].bitcast(BF16).rearrange("p (h c) -> p h c", h=2)
        colf = gflat[:, 1400:1400 + CE]
        parf = gflat[:, 1600:1600 + CE]
        tmpf = gflat[:, 1800:1800 + CE]
        ohs = du[:, :, :, :].rearrange("p h c d -> p (h c d)")[:, 0:R * Z // 2].bitcast(BF16).rearrange(
            "p (c z) -> p c z", z=Z)
        ohd = sq[:, :, :, :].rearrange("p h c d -> p (h c d)")[:, 0:R * Z // 2].bitcast(BF16).rearrange(
            "p (c z) -> p c z", z=Z)
        zbs = du[:, :, :, :].rearrange("p h c d -> p (h c d)")[:, 1700:1700 + CE // 2].bitcast(BF16)
        zbd = du[:, :, :, :].rearrange("p h c d -> p (h c d)")[:, 1800:1800 + CE // 2].bitcast(BF16)
        ea = din[:, 0, 0:R * A_DIM].rearrange("p (c a) -> p c a", a=A_DIM)
        doflat = do[:, :, :, :].rearrange("p h c d -> p (h c d)")
        eaT = doflat[0:A_DIM, 0:512]
        h1T = doflat[0:D + 1, 512:1024]
        zT = doflat[0:Z, 1024:1536]
        zT2 = doflat[0:Z, 1536:2048]
        ejs = doflat[:, 2048:2048 + 4 * G].rearrange("p (c g) -> p c g", g=G)
        prod = doflat[:, 2200:2200 + 4 * G].rearrange("p (c g) -> p c g", g=G)
        gsum = doflat[:, 2400:2400 + 4 * D].rearrange("p (c d) -> p c d", d=D)
        lg = sb("lg", [P, 4])
        iotaz = sb("iotaz", [P, Z], BF16)
        cib = sb("cib", [P, R])
        restT = sb("restT", [D + 1, P])
        ew = t1[:, :]
        psT = [ps("psT0"), ps("psT1")]
        psO = [ps("psO0"), ps("psO1")]
        psA, psB, psC, psG = ps("psA"), ps("psB"), ps("psC"), ps("psG")

        S = {n: sem(n) for n in (
            "dve", "act", "pool",
            "consts", "edges", "ea48", "init", "pool_turns", "pe_turns",
            "hot", "counted", "deg_done", "col_ready", "xa_ld0", "xa_ld1", "xa_done",
            "ld0", "ld1", "in_free", "out_ready", "st0", "st1", "short_done",
            "centered", "squared", "var_ready", "std_ready",
            "fill0", "fill1", "ring_free", "kept", "scanned", "xs_free", "sc0", "sc1", "stage_free",
            "rows_ready", "rows_new", "idx_ready", "s_done",
            "h_ready", "trans", "hT_ready", "mm", "mm_used", "ask_act", "act_done", "ask_pe", "pe_done",
            "mlp_ld", "mlp_free", "hots", "mlp_t", "mlp_a", "mlp_o", "mlp_g", "mlp_used",
            "rec_ready", "rec_st", "srt_ready", "srt_st", "srt_ld")}
        FROM_DMA = ("consts", "edges", "ea48", "xa_ld0", "xa_ld1", "ld0", "ld1", "st0", "st1",
                    "fill0", "fill1", "sc0", "sc1", "mlp_ld", "rec_st", "srt_st", "srt_ld")

        def views(*names):
            return [Count(S[n], 16 if n in FROM_DMA else 1) for n in names]

        block = ctx.enter_context(nc.Block())

        @block.sync
        def _(sp):
            consts, edges, ea48 = views("consts", "edges", "ea48")
            for to, of in ((srcI[:, :], A["src"][1:EP + 1]), (dstI[:, :], A["dst"][1:EP + 1]),
                           (t0[:, :].bitcast(I32), A["dst"][2:EP + 2]), (cnt[:, :].bitcast(I32), A["dst"][0:EP]),
                           (ew, A["ew"])):
                sp.dma_start(to, of.rearrange("(p c) -> p c", p=P)).then_inc(edges.sem, edges.add())
            sp.dma_start(vb[0:SORT_P, :].bitcast(I32), A["src"][1:EP + 1].rearrange("(p c) -> p c", p=SORT_P)).then_inc(edges.sem, edges.add())
            for to, name in ((iota, "iota"), (iotaz[:], "iotaz"), (ident[:], "ident"), (identb[:], "identb"),
                             (w1b[:], "w1b"), (w2b[:], "w2b"), (wm1[:], "wm1"), (bm1[:], "bm1"), (wm2[:], "wm2"),
                             (embw[:], "emb"), (embT[:], "embT"), (adT[:], "adT"), (psgn[:], "psgn"), (pos[:], "pos")):
                sp.dma_start(to, A[name]).then_inc(consts.sem, consts.add())
            for j, name in enumerate(("b2", "gamma", "beta")):
                sp.dma_start(rows[:, j, :], A[name].broadcast_to([P, D])).then_inc(consts.sem, consts.add())
            sp.dma_start(c2e[:, :], A["eps"].broadcast_to([P, 1])).then_inc(consts.sem, consts.add())
            sp.dma_start(M, A["ea48"].rearrange("(p c) d -> p c d", p=P)).then_inc(ea48.sem, ea48.add())

            ld, st = views("ld0", "ld1"), views("st0", "st1")
            xld = views("xa_ld0", "xa_ld1")
            col_ready, = views("col_ready")

            def xa_load(h, k):
                sp.dma_start(din[:, h, :], blk(A["xaux"], k, XW).rearrange("p c d -> p (c d)")).then_inc(xld[h].sem, xld[h].add())

            def xa_store(h, k):
                sp.wait_ge(col_ready.sem, col_ready.up())
                sp.dma_start(blk(XA, k, XW).rearrange("p c d -> p (c d)"), din[:, h, :]).then_inc(st[h].sem, st[h].add())

            xa_load(0, 0)
            xa_load(1, 1)
            with loop(sp, DBLK // 2 - 1, {xld[0]: 1, xld[1]: 1, st[0]: 1, st[1]: 1, col_ready: 2}) as i:
                for h in range(2):
                    xa_store(h, 2 * i + h)
                for h in range(2):
                    sp.wait_ge(st[h].sem, st[h].now())
                    xa_load(h, 2 * i + 2 + h)
            for h in range(2):
                xa_store(h, DBLK - 2 + h)
            for h in range(2):
                sp.wait_ge(st[h].sem, st[h].now())
            sp.sem_inc(S["xa_done"], 1)

            in_free, out_ready = views("in_free", "out_ready")

            def load(h, k, table, w):
                sp.wait_ge(in_free.sem, in_free.up())
                sp.dma_start(din[:, h, 0:R * w], blk(table, k, w).rearrange("p c d -> p (c d)")).then_inc(ld[h].sem, ld[h].add())

            def store(h, k, tables):
                sp.wait_ge(out_ready.sem, out_ready.up())
                for buf, table in tables:
                    sp.dma_start(blk(table, k), buf[:, h, :, :]).then_inc(st[h].sem, st[h].add())

            def dense(table, w, tables, before=None):
                if before:
                    before()
                for h in range(2):
                    load(h, h, table, w)
                with loop(sp, DBLK // 2 - 1, {ld[0]: 1, ld[1]: 1, in_free: 2, out_ready: 2,
                                              st[0]: len(tables), st[1]: len(tables)}) as i:
                    for h in range(2):
                        store(h, 2 * i + h, tables)
                    for h in range(2):
                        load(h, 2 * i + 2 + h, table, w)
                for h in range(2):
                    store(h, DBLK - 2 + h, tables)
                for h in range(2):
                    sp.wait_ge(st[h].sem, st[h].now())
                sp.sem_inc(S["short_done"], 1)

            dense(A["xaux"], XW, [(do, X1), (du, Y1)])
            dense(X1, D, [(do, X2)])

            mld, mfree = views("mlp_ld", "mlp_free")
            with loop(sp, NBLK, {mld: 1, mfree: 1}) as i:
                sp.wait_ge(mfree.sem, mfree.up())
                sp.dma_start(ea, A["ea40"].rearrange("(p c) a -> p c a", p=P)[:, bass.ds(i * R, R), :]).then_inc(mld.sem, mld.add())

            rec_ready, rec_st = views("rec_ready", "rec_st")
            recv = REC.rearrange("(p c) w -> p c w", p=P)
            sp.wait_ge(rec_ready.sem, rec_ready.up())
            sp.dma_start(recv[:, :, D:RW], GX[:, :, :]).then_inc(rec_st.sem, rec_st.add())
            sp.wait_ge(rec_ready.sem, rec_ready.up())
            sp.dma_start(recv[:, :, 0:D], M).then_inc(rec_st.sem, rec_st.add())
            srt_ready, srt_st, srt_ld = views("srt_ready", "srt_st", "srt_ld")
            sp.wait_ge(srt_ready.sem, srt_ready.up())
            sp.dma_start(SRT[1:P * SORT_C + 1].rearrange("(p c) -> p c", p=P), vb[:, :].bitcast(I32)).then_inc(srt_st.sem, srt_st.add())
            sp.dma_start(SRT[0:1].rearrange("(p c) -> p c", p=1), zero1[0:1, 0:1].bitcast(I32)).then_inc(srt_st.sem, srt_st.add())
            sp.wait_ge(srt_st.sem, srt_st.now())
            for at, to in ((1, t0), (2, keyn), (0, cont)):
                sp.dma_start(to[:, :].bitcast(I32), SRT[at:at + EP].rearrange("(p c) -> p c", p=P)).then_inc(srt_ld.sem, srt_ld.add())

            s_done, = views("s_done")

            def scattered():
                sp.wait_ge(s_done.sem, s_done.up(2))
            dense(X2, D, [(do, X3), (do, X3C)], scattered)
            dense(X3C, D, [(do, OUT)])
            sp.wait_ge(s_done.sem, s_done.up(2))

        @block.gpsimd
        def _(pool):
            own, = views("pool")
            fill, sc = views("fill0", "fill1"), views("sc0", "sc1")
            ring_free, rows_ready = views("ring_free", "rows_ready")
            idx_ready, short_done, edges, rec_st = views("idx_ready", "short_done", "edges", "rec_st")
            last_row = pool.to_reg(NP - 1)

            def indices(h, c, of):
                nc.gpsimd.tensor_copy(idx[:, h, :], of[:, bass.ds(c * H, H)]).then_inc(own.sem, own.add())
                pool.wait_ge(own.sem, own.now())
                pool.sem_inc(S["pool_turns"], 1)

            def gather(table, w, of):
                with loop(pool, NBLK, {own: 2, ring_free: 2, fill[0]: H, fill[1]: H}) as i:
                    for h in range(2):
                        pool.wait_ge(ring_free.sem, ring_free.up())
                        indices(h, 2 * i + h, of)
                        for t in range(H):
                            pool.indirect_dma_start(
                                ring[:, h, t, 0:w], None, table,
                                bass.IndirectOffsetOnAxis(ap=idx[:, h, t:t + 1], axis=0)).then_inc(fill[h].sem, fill[h].add())
                for h in range(2):
                    pool.wait_ge(fill[h].sem, fill[h].now())

            def scatter_turn(table, c, h, first):
                pool.wait_ge(rows_ready.sem, rows_ready.up())
                indices(h, c, put)
                for t in range(H):
                    pool.indirect_dma_start(
                        table, bass.IndirectOffsetOnAxis(ap=idx[:, h, t:t + 1], axis=0),
                        stage[:, h, t, :], None, bounds_check=last_row, oob_is_err=False).then_inc(sc[h].sem, sc[h].add())
                    if t == H // 2 and not first:
                        pool.wait_ge(sc[1 - h].sem, sc[1 - h].now())
                        pool.sem_inc(S["stage_free"], 1)

            def scatter(table):
                scatter_turn(table, 0, 0, True)
                scatter_turn(table, 1, 1, False)
                with loop(pool, NBLK - 1, {own: 2, rows_ready: 2, sc[0]: H, sc[1]: H}) as i:
                    scatter_turn(table, 2 * i + 2, 0, False)
                    scatter_turn(table, 2 * i + 3, 1, False)
                pool.wait_ge(sc[1].sem, sc[1].now())
                pool.sem_inc(S["stage_free"], 1)
                pool.sem_inc(S["s_done"], 1)

            pool.wait_ge(edges.sem, edges.up(6))
            gather(A["xaux"], XW, srcI)
            pool.wait_ge(S["xa_done"], 1)
            gather(XA, XW, dstI)
            pool.wait_ge(idx_ready.sem, idx_ready.up())
            pool.wait_ge(short_done.sem, short_done.up())
            scatter(Y1)
            gather(Y1, D, srcI)
            pool.wait_ge(short_done.sem, short_done.up())
            scatter(X2)
            pool.wait_ge(idx_ready.sem, idx_ready.up())
            gather(X2, D, srcI)
            pool.wait_ge(rec_st.sem, rec_st.up(2))
            gather(REC, RW, dstI)
            pool.wait_ge(short_done.sem, short_done.up())
            scatter(X3)
            gather(X3, D, dstS)
            pool.wait_ge(short_done.sem, short_done.up())
            scatter(OUT)

        @block.scalar
        def _(act):
            own, = views("act")
            fill = views("fill0", "fill1")
            centered, var_ready, xs_free, rows_new, stage_free, scanned = views(
                "centered", "var_ready", "xs_free", "rows_new", "stage_free", "scanned")
            trans, ask = views("trans", "ask_act")
            act.wait_ge(S["init"], 1)
            act.wait_ge(S["consts"], 16 * 18)
            act.sem_inc(S["ring_free"], 2)
            act.sem_inc(S["stage_free"], 2)

            def take(h, uses, also=None):
                act.wait_ge(fill[h].sem, fill[h].up(H))
                for to, of in uses:
                    nc.scalar.activation(to, of, ACT.Copy).then_inc(own.sem, own.add())
                act.wait_ge(own.sem, own.now())
                if also:
                    act.wait_ge(also.sem, also.up())
                act.sem_inc(S["ring_free"], 1)
                act.sem_inc(S["kept"], 1)

            def norm(units):
                for h, u in units:
                    act.wait_ge(centered.sem, centered.up())
                    nc.scalar.activation(sq[:, h, :, :], u, ACT.Square).then_inc(S["squared"], 1)
                for h, u in units:
                    act.wait_ge(var_ready.sem, var_ready.up())
                    nc.scalar.activation(var[:, h, :], var[:, h, :], ACT.Sqrt, bias=lneps[:, 0:1],
                                         scale=1.0 / D).then_inc(S["std_ready"], 1)

            def evacuate():
                for g in range(4):
                    w = 256 if g == 3 else 512
                    act.wait_ge(trans.sem, trans.up())
                    nc.scalar.activation(hT[0:96, g % 2, 0:w], psT[g % 2][0:96, 0:w], ACT.Copy
                                         ).then_inc(S["hT_ready"], 1)

            def to_stage(of, i):
                act.wait_ge(rows_new.sem, rows_new.up())
                for h in range(2):
                    act.wait_ge(stage_free.sem, stage_free.up())
                    nc.scalar.activation(stage[:, h, :, :], of[:, bass.ds((2 * i + h) * H, H), :], ACT.Copy
                                         ).then_inc(S["rows_ready"], 1)

            def function(of, what=ACT.Sqrt):
                act.wait_ge(ask.sem, ask.up())
                nc.scalar.activation(of, of, what).then_inc(S["act_done"], 1)

            pair = [(0, du[:, 0, :, :]), (1, du[:, 1, :, :])]

            with loop(act, NBLK, {own: 4, fill[0]: H, fill[1]: H}) as i:
                for h in range(2):
                    cols = bass.ds((2 * i + h) * H, H)
                    take(h, [(XS[:, cols, :], ring[:, h, :, 0:D]),
                             (zs[:, cols], ring[:, h, :, D + 1].bitcast(I32))])
            function(deg[:, :])

            with loop(act, NBLK, {own: 8, fill[0]: H, fill[1]: H, xs_free: 2, centered: PER + 1,
                                  var_ready: PER + 1, ask: 1}) as i:
                act.wait_ge(xs_free.sem, xs_free.up(2))
                for h in range(2):
                    cols = bass.ds((2 * i + h) * H, H)
                    take(h, [(XS[:, cols, :], ring[:, h, :, 0:D]),
                             (nv[:, cols], ring[:, h, :, D]),
                             (zd[:, cols], ring[:, h, :, D + 1].bitcast(I32)),
                             (dg[:, cols], ring[:, h, :, D + 3])])
                for _ in range(PER // 2):
                    norm(pair)
                function(cib[:, :])
                norm([(0, su[:, :, :])])

            with loop(act, NBLK, {stage_free: 2, rows_new: 1, centered: PER, var_ready: PER, trans: 4 * PER}) as i:
                to_stage(M, i)
                for _ in range(PER // 2):
                    evacuate()
                    evacuate()
                    norm(pair)

            function(t1[:, :], ACT.Sin)
            mt, mo = views("mlp_t", "mlp_o")
            with loop(act, NBLK, {mt: 4 * R // 4, mo: R // 4}) as i:
                for g in range(R // 4):
                    act.wait_ge(mt.sem, mt.up())
                    nc.scalar.activation(eaT, psT[0][0:A_DIM, :], ACT.Copy).then_inc(S["mlp_a"], 1)
                    act.wait_ge(mt.sem, mt.up())
                    nc.scalar.activation(zT, psO[0][0:Z, 0:256].bitcast(BF16), ACT.Copy).then_inc(S["mlp_a"], 1)
                    act.wait_ge(mt.sem, mt.up())
                    nc.scalar.activation(zT2, psO[1][0:Z, 0:256].bitcast(BF16), ACT.Copy).then_inc(S["mlp_a"], 1)
                    act.wait_ge(mt.sem, mt.up())
                    nc.scalar.activation(h1T[0:D, :], psA[0:D, :], ACT.Silu, bias=bm1[:, 0:1]).then_inc(S["mlp_a"], 1)
                    act.wait_ge(mo.sem, mo.up())
                    nc.scalar.activation(ejs, psC[:, 0:4 * G].rearrange("p (c g) -> p c g", g=G), ACT.Copy
                                         ).then_inc(S["mlp_a"], 1)

            function(t0[:, :])
            function(t1[:, :])
            with loop(act, NBLK, {stage_free: 2, rows_new: 1, centered: 1, var_ready: 1, trans: 4}) as i:
                evacuate()
                norm(pair[:1])
                to_stage(XS, i)

            for h in range(2):
                fill[h].n += 16 * CE // 2
            with loop(act, NBLK, {own: 2, fill[0]: H, fill[1]: H, centered: PER, var_ready: PER}) as i:
                for h in range(2):
                    cols = bass.ds((2 * i + h) * H, H)
                    take(h, [(XS[:, cols, :], ring[:, h, :, 0:D])])
                for _ in range(PER // 2):
                    norm(pair)

            with loop(act, NBLK, {own: 4, scanned: 2, fill[0]: H, fill[1]: H, centered: 4, var_ready: 4}) as i:
                for h in range(2):
                    cols = bass.ds((2 * i + h) * H, H)
                    take(h, [(GX[:, cols, 0:D + 1], ring[:, h, :, D:RW - 1]),
                             (dstS[:, cols], ring[:, h, :, RW - 1].bitcast(I32))], scanned)
                norm(pair)
                norm(pair)

            function(t0[:, :])
            with loop(act, NBLK, {stage_free: 2, rows_new: 1, centered: 1, var_ready: 1, trans: 4}) as i:
                evacuate()
                norm(pair[:1])
                to_stage(XS, i)

            with loop(act, NBLK, {centered: 4, var_ready: 4}) as i:
                norm(pair)
                norm(pair)

            with loop(act, NBLK, {stage_free: 2, rows_new: 1, centered: 2, var_ready: 2}) as i:
                norm([(0, su[:, :, :])])
                norm([(0, su[:, :, :])])
                to_stage(XS, i)

        @block.tensor
        def _(pe):
            T = nc.tensor
            hot, ask, h_ready, hT_ready, mm_used = views("hot", "ask_pe", "h_ready", "hT_ready", "mm_used")
            ld = views("ld0", "ld1")
            pe.wait_ge(S["consts"], 16 * 18)
            pe.wait_ge(S["init"], 1)

            def flip():
                pe.wait_ge(ask.sem, ask.up())
                T.transpose(psG[0:D + 1, 0:P], tail[:, :], ident[:, :]).then_inc(S["pe_done"], 1)

            def flip_back(at):
                pe.wait_ge(ask.sem, ask.up())
                T.transpose(psG[:, P:P + D + 1], shT[:, at:at + P], ident[0:D + 1, 0:D + 1]).then_inc(S["pe_done"], 1)

            def product(rows_of, weights):
                for g in range(4):
                    n = 2 if g == 3 else 4
                    for j in range(n):
                        last = T.transpose(psT[g % 2][0:96, j * P:(j + 1) * P],
                                           rows_of[:, (4 * g + j) * 96:(4 * g + j + 1) * 96], ident[:, :])
                    last.then_inc(S["trans"], 1)
                    pe.wait_ge(hT_ready.sem, hT_ready.up())
                    pe.wait_ge(mm_used.sem, mm_used.up())
                    for j in range(n):
                        last = T.matmul(psO[g % 2][:, j * 96:(j + 1) * 96], hT[0:97, g % 2, j * P:(j + 1) * P],
                                        weights[:, :], start=True, stop=True)
                    last.then_inc(S["mm"], 1)

            T.matmul(psG[0:Z, 0:G], embT[:, :], adT[:, :], start=True, stop=True).then_inc(S["pe_done"], 1)
            flip()
            flip()

            pe.sem_inc(S["counted"], 2)

            def count_edges(g, start, stop):
                pe.wait_ge(hot.sem, hot.up())
                for c in range(2):
                    last = T.matmul((psA, psB)[c][:, 0:CN // 2], ohp[:, g, :],
                                    ohc[:, g, c * (CN // 2):(c + 1) * (CN // 2)],
                                    start=start, stop=stop, skip_group_check=True)
                last.then_inc(S["counted"], 1)
            count_edges(0, True, False)
            count_edges(1, False, False)
            with loop(pe, CE // 2 - 2, {hot: 2}) as i:
                count_edges(0, False, False)
                count_edges(1, False, False)
            count_edges(0, False, False)
            count_edges(1, False, True)

            flip()
            flip_back(0)
            for h in range(2):
                ld[h].n = 16 * DBLK // 2
            with loop(pe, NBLK, {ld[0]: PER // 2, ld[1]: PER // 2, hT_ready: 4 * PER, mm_used: 4 * PER}) as i:
                for _ in range(PER // 2):
                    for h in range(2):
                        pe.wait_ge(ld[h].sem, ld[h].up())
                        product(din[:, h, :], w1b)

            hots, mld, ma, mused = views("hots", "mlp_ld", "mlp_a", "mlp_used")
            with loop(pe, NBLK, {hots: 1, mld: 1, ma: 5 * R // 4, mused: R // 4}) as i:
                pe.wait_ge(hots.sem, hots.up())
                pe.wait_ge(mld.sem, mld.up())
                pe.sem_inc(S["pe_turns"], 1)
                for g in range(R // 4):
                    for j in range(4):
                        last = T.transpose(psT[0][0:A_DIM, j * P:(j + 1) * P], ea[:, 4 * g + j, :], ident[:, :])
                    last.then_inc(S["mlp_t"], 1)
                    for oh, bank in ((ohs, psO[0]), (ohd, psO[1])):
                        for j in range(4):
                            last = T.transpose(bank[0:Z, 0:256].bitcast(BF16)[:, j * P:(j + 1) * P],
                                               oh[:, 4 * g + j, :], identb[:, :])
                        last.then_inc(S["mlp_t"], 1)
                    pe.wait_ge(ma.sem, ma.up())
                    pe.sem_inc(S["pe_turns"], 1)
                    T.matmul(psA[0:D, :], wm1[:, :], eaT, start=True, stop=True).then_inc(S["mlp_t"], 1)
                    pe.wait_ge(ma.sem, ma.up(2))
                    pe.wait_ge(mused.sem, mused.up())
                    for j in range(4):
                        T.matmul(psB[:, j * G:(j + 1) * G], zT[:, j * P:(j + 1) * P], embw[:, :], start=True, stop=True)
                        last = T.matmul(psC[:, j * G:(j + 1) * G], zT2[:, j * P:(j + 1) * P], eaw[:, :],
                                        start=True, stop=True)
                    last.then_inc(S["mlp_o"], 1)
                    pe.wait_ge(ma.sem, ma.up(2))
                    for j in range(4):
                        last = T.matmul(psG[:, j * D:(j + 1) * D], h1T[:, j * P:(j + 1) * P], wm2[:, :],
                                        start=True, stop=True)
                    last.then_inc(S["mlp_g"], 1)

            flip()
            flip_back(0)
            suf_rows = su[:, :, :].rearrange("p c d -> p (c d)")

            def products(weights):
                with loop(pe, NBLK, {h_ready: 1, hT_ready: 4, mm_used: 4}) as i:
                    pe.wait_ge(h_ready.sem, h_ready.up())
                    product(suf_rows, weights)
            products(w1b)
            flip()
            flip_back(1)
            for n in sort_turns()[0]:
                pe.wait_ge(ask.sem, ask.up())
                for h in range(2):
                    last = T.transpose(psT[0][:, h * P:(h + 1) * P], (vb, va)[n][:, h * P:(h + 1) * P], ident[:, :])
                last.then_inc(S["pe_done"], 1)
            flip()
            flip()
            flip_back(0)
            products(w2b)
            flip()
            flip_back(0)

        @block.vector
        def _(dve):
            V = nc.vector
            own, = views("dve")

            def one(instruction):
                instruction.then_inc(own.sem, own.add())
                dve.wait_ge(own.sem, own.now())

            def along(t, w=D):
                return t.unsqueeze(2).broadcast_to([P, t.shape[1], w])

            def down(t, n=R):
                return t.unsqueeze(1).broadcast_to([P, n, t.shape[1]])

            act_done, pe_done = views("act_done", "pe_done")
            ld, st, xld = views("ld0", "ld1"), views("st0", "st1"), views("xa_ld0", "xa_ld1")
            squared, std_ready, kept, mm, counted = views("squared", "std_ready", "kept", "mm", "counted")
            fill = views("fill0", "fill1")

            def ask_act():
                dve.sem_inc(S["ask_act"], 1)
                dve.wait_ge(act_done.sem, act_done.up())

            def ask_pe():
                dve.sem_inc(S["ask_pe"], 1)
                dve.wait_ge(pe_done.sem, pe_done.up())

            V.memset(hT[:, :, :], 1.0).then_inc(own.sem, own.add())
            V.memset(lneps[:, :], EPS).then_inc(own.sem, own.add())
            V.memset(zero1[:, :], 0.0).then_inc(own.sem, own.add())
            V.memset(MG[:, 0:1, :], 0.0).then_inc(own.sem, own.add())
            dve.wait_ge(S["consts"], 16 * 18)
            one(V.tensor_scalar(c2e[:, :], c2e[:, :], 2.0, None, ALU.add))
            one(V.tensor_scalar(rows[:, 0, :], rows[:, 0, :], 0.0, None, ALU.max))
            dve.sem_inc(S["init"], 1)
            dve.sem_inc(S["mm_used"], 2)
            dve.sem_inc(S["in_free"], 2)
            dve.wait_ge(pe_done.sem, pe_done.up())
            one(V.tensor_copy(eaw[:, :], psG[0:Z, 0:G]))

            def flipped(to, column):
                one(V.tensor_copy(tail[:, :], column.broadcast_to([P, D + 1])))
                ask_pe()
                one(V.tensor_copy(to[:, :], psG[0:D + 1, 0:P]))

            def order(key, after, before):
                V.tensor_tensor(end[:, :], key, after, ALU.not_equal).then_inc(own.sem, own.add())
                one(V.tensor_tensor(cont[:, :], key, before, ALU.is_equal))
                V.tensor_scalar(carry[:, 0:1], end[:, CE - 1:CE], -1.0, 1.0, ALU.mult, ALU.add).then_inc(own.sem, own.add())
                one(V.tensor_scalar(pre[:, :], key, key[:, 0:1], cont[:, 0:1], ALU.is_equal, ALU.mult))
                one(V.tensor_scalar(suf[:, :], key, key[:, CE - 1:CE], carry[:, 0:1], ALU.is_equal, ALU.mult))
                flipped(fullT, pre[:, CE - 1:CE])

            def writers(node):
                one(V.tensor_scalar(t0[:, :], end[:, :], -SKIP, SKIP, ALU.mult, ALU.add))
                one(V.tensor_tensor(t0[:, :], t0[:, :], node, ALU.add))
                one(V.tensor_copy(put[:, :], t0[:, :]))
                dve.sem_inc(S["idx_ready"], 1)

            dve.wait_ge(S["edges"], 16 * 6)
            V.tensor_copy(key[:, :], dstI[:, :]).then_inc(own.sem, own.add())
            V.tensor_copy(keyn[:, :], t0[:, :].bitcast(I32)).then_inc(own.sem, own.add())
            one(V.tensor_copy(dg[:, :], cnt[:, :].bitcast(I32)))
            order(key[:, :], keyn[:, :], dg[:, :])
            flipped(restT, suf[:, 0:1])
            writers(key[:, :])

            one(V.tensor_copy(colf, srcI[:, :]))
            one(V.tensor_scalar(tmpf, colf, 1.0 / CN, None, ALU.mult))
            one(V.tensor_copy(keyn[:, :].bitcast(I32), tmpf))
            one(V.tensor_copy(parf, keyn[:, :].bitcast(I32)))
            one(V.scalar_tensor_tensor(colf, parf, -float(CN), colf, ALU.mult, ALU.add))
            one(V.tensor_scalar(tmpf, colf, 0.0, None, ALU.is_lt))
            V.tensor_tensor(parf, parf, tmpf, ALU.subtract).then_inc(own.sem, own.add())
            one(V.scalar_tensor_tensor(colf, tmpf, float(CN), colf, ALU.mult, ALU.add))
            one(V.tensor_scalar(tmpf, colf, float(CN), None, ALU.is_ge))
            V.tensor_tensor(parf, parf, tmpf, ALU.add).then_inc(own.sem, own.add())
            one(V.scalar_tensor_tensor(colf, tmpf, -float(CN), colf, ALU.mult, ALU.add))
            with loop(dve, CE // H, {counted: H}) as i:
                for t in range(H):
                    g = t % 2
                    dve.wait_ge(counted.sem, counted.up())
                    V.tensor_scalar(ohp[:, g, :], iota[:, 0:P], parf[:, bass.ds(i * H + t, 1)], None, ALU.is_equal)
                    V.tensor_scalar(ohc[:, g, :], iota[:, :], colf[:, bass.ds(i * H + t, 1)], None, ALU.is_equal
                                    ).then_inc(S["hot"], 1)
            dve.wait_ge(counted.sem, counted.up(2))
            V.tensor_copy(deg[:, 0:CN // 2], psA[:, 0:CN // 2]).then_inc(own.sem, own.add())
            one(V.tensor_copy(deg[:, CN // 2:CN], psB[:, 0:CN // 2]))

            def scans(c, of):
                cols = bass.ds(c * H, H)
                for f in range(D):
                    V.tensor_tensor_scan(M[:, cols, f], cont[:, cols], of(f), MG[:, bass.ds(c * H, 1), f],
                                            ALU.mult, ALU.add).then_inc(own.sem, own.add())
                dve.wait_ge(own.sem, own.now())

            dve.wait_ge(S["ea48"], 16)
            with loop(dve, DBLK // 2, {own: 2 + D, xld[0]: 1, xld[1]: 1, kept: 1, st[0]: 1, st[1]: 1}) as i:
                for h in range(2):
                    dve.wait_ge(xld[h].sem, xld[h].up())
                    V.tensor_copy(din[:, h, :].rearrange("p (c w) -> p c w", w=XW)[:, :, D + 3],
                                  deg[:, bass.ds((2 * i + h) * R, R)]).then_inc(S["col_ready"], 1)
                    st[h].n += 16
                dve.wait_ge(kept.sem, kept.up())
                cols = bass.ds(i * H, H)
                one(V.tensor_tensor(M[:, cols, :], M[:, cols, :], XS[:, cols, :], ALU.add))
                dve.sem_inc(S["xs_free"], 1)
                one(V.tensor_scalar(M[:, cols, :], M[:, cols, :], 0.0, None, ALU.max))
                scans(i, lambda f: M[:, cols, f])
            one(V.tensor_scalar(deg[:, :], deg[:, :], 1.0, None, ALU.max))
            ask_act()
            one(V.reciprocal(deg[:, :], deg[:, :]))

            def counts(of):
                one(V.tensor_tensor_scan(cnt[:, :], cont[:, :], of, 0.0, ALU.mult, ALU.add))

            def carries(with_counts):
                V.memset(shT[:, 0:1], 0.0).then_inc(own.sem, own.add())
                V.tensor_copy(tail[:, 0:D], M[:, CE - 1, :]).then_inc(own.sem, own.add())
                one(V.tensor_copy(tail[:, D:D + 1], cnt[:, CE - 1:CE]))
                ask_pe()
                one(V.tensor_copy(tailT[:, :], psG[0:D + 1, 0:P]))
                one(V.tensor_tensor_scan(shT[:, 1:P + 1], fullT[:, :], tailT[:, :], 0.0, ALU.mult, ALU.add))
                ask_pe()
                one(V.tensor_copy(carry[:, :], psG[:, P:P + D + 1]))
                if with_counts:
                    one(V.scalar_tensor_tensor(cnt[:, :], pre[:, :], carry[:, D:D + 1], cnt[:, :], ALU.mult, ALU.add))

            def carried(cols, mask=pre, n=R):
                one(V.tensor_tensor(su[:, :, :], along(mask[:, cols]), down(carry[:, 0:D]), ALU.mult))
                one(V.tensor_tensor(M[:, cols, :], M[:, cols, :], su[:, :, :], ALU.add))

            def norm(units):
                for h, x, u, out in units:
                    V.tensor_reduce(mu[:, h, :], x, X, ALU.add).then_inc(own.sem, own.add())
                dve.wait_ge(own.sem, own.now())
                for h, x, u, out in units:
                    V.scalar_tensor_tensor(u, along(mu[:, h, :]), -1.0 / D, x, ALU.mult, ALU.add
                                           ).then_inc(S["centered"], 1)
                for h, x, u, out in units:
                    dve.wait_ge(squared.sem, squared.up())
                    V.tensor_reduce(var[:, h, :], sq[:, h, :, :], X, ALU.add).then_inc(S["var_ready"], 1)
                for h, x, u, out in units:
                    dve.wait_ge(std_ready.sem, std_ready.up())
                    V.reciprocal(srs[:, h, :], var[:, h, :]).then_inc(own.sem, own.add())
                dve.wait_ge(own.sem, own.now())
                for h, x, u, out in units:
                    V.tensor_tensor(out, u, along(srs[:, h, :]), ALU.mult).then_inc(own.sem, own.add())
                dve.wait_ge(own.sem, own.now())

            NORM1, NORM2 = 3, 6
            DU = [du[:, h, :, :] for h in range(2)]
            DO = [do[:, h, :, :] for h in range(2)]
            pair = [(h, DU[h], DU[h], DO[h]) for h in range(2)]

            def wide(h, w):
                return din[:, h, 0:R * w].rearrange("p (c w) -> p c w", w=w)[:, :, 0:D]

            one(V.memset(t0[:, :], 1.0))
            counts(t0[:, :])
            carries(True)
            per = {own: 2 * (2 + NORM2) + 6 + NORM1, ld[0]: 2, ld[1]: 2, st[0]: 4, st[1]: 4, kept: 2,
                   squared: PER + 1, std_ready: PER + 1, act_done: 1}
            with loop(dve, NBLK, per) as i:
                for q in range(PER // 2):
                    for h in range(2):
                        dve.wait_ge(ld[h].sem, ld[h].up())
                        dve.wait_ge(st[h].sem, st[h].now())
                        V.tensor_scalar(DU[h], wide(h, XW), c2e[:, 0:1], None, ALU.mult).then_inc(own.sem, own.add())
                    dve.wait_ge(own.sem, own.now())
                    dve.sem_inc(S["in_free"], 2)
                    norm(pair)
                    for h in range(2):
                        V.tensor_tensor(DU[h], DO[h], along(deg[:, bass.ds((PER * i + 2 * q + h) * R, R)]), ALU.mult
                                        ).then_inc(S["out_ready"], 1)
                        st[h].n += 32
                dve.wait_ge(kept.sem, kept.up(2))
                cols = bass.ds(i * R, R)
                V.tensor_scalar(cib[:, :], dg[:, cols], 1.0, None, ALU.max).then_inc(own.sem, own.add())
                carried(cols)
                ask_act()
                V.reciprocal(cib[:, :], cib[:, :]).then_inc(own.sem, own.add())
                one(V.scalar_tensor_tensor(su[:, :, :], XS[:, cols, :], c2e[:, 0:1], M[:, cols, :], ALU.mult, ALU.add))
                norm([(0, su[:, :, :], su[:, :, :], XS[:, cols, :])])
                one(V.tensor_tensor(M[:, cols, :], XS[:, cols, :], along(cib[:, :]), ALU.mult))
                dve.sem_inc(S["rows_new"], 1)

            def taken(h, x):
                for g in range(4):
                    n = 4 if g == 3 else 8
                    dve.wait_ge(mm.sem, mm.up())
                    V.scalar_tensor_tensor(DU[h][:, 8 * g:8 * g + n, :],
                                              psO[g % 2][:, 0:n * D].rearrange("p (c d) -> p c d", d=D), 0.0,
                                              x(g, n), ALU.max, ALU.add).then_inc(own.sem, own.add())
                    dve.wait_ge(own.sem, own.now())
                    dve.sem_inc(S["mm_used"], 1)

            with loop(dve, NBLK, {own: 2 * (8 + NORM2), mm: 16, ld[0]: 2, ld[1]: 2, st[0]: 2, st[1]: 2,
                                  squared: PER, std_ready: PER}) as i:
                for q in range(PER // 2):
                    for h in range(2):
                        dve.wait_ge(ld[h].sem, ld[h].up())
                        taken(h, lambda g, n: wide(h, D)[:, 8 * g:8 * g + n, :])
                        dve.wait_ge(st[h].sem, st[h].now())
                        st[h].n += 16
                    dve.sem_inc(S["in_free"], 2)
                    norm(pair)
                    dve.sem_inc(S["out_ready"], 2)

            for h in range(2):
                dve.wait_ge(st[h].sem, st[h].now())
            V.tensor_copy(zbs, zs[:, :]).then_inc(own.sem, own.add())
            V.tensor_copy(zbd, zd[:, :]).then_inc(own.sem, own.add())
            V.memset(h1T, 1.0).then_inc(own.sem, own.add())
            one(V.tensor_scalar(t0[:, :], ew[:, :], 6.0, 0.5, ALU.is_lt, ALU.mult))
            one(V.tensor_scalar(t1[:, :], ew[:, :], 0.0, 6.0, ALU.max, ALU.min))
            one(V.tensor_scalar(t1[:, :], t1[:, :], -3.14159265358979 / 6, 3.14159265358979 / 2, ALU.mult, ALU.add))
            ask_act()
            one(V.scalar_tensor_tensor(t1[:, :], t1[:, :], 1.0, t0[:, :], ALU.add, ALU.mult))
            one(V.tensor_tensor(t1[:, :], t1[:, :], nv[:, :], ALU.mult))
            dve.sem_inc(S["mlp_free"], 1)
            dve.sem_inc(S["mlp_used"], 1)
            for h in range(2):
                fill[h].n = 2 * CE // 2 * 16
            ma, mg = views("mlp_a", "mlp_g")
            with loop(dve, NBLK, {own: 2 * D + 2 + 4 * R // 4, ma: 5 * R // 4, mg: R // 4, fill[0]: H, fill[1]: H}) as i:
                for h in range(2):
                    dve.wait_ge(fill[h].sem, fill[h].up(H))
                    scans(2 * i + h, lambda f: ring[:, h, :, f])
                    dve.sem_inc(S["ring_free"], 1)
                cols = bass.ds(i * R, R)
                V.tensor_tensor(ohs, down(iotaz[:, :]), along(zbs[:, cols], Z), ALU.is_equal).then_inc(own.sem, own.add())
                one(V.tensor_tensor(ohd, down(iotaz[:, :]), along(zbd[:, cols], Z), ALU.is_equal))
                dve.sem_inc(S["hots"], 1)
                for g in range(R // 4):
                    c4 = bass.ds(i * R + 4 * g, 4)
                    dve.wait_ge(ma.sem, ma.up(5))
                    one(V.tensor_tensor(prod, psB[:, 0:4 * G].rearrange("p (c g) -> p c g", g=G), ejs, ALU.mult))
                    one(V.tensor_reduce(lg[:, :], prod, X, ALU.add))
                    dve.wait_ge(mg.sem, mg.up())
                    one(V.tensor_tensor(gsum, psG[:, 0:4 * D].rearrange("p (c d) -> p c d", d=D), along(lg[:, :]), ALU.add))
                    dve.sem_inc(S["mlp_used"], 1)
                    one(V.tensor_tensor(GX[:, c4, 0:D], gsum, along(t1[:, c4]), ALU.mult))
                dve.sem_inc(S["mlp_free"], 1)
            V.tensor_copy(GX[:, :, D], nv[:, :]).then_inc(own.sem, own.add())
            one(V.tensor_copy(GX[:, :, D + 1].bitcast(I32), dstI[:, :]))
            dve.sem_inc(S["rec_ready"], 1)

            carries(False)
            one(V.tensor_scalar(t0[:, :], cnt[:, :], 1.0, None, ALU.max))
            ask_act()
            one(V.reciprocal(t0[:, :], t0[:, :]))
            one(V.tensor_scalar(t1[:, :], dg[:, :], 1.0, None, ALU.max))
            ask_act()
            one(V.reciprocal(t1[:, :], t1[:, :]))
            one(V.tensor_scalar(dg[:, :], dg[:, :], 1.0, None, ALU.min))
            one(V.tensor_tensor(t1[:, :], t1[:, :], dg[:, :], ALU.mult))

            def update_by_product():
                with loop(dve, NBLK, {own: 2 + 1 + 4 + NORM1, mm: 4, squared: 1, std_ready: 1}) as i:
                    cols = bass.ds(i * R, R)
                    carried(cols)
                    one(V.tensor_tensor(su[:, :, :], M[:, cols, :], along(t0[:, cols]), ALU.mult))
                    dve.sem_inc(S["h_ready"], 1)
                    taken(0, lambda g, n: XS[:, bass.ds(i * R + 8 * g, n), :])
                    norm([(0, DU[0], DU[0], XS[:, cols, :])])
                    dve.sem_inc(S["rows_new"], 1)
            update_by_product()

            one(V.tensor_tensor(M, XS[:, :, :], along(end[:, :]), ALU.mult))
            one(V.tensor_scalar(t0[:, :], end[:, :], -1.0, 1.0, ALU.mult, ALU.add))
            for f in range(D):
                V.tensor_tensor_scan(M[:, ::-1, f], t0[:, ::-1], M[:, ::-1, f], 0.0, ALU.mult, ALU.add).then_inc(own.sem, own.add())
            dve.wait_ge(own.sem, own.now())
            V.memset(shT[:, P:P + 1], 0.0).then_inc(own.sem, own.add())
            one(V.tensor_copy(tail[:, 0:D], M[:, 0, :]))
            ask_pe()
            one(V.tensor_copy(tailT[:, :], psG[0:D + 1, 0:P]))
            one(V.tensor_tensor_scan(shT[:, 0:P][:, ::-1], restT[:, ::-1], tailT[:, ::-1], 0.0, ALU.mult, ALU.add))
            ask_pe()
            one(V.tensor_copy(carry[:, :], psG[:, P:P + D + 1]))
            with loop(dve, NBLK, {own: 3}) as i:
                cols = bass.ds(i * R, R)
                carried(cols, suf)
                one(V.tensor_tensor(M[:, cols, :], M[:, cols, :], along(t1[:, cols]), ALU.mult))
            dve.sem_inc(S["rec_ready"], 1)

            one(V.tensor_copy(va[0:SORT_P, :], vb[0:SORT_P, :].bitcast(I32)))
            one(V.memset(vb[96:P, :], 3.4028234e38))
            one(V.tensor_scalar(vb[0:SORT_P, :], va[0:SORT_P, :], float(HALF_NODES), float(65536 - HALF_NODES),
                                ALU.is_ge, ALU.mult))
            one(V.scalar_tensor_tensor(va[0:SORT_P, :], va[0:SORT_P, :], 256.0, vb[0:SORT_P, :], ALU.add, ALU.add))
            vi = vb[0:SORT_P, :].bitcast(I32)
            one(V.tensor_copy(vi, va[0:SORT_P, :]))
            one(V.tensor_scalar(vi, vi, 15, None, ALU.logical_shift_left))
            one(V.tensor_tensor(vi, vi, pos[0:SORT_P, :], ALU.bitwise_or))
            now = [vb, va]

            def compare(d):
                lo, hi = (now[0][:, :].rearrange("p (b two d) -> p b two d", two=2, d=d)[:, :, j, :] for j in range(2))
                a, b = (now[1][:, :].rearrange("p (b two d) -> p b two d", two=2, d=d)[:, :, j, :] for j in range(2))
                V.tensor_tensor(a, lo, hi, ALU.min).then_inc(own.sem, own.add())
                one(V.tensor_tensor(b, lo, hi, ALU.max))
                now.reverse()

            def turned():
                dve.sem_inc(S["ask_pe"], 1)
                dve.wait_ge(pe_done.sem, pe_done.up())
                one(V.tensor_copy(now[1][:, :], psT[0][:, 0:SORT_C]))
                now.reverse()

            def negate(m):
                v = now[0][:, :].rearrange("p (b two d) -> p b two d", two=2, d=1 << m)[:, :, 1, :]
                one(V.tensor_scalar(v, v, -1.0, None, ALU.mult))

            for m in range(1, 16):
                if m >= 9:
                    one(V.tensor_scalar(now[0][:, :], now[0][:, :], psgn[:, m - 8:m - 7], None, ALU.mult))
                elif m == 8:
                    negate(7)
                    one(V.tensor_scalar(now[0][:, :], now[0][:, :], psgn[:, 0:1], None, ALU.mult))
                else:
                    if m > 1:
                        negate(m - 1)
                    negate(m)
                if m > 8:
                    turned()
                    for b in range(m - 9, -1, -1):
                        compare(1 << b)
                    turned()
                for b in range(min(m, 8) - 1, -1, -1):
                    compare(1 << b)
            assert now[0] is vb
            dve.sem_inc(S["srt_ready"], 1)

            dve.wait_ge(S["srt_ld"], 16 * 3)
            dve.wait_ge(S["s_done"], 2)
            one(V.tensor_scalar(dstI[:, :], t0[:, :].bitcast(I32), 0x7FFF, None, ALU.bitwise_and))
            for t in (t0, keyn, cont):
                V.tensor_scalar(t[:, :].bitcast(I32), t[:, :].bitcast(I32), 15, None, ALU.logical_shift_right).then_inc(own.sem, own.add())
            dve.wait_ge(own.sem, own.now())
            V.tensor_copy(key[:, :], t0[:, :].bitcast(I32)).then_inc(own.sem, own.add())
            V.tensor_copy(dg[:, :], keyn[:, :].bitcast(I32)).then_inc(own.sem, own.add())
            one(V.tensor_copy(cnt[:, :], cont[:, :].bitcast(I32)))
            order(key[:, :], dg[:, :], cnt[:, :])
            one(V.tensor_scalar(t0[:, :], key[:, :], 65536.0, -float(65536 - HALF_NODES), ALU.is_ge, ALU.mult))
            one(V.scalar_tensor_tensor(key[:, :], key[:, :], -256.0, t0[:, :], ALU.add, ALU.add))
            one(V.tensor_copy(srcI[:, :], key[:, :]))
            writers(key[:, :])
            one(V.memset(t0[:, :], 1.0))
            counts(t0[:, :])

            with loop(dve, NBLK, {own: 2 * (2 + NORM2), ld[0]: 2, ld[1]: 2, st[0]: 4, st[1]: 4,
                                  squared: PER, std_ready: PER}) as i:
                for q in range(PER // 2):
                    for h in range(2):
                        dve.wait_ge(ld[h].sem, ld[h].up())
                        dve.wait_ge(st[h].sem, st[h].now())
                        V.tensor_tensor(DU[h], wide(h, D), down(rows[:, 0, :]), ALU.add).then_inc(own.sem, own.add())
                        st[h].n += 32
                    dve.wait_ge(own.sem, own.now())
                    dve.sem_inc(S["in_free"], 2)
                    norm(pair)
                    dve.sem_inc(S["out_ready"], 2)

            def short3():
                for h in range(2):
                    dve.wait_ge(ld[h].sem, ld[h].up())
                norm([(h, wide(h, D), DU[h], DU[h]) for h in range(2)])
                for what, of in ((ALU.mult, lambda h: down(rows[:, 1, :])), (ALU.add, lambda h: down(rows[:, 2, :])),
                                 (ALU.add, lambda h: wide(h, D))):
                    for h in range(2):
                        V.tensor_tensor(DU[h], DU[h], of(h), what).then_inc(own.sem, own.add())
                    dve.wait_ge(own.sem, own.now())
                dve.sem_inc(S["in_free"], 2)
                for h in range(2):
                    dve.wait_ge(st[h].sem, st[h].now())
                    st[h].n += 16
                norm(pair)
                dve.sem_inc(S["out_ready"], 2)

            for h in range(2):
                fill[h].n = 4 * CE // 2 * 16
            short = {ld[0]: 1, ld[1]: 1, st[0]: 1, st[1]: 1, squared: 4, std_ready: 4}
            with loop(dve, NBLK, {own: 2 * D + 2 * NORM2 + 6, fill[0]: H, fill[1]: H, **short}) as i:
                for h in range(2):
                    dve.wait_ge(fill[h].sem, fill[h].up(H))
                    scans(2 * i + h, lambda f: ring[:, h, :, f])
                    dve.sem_inc(S["scanned"], 1)
                short3()

            dve.wait_ge(kept.sem, kept.up(2 * CE // H))
            carries(True)
            one(V.tensor_copy(t0[:, :], cnt[:, :]))
            ask_act()
            one(V.reciprocal(t0[:, :], t0[:, :]))
            update_by_product()

            for h in range(2):
                assert fill[h].n == 5 * CE // 2 * 16
            with loop(dve, NBLK, {own: 2 + 2 * D + 2 * NORM2 + 6, fill[0]: H, fill[1]: H, **short}) as i:
                for h in range(2):
                    dve.wait_ge(fill[h].sem, fill[h].up(H))
                    cols = bass.ds((2 * i + h) * H, H)
                    one(V.tensor_tensor(M[:, cols, :], ring[:, h, :, 0:D], GX[:, cols, 0:D], ALU.mult))
                    dve.sem_inc(S["ring_free"], 1)
                    scans(2 * i + h, lambda f: M[:, cols, f])
                short3()
            one(V.tensor_copy(nv[:, :], GX[:, :, D]))
            counts(nv[:, :])
            carries(True)
            one(V.tensor_scalar(t0[:, :], cnt[:, :], 1e-8, None, ALU.max))
            one(V.reciprocal(t0[:, :], t0[:, :]))

            with loop(dve, NBLK, {own: 2 + 2 + 3 + 2 * NORM1, squared: 2, std_ready: 2}) as i:
                cols = bass.ds(i * R, R)
                carried(cols)
                one(V.tensor_tensor(su[:, :, :], M[:, cols, :], along(t0[:, cols]), ALU.mult))
                one(V.tensor_tensor(su[:, :, :], su[:, :, :], XS[:, cols, :], ALU.add))
                norm([(0, su[:, :, :], su[:, :, :], su[:, :, :])])
                one(V.tensor_tensor(su[:, :, :], su[:, :, :], down(rows[:, 1, :]), ALU.mult))
                one(V.tensor_tensor(su[:, :, :], su[:, :, :], down(rows[:, 2, :]), ALU.add))
                one(V.tensor_tensor(su[:, :, :], su[:, :, :], XS[:, cols, :], ALU.add))
                norm([(0, su[:, :, :], su[:, :, :], XS[:, cols, :])])
                dve.sem_inc(S["rows_new"], 1)


def kernel(**inputs):
    import ml_dtypes
    import numpy as np
    from concourse import bacc
    from concourse.bass_utils import run_bass_kernel_spmd

    f = {k: np.asarray(v) for k, v in inputs.items()}
    f32 = np.float32

    def padded(a, rows, width):
        out = np.zeros((rows, width), a.dtype)
        out[:a.shape[0], :a.shape[1]] = a
        return out

    def edges(a):
        return np.concatenate([[-1], a, np.full(EP - E, NP - 1), [-1]]).astype(np.int32)

    def twice(w, b):
        out = np.zeros((97, 96), f32)
        out[0:D, 0:D] = w.T
        out[D:96, D:96] = w.T
        out[96, 0:D] = b
        out[96, D:96] = b
        return out

    xaux = np.zeros((NP, XW), f32)
    xaux[:N, 0:D] = f["x"]
    xaux[:N, D] = f["node_vec"]
    xaux[:N, D + 1] = f["node_type_119"].astype(np.int32).view(f32)
    place = np.arange(P)
    psgn = np.ones((P, 8), f32)
    psgn[:, 0] = 1 - 2 * (place & 1)
    for m in range(9, 16):
        now = (place >> (m - 8)) & 1 if m < 15 else 0
        psgn[:, m - 8] = (1 - 2 * now) * (1 - 2 * ((place >> (m - 9)) & 1))
    arrays = {
        "xaux": xaux,
        "src": edges(f["src"]), "dst": edges(f["dst"]),
        "ea48": padded(f["edge_attr_48"], EP, D), "ea40": padded(f["edge_attr_40"], EP, A_DIM),
        "ew": padded(f["edge_weight"][:, None], EP, 1)[:, 0],
        "iota": np.tile(np.arange(CN, dtype=np.int16), (P, 1)),
        "iotaz": np.tile(np.arange(Z), (P, 1)).astype(ml_dtypes.bfloat16),
        "ident": np.eye(P, dtype=f32), "identb": np.eye(P).astype(ml_dtypes.bfloat16),
        "w1b": twice(f["L1_gnn_W"], f["L1_gnn_b"]), "w2b": twice(f["L2_gnn_W"], f["L2_gnn_b"]),
        "wm1": np.ascontiguousarray(f["L3_gnn_W1"].T), "bm1": f["L3_gnn_b1"][:, None],
        "wm2": np.concatenate([f["L3_gnn_W2"].T, f["L3_gnn_b2"][None]]),
        "emb": padded(f["L3_gnn_emb"], Z, G), "embT": np.ascontiguousarray(padded(f["L3_gnn_emb"], Z, G).T),
        "adT": np.ascontiguousarray(f["L3_gnn_adaptW"].T),
        "psgn": psgn, "pos": np.arange(P * SORT_C, dtype=np.int32).reshape(P, SORT_C),
        "b2": f["L2_gnn_b"][None], "gamma": f["L3_gnn_gamma"][None], "beta": f["L3_gnn_beta"][None],
        "eps": f["L0_gnn_eps"][None],
    }
    nc = bacc.Bacc("TRN2", target_bir_lowering=False, num_devices=1)
    aps = {k: nc.dram_tensor(f"in_{k}", a.shape, mybir.dt.from_np(a.dtype), kind="ExternalInput").ap()
           for k, a in arrays.items()}
    out = nc.dram_tensor("out", [NP, D], F32, kind="ExternalOutput").ap()
    bass_gnn(nc, aps, out)
    r = run_bass_kernel_spmd(nc, [{f"in_{k}": a for k, a in arrays.items()}], core_ids=[0])
    return r.results[0]["out"][:N]
```

```python
from contextlib import ExitStack, contextmanager

import concourse.bass as bass
from concourse import mybir

P = 128
D = 48
N = 100000
CN = 784
NP = P * CN
E = 25000
CE = 196
EP = P * CE
R = 28
H = 14
NBLK = CE // R
DBLK = CN // R
PER = DBLK // NBLK
XW = 52
RW = 98
A_DIM = 40
Z = 120
G = 32
EPS = 1e-5
SORT_C = 256
SORT_P = EP // SORT_C
SKIP = float(1 << 20)
HALF_NODES = NP // 2
F32 = mybir.dt.float32
I32 = mybir.dt.int32
I16 = mybir.dt.int16
BF16 = mybir.dt.bfloat16


class Count:

    def __init__(self, sem, step=1):
        self.sem, self.step, self.n, self.turn = sem, step, 0, 0

    def add(self):
        self.n += self.step
        return self.step

    def up(self, times=1):
        self.n += self.step * times
        return self.now()

    def now(self):
        return self.turn + self.n


def sort_turns():
    now, turns = 0, []
    for m in range(1, 16):
        if m > 8:
            turns.append(now)
            now = (now + 1 + m - 8) % 2
            turns.append(now)
            now = (now + 1) % 2
        now = (now + min(m, 8)) % 2
    return turns, now


@contextmanager
def loop(eng, times, per):
    with eng.Fori(0, times) as i:
        before = {c: c.n for c in per}
        for c, k in per.items():
            c.turn = i * (k * c.step)
        yield i
        for c, k in per.items():
            assert c.n - before[c] == k * c.step, (c.sem, c.n - before[c], k * c.step)
            c.turn = 0
    for c, k in per.items():
        c.n = before[c] + times * k * c.step


def bass_gnn(nc, A, OUT):
    ALU, ACT, X = mybir.AluOpType, mybir.ActivationFunctionType, mybir.AxisListType.X
    ctx = ExitStack()
    with ctx:
        def sb(name, shape, dt=F32):
            return ctx.enter_context(nc.sbuf_tensor(name, shape, dt))

        def ps(name):
            return ctx.enter_context(nc.psum_tensor(name, [P, 512], F32))

        def sem(name):
            return ctx.enter_context(nc.semaphore(name))

        def dram(name, shape, dt=F32):
            return nc.dram_tensor(name, shape, dt, kind="Internal").ap()

        XA = dram("xa_table", [NP, XW])
        X1 = dram("x1_table", [NP, D])
        Y1 = dram("y1_table", [NP, D])
        X2 = dram("x2_table", [NP, D])
        X3 = dram("x3_table", [NP, D])
        X3C = dram("x3_copy", [NP, D])
        REC = dram("edge_records", [EP, RW])
        SRT = dram("sorted_src", [P * SORT_C + 2], I32)

        def blk(table, k, w=D):
            return table.rearrange("(p c) d -> p c d", p=P)[:, bass.ds(k * R, R), 0:w]

        MG = sb("MG", [P, 1 + CE, D])
        M = MG[:, 1:1 + CE, :]
        XS = sb("XS", [P, CE, D])
        GX = sb("GX", [P, CE, D + 2])
        ring = sb("ring", [P, 2, H, RW])
        idx = sb("idx", [P, 2, H], I32)
        stage = sb("stage", [P, 2, H, D])
        din = sb("din", [P, 2, R * XW])
        du = sb("du", [P, 2, R, D])
        sq = sb("sq", [P, 2, R, D])
        do = sb("do", [P, 2, R, D])
        su = sb("su", [P, R, D])
        hT = sb("hT", [97, 2, 512])
        mu = sb("mu", [P, 2, R])
        var = sb("var", [P, 2, R])
        std = sb("std", [P, 2, R])
        c2s = sb("c2s", [P, 1])
        srs = sb("srs", [P, 2, R])
        deg = sb("deg", [P, CN])
        srcI = sb("srcI", [P, CE], I32)
        dstI = sb("dstI", [P, CE], I32)
        dstS = sb("dstS", [P, CE], I32)
        key = sb("key", [P, CE])
        keyn = sb("keyn", [P, CE])
        cont = sb("cont", [P, CE])
        pre = sb("pre", [P, CE])
        suf = sb("suf", [P, CE])
        end = sb("end", [P, CE])
        cnt = sb("cnt", [P, CE])
        put = sb("put", [P, CE], I32)
        zs = sb("zs", [P, CE])
        zd = sb("zd", [P, CE])
        nv = sb("nv", [P, CE])
        dg = sb("dg", [P, CE])
        t0 = sb("t0", [P, CE])
        t1 = sb("t1", [P, CE])
        tail = sb("tail", [P, D + 1])
        carry = sb("carry", [P, D + 1])
        ident = sb("ident", [P, P])
        identb = sb("identb", [P, P], BF16)
        fullT = sb("fullT", [D + 1, P])
        tailT = sb("tailT", [D + 1, P])
        shT = sb("shT", [D + 1, P + 1])
        w1b = sb("w1b", [97, 96])
        w2b = sb("w2b", [97, 96])
        wm1 = sb("wm1", [A_DIM, D])
        bm1 = sb("bm1", [D, 1])
        wm2 = sb("wm2", [D + 1, D])
        embw = sb("embw", [Z, G])
        embT = sb("embT", [G, Z])
        adT = sb("adT", [G, G])
        eaw = sb("eaw", [Z, G])
        rows = sb("rows", [P, 3, D])
        c2e = sb("c2e", [P, 1])
        lneps = sb("lneps", [P, 1])
        psgn = sb("psgn", [P, 8])
        pos = sb("pos", [P, SORT_C], I32)
        va = sb("va", [P, SORT_C])
        vb = sb("vb", [P, SORT_C])
        zero1 = sb("zero1", [P, 1])
        gflat = GX[:, :, :].rearrange("p c w -> p (c w)")
        iota = gflat[:, 0:CN // 2].bitcast(I16)
        ohc = gflat[:, 400:400 + 2 * CN].bitcast(BF16).rearrange("p (h c) -> p h c", h=4)
        ohp = gflat[:, 2000:2000 + 2 * P].bitcast(BF16).rearrange("p (h c) -> p h c", h=4)
        colf = gflat[:, 2300:2300 + CE]
        parf = gflat[:, 2500:2500 + CE]
        tmpf = gflat[:, 2700:2700 + CE]
        dy = gflat[:, 3000:3000 + 2 * R * D].rearrange("p (h c d) -> p h c d", h=2, d=D)
        ohs = du[:, :, :, :].rearrange("p h c d -> p (h c d)")[:, 0:R * Z // 2].bitcast(BF16).rearrange(
            "p (c z) -> p c z", z=Z)
        ohd = sq[:, :, :, :].rearrange("p h c d -> p (h c d)")[:, 0:R * Z // 2].bitcast(BF16).rearrange(
            "p (c z) -> p c z", z=Z)
        zbs = du[:, :, :, :].rearrange("p h c d -> p (h c d)")[:, 1700:1700 + CE // 2].bitcast(BF16)
        zbd = du[:, :, :, :].rearrange("p h c d -> p (h c d)")[:, 1800:1800 + CE // 2].bitcast(BF16)
        ea = din[:, 0, 0:R * A_DIM].rearrange("p (c a) -> p c a", a=A_DIM)
        doflat = do[:, :, :, :].rearrange("p h c d -> p (h c d)")
        eaT = doflat[0:A_DIM, 0:512]
        h1T = doflat[0:D + 1, 512:1024]
        zT = doflat[0:Z, 1024:2048]
        ejs = [doflat[:, 2048 + 128 * k:2048 + 128 * k + 4 * G].rearrange("p (c g) -> p c g", g=G) for k in range(2)]
        prod = sq[:, 1, R - 4:R, 0:G]
        gsum = doflat[:, 2400:2400 + 4 * D].rearrange("p (c d) -> p c d", d=D)
        lg = sb("lg", [P, 4])
        iotaz = sb("iotaz", [P, Z], BF16)
        cib = sb("cib", [P, R])
        restT = sb("restT", [D + 1, P])
        ew = t1[:, :]
        psT = [ps("psT0"), ps("psT1")]
        psA, psB, psC, psG = ps("psA"), ps("psB"), ps("psC"), ps("psG")
        psO = [ps("psO0"), ps("psO1"), psA, psB]

        S = {n: sem(n) for n in (
            "dve", "act", "pool",
            "consts", "edges", "ea48", "init", "pool_turns", "pe_turns",
            "hot", "counted", "deg_done", "col_ready", "xa_ld0", "xa_ld1", "xa_done",
            "ld0", "ld1", "in_free", "out_ready", "st0", "st1", "short_done",
            "centered", "squared", "var_ready", "std_ready",
            "fill0", "fill1", "ring_free", "kept", "scanned", "xs_free", "sc0", "sc1", "stage_free",
            "rows_ready", "rows_new", "idx_ready", "s_done",
            "h_ready", "trans", "hT_ready", "mm", "mm_used", "ask_act", "act_done", "ask_pe", "pe_done",
            "mlp_ld", "mlp_free", "hots", "mlp_t", "mlp_a", "mlp_o", "mlp_g", "mlp_used",
            "rec_ready", "rec_st", "srt_ready", "srt_st", "srt_ld")}
        FROM_DMA = ("consts", "edges", "ea48", "xa_ld0", "xa_ld1", "ld0", "ld1", "st0", "st1",
                    "fill0", "fill1", "sc0", "sc1", "mlp_ld", "rec_st", "srt_st", "srt_ld")

        def views(*names):
            return [Count(S[n], 16 if n in FROM_DMA else 1) for n in names]

        block = ctx.enter_context(nc.Block())

        @block.sync
        def _(sp):
            consts, edges, ea48 = views("consts", "edges", "ea48")
            for to, of in ((srcI[:, :], A["src"][1:EP + 1]), (dstI[:, :], A["dst"][1:EP + 1]),
                           (t0[:, :].bitcast(I32), A["dst"][2:EP + 2]), (cnt[:, :].bitcast(I32), A["dst"][0:EP]),
                           (ew, A["ew"])):
                sp.dma_start(to, of.rearrange("(p c) -> p c", p=P)).then_inc(edges.sem, edges.add())
            sp.dma_start(vb[0:SORT_P, :].bitcast(I32), A["src"][1:EP + 1].rearrange("(p c) -> p c", p=SORT_P)).then_inc(edges.sem, edges.add())
            for to, name in ((iota, "iota"), (iotaz[:], "iotaz"), (ident[:], "ident"), (identb[:], "identb"),
                             (w1b[:], "w1b"), (w2b[:], "w2b"), (wm1[:], "wm1"), (bm1[:], "bm1"), (wm2[:], "wm2"),
                             (embw[:], "emb"), (embT[:], "embT"), (adT[:], "adT"), (psgn[:], "psgn"), (pos[:], "pos")):
                sp.dma_start(to, A[name]).then_inc(consts.sem, consts.add())
            for j, name in enumerate(("b2", "gamma", "beta")):
                sp.dma_start(rows[:, j, :], A[name].broadcast_to([P, D])).then_inc(consts.sem, consts.add())
            sp.dma_start(c2e[:, :], A["eps"].broadcast_to([P, 1])).then_inc(consts.sem, consts.add())
            sp.dma_start(M, A["ea48"].rearrange("(p c) d -> p c d", p=P)).then_inc(ea48.sem, ea48.add())

            ld, st = views("ld0", "ld1"), views("st0", "st1")
            xld = views("xa_ld0", "xa_ld1")
            col_ready, = views("col_ready")

            def xa_load(h, k):
                sp.dma_start(din[:, h, :], blk(A["xaux"], k, XW).rearrange("p c d -> p (c d)")).then_inc(xld[h].sem, xld[h].add())

            def xa_store(h, k):
                sp.wait_ge(col_ready.sem, col_ready.up())
                sp.dma_start(blk(XA, k, XW).rearrange("p c d -> p (c d)"), din[:, h, :]).then_inc(st[h].sem, st[h].add())

            xa_load(0, 0)
            xa_load(1, 1)
            with loop(sp, DBLK // 2 - 1, {xld[0]: 1, xld[1]: 1, st[0]: 1, st[1]: 1, col_ready: 2}) as i:
                for h in range(2):
                    xa_store(h, 2 * i + h)
                for h in range(2):
                    sp.wait_ge(st[h].sem, st[h].now())
                    xa_load(h, 2 * i + 2 + h)
            for h in range(2):
                xa_store(h, DBLK - 2 + h)
            for h in range(2):
                sp.wait_ge(st[h].sem, st[h].now())
            sp.sem_inc(S["xa_done"], 1)

            in_free, out_ready = views("in_free", "out_ready")

            def load(h, k, table, w):
                sp.wait_ge(in_free.sem, in_free.up())
                sp.dma_start(din[:, h, 0:R * w], blk(table, k, w).rearrange("p c d -> p (c d)")).then_inc(ld[h].sem, ld[h].add())

            def store(h, k, tables):
                sp.wait_ge(out_ready.sem, out_ready.up())
                for buf, table in tables:
                    sp.dma_start(blk(table, k), buf[:, h, :, :]).then_inc(st[h].sem, st[h].add())

            def dense(table, w, tables, before=None):
                if before:
                    before()
                for h in range(2):
                    load(h, h, table, w)
                with loop(sp, DBLK // 2 - 1, {ld[0]: 1, ld[1]: 1, in_free: 2, out_ready: 2,
                                              st[0]: len(tables), st[1]: len(tables)}) as i:
                    for h in range(2):
                        load(h, 2 * i + 2 + h, table, w)
                    for h in range(2):
                        store(h, 2 * i + h, tables)
                for h in range(2):
                    store(h, DBLK - 2 + h, tables)
                for h in range(2):
                    sp.wait_ge(st[h].sem, st[h].now())
                sp.sem_inc(S["short_done"], 1)

            dense(A["xaux"], XW, [(do, X1), (dy, Y1)])
            dense(X1, D, [(do, X2)])

            mld, mfree = views("mlp_ld", "mlp_free")
            with loop(sp, NBLK, {mld: 1, mfree: 1}) as i:
                sp.wait_ge(mfree.sem, mfree.up())
                sp.dma_start(ea, A["ea40"].rearrange("(p c) a -> p c a", p=P)[:, bass.ds(i * R, R), :]).then_inc(mld.sem, mld.add())

            rec_ready, rec_st = views("rec_ready", "rec_st")
            recv = REC.rearrange("(p c) w -> p c w", p=P)
            sp.wait_ge(rec_ready.sem, rec_ready.up())
            sp.dma_start(recv[:, :, D:RW], GX[:, :, :]).then_inc(rec_st.sem, rec_st.add())
            sp.wait_ge(rec_ready.sem, rec_ready.up())
            sp.dma_start(recv[:, :, 0:D], M).then_inc(rec_st.sem, rec_st.add())
            srt_ready, srt_st, srt_ld = views("srt_ready", "srt_st", "srt_ld")
            sp.wait_ge(srt_ready.sem, srt_ready.up())
            sp.dma_start(SRT[1:P * SORT_C + 1].rearrange("(p c) -> p c", p=P), vb[:, :].bitcast(I32)).then_inc(srt_st.sem, srt_st.add())
            sp.dma_start(SRT[0:1].rearrange("(p c) -> p c", p=1), zero1[0:1, 0:1].bitcast(I32)).then_inc(srt_st.sem, srt_st.add())
            sp.wait_ge(srt_st.sem, srt_st.now())
            for at, to in ((1, t0), (2, keyn), (0, cont)):
                sp.dma_start(to[:, :].bitcast(I32), SRT[at:at + EP].rearrange("(p c) -> p c", p=P)).then_inc(srt_ld.sem, srt_ld.add())

            s_done, = views("s_done")

            def scattered():
                sp.wait_ge(s_done.sem, s_done.up(2))
            dense(X2, D, [(do, X3), (do, X3C)], scattered)
            dense(X3C, D, [(do, OUT)])
            sp.wait_ge(s_done.sem, s_done.up(2))

        @block.gpsimd
        def _(pool):
            own, = views("pool")
            fill, sc = views("fill0", "fill1"), views("sc0", "sc1")
            ring_free, rows_ready = views("ring_free", "rows_ready")
            idx_ready, short_done, edges, rec_st = views("idx_ready", "short_done", "edges", "rec_st")
            last_row = pool.to_reg(NP - 1)

            def indices(h, c, of):
                nc.gpsimd.tensor_copy(idx[:, h, :], of[:, bass.ds(c * H, H)]).then_inc(own.sem, own.add())
                pool.wait_ge(own.sem, own.now())
                pool.sem_inc(S["pool_turns"], 1)

            def gather(table, w, of):
                with loop(pool, NBLK, {own: 2, ring_free: 2, fill[0]: H, fill[1]: H}) as i:
                    for h in range(2):
                        pool.wait_ge(ring_free.sem, ring_free.up())
                        indices(h, 2 * i + h, of)
                        for t in range(H):
                            pool.indirect_dma_start(
                                ring[:, h, t, 0:w], None, table,
                                bass.IndirectOffsetOnAxis(ap=idx[:, h, t:t + 1], axis=0)).then_inc(fill[h].sem, fill[h].add())
                for h in range(2):
                    pool.wait_ge(fill[h].sem, fill[h].now())

            def scatter_turn(table, c, h, first):
                pool.wait_ge(rows_ready.sem, rows_ready.up())
                indices(h, c, put)
                for t in range(H):
                    pool.indirect_dma_start(
                        table, bass.IndirectOffsetOnAxis(ap=idx[:, h, t:t + 1], axis=0),
                        stage[:, h, t, :], None, bounds_check=last_row, oob_is_err=False).then_inc(sc[h].sem, sc[h].add())
                    if t == H // 2 and not first:
                        pool.wait_ge(sc[1 - h].sem, sc[1 - h].now())
                        pool.sem_inc(S["stage_free"], 1)

            def scatter(table):
                scatter_turn(table, 0, 0, True)
                scatter_turn(table, 1, 1, False)
                with loop(pool, NBLK - 1, {own: 2, rows_ready: 2, sc[0]: H, sc[1]: H}) as i:
                    scatter_turn(table, 2 * i + 2, 0, False)
                    scatter_turn(table, 2 * i + 3, 1, False)
                pool.wait_ge(sc[1].sem, sc[1].now())
                pool.sem_inc(S["stage_free"], 1)
                pool.sem_inc(S["s_done"], 1)

            pool.wait_ge(edges.sem, edges.up(6))
            gather(A["xaux"], XW, srcI)
            pool.wait_ge(S["xa_done"], 1)
            gather(XA, XW, dstI)
            pool.wait_ge(idx_ready.sem, idx_ready.up())
            pool.wait_ge(short_done.sem, short_done.up())
            scatter(Y1)
            gather(Y1, D, srcI)
            pool.wait_ge(short_done.sem, short_done.up())
            scatter(X2)
            pool.wait_ge(idx_ready.sem, idx_ready.up())
            gather(X2, D, srcI)
            pool.wait_ge(rec_st.sem, rec_st.up(2))
            gather(REC, RW, dstI)
            pool.wait_ge(short_done.sem, short_done.up())
            scatter(X3)
            gather(X3, D, dstS)
            pool.wait_ge(short_done.sem, short_done.up())
            scatter(OUT)

        @block.scalar
        def _(act):
            own, = views("act")
            fill = views("fill0", "fill1")
            centered, var_ready, xs_free, rows_new, stage_free, scanned = views(
                "centered", "var_ready", "xs_free", "rows_new", "stage_free", "scanned")
            trans, ask = views("trans", "ask_act")
            act.wait_ge(S["init"], 1)
            act.wait_ge(S["consts"], 16 * 18)
            act.sem_inc(S["ring_free"], 2)
            act.sem_inc(S["stage_free"], 2)

            def take(h, uses, also=None):
                act.wait_ge(fill[h].sem, fill[h].up(H))
                for to, of in uses:
                    nc.scalar.activation(to, of, ACT.Copy).then_inc(own.sem, own.add())
                act.wait_ge(own.sem, own.now())
                if also:
                    act.wait_ge(also.sem, also.up())
                act.sem_inc(S["ring_free"], 1)
                act.sem_inc(S["kept"], 1)

            def squares(units):
                for h, u in units:
                    act.wait_ge(centered.sem, centered.up())
                    nc.scalar.activation(sq[:, h, :, :], u, ACT.Square).then_inc(S["squared"], 1)

            def roots(units, scale=1.0 / D):
                for h, u in units:
                    act.wait_ge(var_ready.sem, var_ready.up())
                    nc.scalar.activation(std[:, h, :], var[:, h, :], ACT.Sqrt, bias=lneps[:, 0:1],
                                         scale=scale).then_inc(S["std_ready"], 1)

            def norm(units, scale=1.0 / D):
                squares(units)
                roots(units, scale)

            def evacuate(groups=range(4)):
                for g in groups:
                    w = 256 if g == 3 else 512
                    act.wait_ge(trans.sem, trans.up())
                    nc.scalar.activation(hT[0:96, g % 2, 0:w], psT[g % 2][0:96, 0:w], ACT.Copy
                                         ).then_inc(S["hT_ready"], 1)

            def to_stage(of, i):
                act.wait_ge(rows_new.sem, rows_new.up())
                for h in range(2):
                    act.wait_ge(stage_free.sem, stage_free.up())
                    nc.scalar.activation(stage[:, h, :, :], of[:, bass.ds((2 * i + h) * H, H), :], ACT.Copy
                                         ).then_inc(S["rows_ready"], 1)

            def function(of, what=ACT.Sqrt):
                act.wait_ge(ask.sem, ask.up())
                nc.scalar.activation(of, of, what).then_inc(S["act_done"], 1)

            pair = [(0, du[:, 0, :, :]), (1, du[:, 1, :, :])]

            with loop(act, NBLK, {own: 4, fill[0]: H, fill[1]: H}) as i:
                for h in range(2):
                    cols = bass.ds((2 * i + h) * H, H)
                    take(h, [(XS[:, cols, :], ring[:, h, :, 0:D]),
                             (zs[:, cols], ring[:, h, :, D + 1].bitcast(I32))])
            function(deg[:, :])

            with loop(act, NBLK, {own: 8, fill[0]: H, fill[1]: H, xs_free: 2, centered: PER + 1,
                                  var_ready: PER + 1, ask: 1}) as i:
                act.wait_ge(xs_free.sem, xs_free.up(2))
                for h in range(2):
                    cols = bass.ds((2 * i + h) * H, H)
                    take(h, [(XS[:, cols, :], ring[:, h, :, 0:D]),
                             (nv[:, cols], ring[:, h, :, D]),
                             (zd[:, cols], ring[:, h, :, D + 1].bitcast(I32)),
                             (dg[:, cols], ring[:, h, :, D + 3])])
                for _ in range(PER // 2):
                    norm(pair, c2s[:, 0:1])
                function(cib[:, :])
                norm([(0, su[:, :, :])])

            def short1(i, last=False):
                to_stage(M, i)
                for q in range(PER // 2):
                    ahead = not (last and q == PER // 2 - 1)
                    evacuate()
                    squares(pair)
                    if ahead:
                        evacuate((0, 1))
                    roots(pair)
                    if ahead:
                        evacuate((2, 3))
            evacuate()
            with loop(act, NBLK - 1, {stage_free: 2, rows_new: 1, centered: PER, var_ready: PER, trans: 4 * PER}) as i:
                short1(i)
            short1(NBLK - 1, True)

            function(t1[:, :], ACT.Sin)
            mt, mo = views("mlp_t", "mlp_o")
            with loop(act, NBLK, {mt: 3 * R // 4, mo: R // 4}) as i:
                def operands():
                    act.wait_ge(mt.sem, mt.up())
                    nc.scalar.activation(zT, psO[0][0:Z, :].bitcast(BF16), ACT.Copy).then_inc(S["mlp_a"], 1)
                    act.wait_ge(mt.sem, mt.up())
                    nc.scalar.activation(eaT, psT[0][0:A_DIM, :], ACT.Copy).then_inc(S["mlp_a"], 1)
                operands()
                for g in range(R // 4):
                    act.wait_ge(mo.sem, mo.up())
                    nc.scalar.activation(ejs[g % 2], (psB, psC)[g % 2][:, 4 * G:8 * G].rearrange("p (c g) -> p c g", g=G),
                                         ACT.Copy).then_inc(S["mlp_a"], 1)
                    act.wait_ge(mt.sem, mt.up())
                    nc.scalar.activation(h1T[0:D, :], psA[0:D, :], ACT.Silu, bias=bm1[:, 0:1]).then_inc(S["mlp_a"], 1)
                    if g + 1 < R // 4:
                        operands()

            function(t0[:, :])
            function(t1[:, :])
            with loop(act, NBLK, {stage_free: 2, rows_new: 1, centered: 1, var_ready: 1, trans: 4}) as i:
                evacuate()
                norm(pair[:1])
                to_stage(XS, i)

            for h in range(2):
                fill[h].n += 16 * CE // 2
            with loop(act, NBLK, {own: 2, fill[0]: H, fill[1]: H, centered: PER, var_ready: PER}) as i:
                for h in range(2):
                    cols = bass.ds((2 * i + h) * H, H)
                    take(h, [(XS[:, cols, :], ring[:, h, :, 0:D])])
                for _ in range(PER // 2):
                    norm(pair)

            function(deg[:, :])

            with loop(act, NBLK, {own: 4, scanned: 2, fill[0]: H, fill[1]: H, centered: 2, var_ready: 2}) as i:
                for h in range(2):
                    cols = bass.ds((2 * i + h) * H, H)
                    take(h, [(GX[:, cols, 0:D + 1], ring[:, h, :, D:RW - 1]),
                             (dstS[:, cols], ring[:, h, :, RW - 1].bitcast(I32))], scanned)
                norm(pair)

            function(t0[:, :])
            with loop(act, NBLK, {stage_free: 2, rows_new: 1, centered: 1, var_ready: 1, trans: 4}) as i:
                evacuate()
                norm(pair[:1])
                to_stage(XS, i)

            with loop(act, NBLK, {centered: 2, var_ready: 2}) as i:
                norm(pair)

            with loop(act, NBLK, {stage_free: 2, rows_new: 1, centered: 2, var_ready: 2}) as i:
                norm([(0, su[:, :, :])])
                norm([(0, su[:, :, :])])
                to_stage(XS, i)

        @block.tensor
        def _(pe):
            T = nc.tensor
            hot, ask, h_ready, hT_ready, mm_used = views("hot", "ask_pe", "h_ready", "hT_ready", "mm_used")
            ld = views("ld0", "ld1")
            pe.wait_ge(S["consts"], 16 * 18)
            pe.wait_ge(S["init"], 1)

            def flip():
                pe.wait_ge(ask.sem, ask.up())
                T.transpose(psG[0:D + 1, 0:P], tail[:, :], ident[:, :]).then_inc(S["pe_done"], 1)

            def flip_back(at):
                pe.wait_ge(ask.sem, ask.up())
                T.transpose(psG[:, P:P + D + 1], shT[:, at:at + P], ident[0:D + 1, 0:D + 1]).then_inc(S["pe_done"], 1)

            def product(blocks, weights):
                def turn(k):
                    rows_of, h = blocks[k // 4]
                    g = k % 4
                    if g == 0 and h is not None:
                        pe.wait_ge(ld[h].sem, ld[h].up())
                    for j in range(2 if g == 3 else 4):
                        last = T.transpose(psT[g % 2][0:96, j * P:(j + 1) * P],
                                           rows_of[:, (4 * g + j) * 96:(4 * g + j + 1) * 96], ident[:, :])
                    last.then_inc(S["trans"], 1)

                turn(0)
                turn(1)
                for k in range(4 * len(blocks)):
                    g = k % 4
                    pe.wait_ge(hT_ready.sem, hT_ready.up())
                    pe.wait_ge(mm_used.sem, mm_used.up())
                    for j in range(2 if g == 3 else 4):
                        last = T.matmul(psO[g][:, j * 96:(j + 1) * 96], hT[0:97, g % 2, j * P:(j + 1) * P],
                                        weights[:, :], start=True, stop=True)
                    last.then_inc(S["mm"], 1)
                    if k + 2 < 4 * len(blocks):
                        turn(k + 2)

            T.matmul(psG[0:Z, 0:G], embT[:, :], adT[:, :], start=True, stop=True).then_inc(S["pe_done"], 1)
            flip()
            flip()

            pe.sem_inc(S["counted"], 4)

            def count_edges(g, start, stop):
                pe.wait_ge(hot.sem, hot.up())
                for c in range(2):
                    last = T.matmul((psA, psB)[c][:, 0:CN // 2], ohp[:, g, :],
                                    ohc[:, g, c * (CN // 2):(c + 1) * (CN // 2)],
                                    start=start, stop=stop, skip_group_check=True)
                last.then_inc(S["counted"], 1)
            for g in range(4):
                count_edges(g, g == 0, False)
            with loop(pe, CE // 4 - 2, {hot: 4}) as i:
                for g in range(4):
                    count_edges(g, False, False)
            for g in range(4):
                count_edges(g, False, g == 3)

            flip()
            flip_back(0)
            for h in range(2):
                ld[h].n = 16 * DBLK // 2
            with loop(pe, NBLK, {ld[0]: PER // 2, ld[1]: PER // 2, hT_ready: 4 * PER, mm_used: 4 * PER}) as i:
                for _ in range(PER // 2):
                    product([(din[:, h, :], h) for h in range(2)], w1b)

            hots, mld, ma, mused = views("hots", "mlp_ld", "mlp_a", "mlp_used")
            with loop(pe, NBLK, {hots: 1, mld: 1, ma: 4 * R // 4, mused: R // 4}) as i:
                def operands(g):
                    for k, oh in enumerate((ohs, ohd)):
                        for j in range(4):
                            last = T.transpose(psO[0][0:Z, :].bitcast(BF16)[:, (4 * k + j) * P:(4 * k + j + 1) * P],
                                               oh[:, 4 * g + j, :], identb[:, :])
                    last.then_inc(S["mlp_t"], 1)
                    for j in range(4):
                        last = T.transpose(psT[0][0:A_DIM, j * P:(j + 1) * P], ea[:, 4 * g + j, :], ident[:, :])
                    last.then_inc(S["mlp_t"], 1)

                pe.wait_ge(hots.sem, hots.up())
                pe.wait_ge(mld.sem, mld.up())
                pe.sem_inc(S["pe_turns"], 1)
                operands(0)
                for g in range(R // 4):
                    bank = (psB, psC)[g % 2]
                    pe.wait_ge(ma.sem, ma.up())
                    pe.wait_ge(mused.sem, mused.up())
                    for j in range(4):
                        T.matmul(bank[:, j * G:(j + 1) * G], zT[:, j * P:(j + 1) * P], embw[:, :], start=True, stop=True)
                        last = T.matmul(bank[:, (4 + j) * G:(5 + j) * G], zT[:, (4 + j) * P:(5 + j) * P], eaw[:, :],
                                        start=True, stop=True)
                    last.then_inc(S["mlp_o"], 1)
                    pe.wait_ge(ma.sem, ma.up())
                    pe.sem_inc(S["pe_turns"], 1)
                    T.matmul(psA[0:D, :], wm1[:, :], eaT, start=True, stop=True).then_inc(S["mlp_t"], 1)
                    if g + 1 < R // 4:
                        operands(g + 1)
                    pe.wait_ge(ma.sem, ma.up(2))
                    for j in range(4):
                        last = T.matmul((psG, psT[1])[g % 2][:, j * D:(j + 1) * D],
                                        h1T[:, j * P:(j + 1) * P], wm2[:, :], start=True, stop=True)
                    last.then_inc(S["mlp_g"], 1)

            flip()
            flip_back(0)
            su_rows = su[:, :, :].rearrange("p c d -> p (c d)")

            def products(weights):
                with loop(pe, NBLK, {h_ready: 1, hT_ready: 4, mm_used: 4}) as i:
                    pe.wait_ge(h_ready.sem, h_ready.up())
                    product([(su_rows, None)], weights)
            products(w1b)
            flip()
            flip_back(1)
            for n in sort_turns()[0]:
                pe.wait_ge(ask.sem, ask.up())
                for h in range(2):
                    last = T.transpose(psT[0][:, h * P:(h + 1) * P], (vb, va)[n][:, h * P:(h + 1) * P], ident[:, :])
                last.then_inc(S["pe_done"], 1)
            flip()
            flip()
            flip_back(0)
            products(w2b)
            flip()
            flip_back(0)

        @block.vector
        def _(dve):
            V = nc.vector
            own, = views("dve")

            def one(instruction):
                instruction.then_inc(own.sem, own.add())
                dve.wait_ge(own.sem, own.now())

            def along(t, w=D):
                return t.unsqueeze(2).broadcast_to([P, t.shape[1], w])

            def down(t, n=R):
                return t.unsqueeze(1).broadcast_to([P, n, t.shape[1]])

            act_done, pe_done = views("act_done", "pe_done")
            ld, st, xld = views("ld0", "ld1"), views("st0", "st1"), views("xa_ld0", "xa_ld1")
            squared, std_ready, kept, mm, counted = views("squared", "std_ready", "kept", "mm", "counted")
            mm_used, = views("mm_used")
            fill = views("fill0", "fill1")

            def ask_act():
                dve.sem_inc(S["ask_act"], 1)
                dve.wait_ge(act_done.sem, act_done.up())

            def ask_pe():
                dve.sem_inc(S["ask_pe"], 1)
                dve.wait_ge(pe_done.sem, pe_done.up())

            V.memset(hT[:, :, :], 1.0).then_inc(own.sem, own.add())
            V.memset(lneps[:, :], EPS).then_inc(own.sem, own.add())
            V.memset(zero1[:, :], 0.0).then_inc(own.sem, own.add())
            V.memset(MG[:, 0:1, :], 0.0).then_inc(own.sem, own.add())
            dve.wait_ge(S["consts"], 16 * 18)
            one(V.tensor_scalar(c2e[:, :], c2e[:, :], 2.0, None, ALU.add))
            one(V.tensor_scalar(rows[:, 0, :], rows[:, 0, :], 0.0, None, ALU.max))
            dve.sem_inc(S["init"], 1)
            dve.sem_inc(mm_used.sem, mm_used.up(4))
            dve.sem_inc(S["in_free"], 2)
            dve.wait_ge(pe_done.sem, pe_done.up())
            one(V.tensor_copy(eaw[:, :], psG[0:Z, 0:G]))

            def flipped(to, column):
                one(V.tensor_copy(tail[:, :], column.broadcast_to([P, D + 1])))
                ask_pe()
                one(V.tensor_copy(to[:, :], psG[0:D + 1, 0:P]))

            def order(key, after, before):
                V.tensor_tensor(end[:, :], key, after, ALU.not_equal).then_inc(own.sem, own.add())
                one(V.tensor_tensor(cont[:, :], key, before, ALU.is_equal))
                V.tensor_scalar(carry[:, 0:1], end[:, CE - 1:CE], -1.0, 1.0, ALU.mult, ALU.add).then_inc(own.sem, own.add())
                one(V.tensor_scalar(pre[:, :], key, key[:, 0:1], cont[:, 0:1], ALU.is_equal, ALU.mult))
                one(V.tensor_scalar(suf[:, :], key, key[:, CE - 1:CE], carry[:, 0:1], ALU.is_equal, ALU.mult))
                flipped(fullT, pre[:, CE - 1:CE])

            def writers(node):
                one(V.tensor_scalar(t0[:, :], end[:, :], -SKIP, SKIP, ALU.mult, ALU.add))
                one(V.tensor_tensor(t0[:, :], t0[:, :], node, ALU.add))
                one(V.tensor_copy(put[:, :], t0[:, :]))
                dve.sem_inc(S["idx_ready"], 1)

            dve.wait_ge(S["edges"], 16 * 6)
            V.tensor_copy(key[:, :], dstI[:, :]).then_inc(own.sem, own.add())
            V.tensor_copy(keyn[:, :], t0[:, :].bitcast(I32)).then_inc(own.sem, own.add())
            one(V.tensor_copy(dg[:, :], cnt[:, :].bitcast(I32)))
            order(key[:, :], keyn[:, :], dg[:, :])
            flipped(restT, suf[:, 0:1])
            writers(key[:, :])

            one(V.tensor_copy(colf, srcI[:, :]))
            one(V.tensor_scalar(tmpf, colf, 1.0 / CN, None, ALU.mult))
            one(V.tensor_copy(keyn[:, :].bitcast(I32), tmpf))
            one(V.tensor_copy(parf, keyn[:, :].bitcast(I32)))
            one(V.scalar_tensor_tensor(colf, parf, -float(CN), colf, ALU.mult, ALU.add))
            one(V.tensor_scalar(tmpf, colf, 0.0, None, ALU.is_lt))
            V.tensor_tensor(parf, parf, tmpf, ALU.subtract).then_inc(own.sem, own.add())
            one(V.scalar_tensor_tensor(colf, tmpf, float(CN), colf, ALU.mult, ALU.add))
            one(V.tensor_scalar(tmpf, colf, float(CN), None, ALU.is_ge))
            V.tensor_tensor(parf, parf, tmpf, ALU.add).then_inc(own.sem, own.add())
            one(V.scalar_tensor_tensor(colf, tmpf, -float(CN), colf, ALU.mult, ALU.add))
            with loop(dve, CE // R, {counted: R}) as i:
                for t in range(R):
                    g = t % 4
                    dve.wait_ge(counted.sem, counted.up())
                    V.tensor_scalar(ohp[:, g, :], iota[:, 0:P], parf[:, bass.ds(i * R + t, 1)], None, ALU.is_equal)
                    V.tensor_scalar(ohc[:, g, :], iota[:, :], colf[:, bass.ds(i * R + t, 1)], None, ALU.is_equal
                                    ).then_inc(S["hot"], 1)
            dve.wait_ge(counted.sem, counted.up(4))
            V.tensor_copy(deg[:, 0:CN // 2], psA[:, 0:CN // 2]).then_inc(own.sem, own.add())
            one(V.tensor_copy(deg[:, CN // 2:CN], psB[:, 0:CN // 2]))

            def scans(c, of):
                cols = bass.ds(c * H, H)
                for f in range(D):
                    V.tensor_tensor_scan(M[:, cols, f], cont[:, cols], of(f), MG[:, bass.ds(c * H, 1), f],
                                            ALU.mult, ALU.add).then_inc(own.sem, own.add())
                dve.wait_ge(own.sem, own.now())

            dve.wait_ge(S["ea48"], 16)
            with loop(dve, DBLK // 2, {own: 2 + D, xld[0]: 1, xld[1]: 1, kept: 1, st[0]: 1, st[1]: 1}) as i:
                for h in range(2):
                    dve.wait_ge(xld[h].sem, xld[h].up())
                    V.tensor_copy(din[:, h, :].rearrange("p (c w) -> p c w", w=XW)[:, :, D + 3],
                                  deg[:, bass.ds((2 * i + h) * R, R)]).then_inc(S["col_ready"], 1)
                    st[h].n += 16
                dve.wait_ge(kept.sem, kept.up())
                cols = bass.ds(i * H, H)
                one(V.tensor_tensor(M[:, cols, :], M[:, cols, :], XS[:, cols, :], ALU.add))
                dve.sem_inc(S["xs_free"], 1)
                one(V.tensor_scalar(M[:, cols, :], M[:, cols, :], 0.0, None, ALU.max))
                scans(i, lambda f: M[:, cols, f])
            one(V.tensor_scalar(deg[:, :], deg[:, :], 1.0, None, ALU.max))
            ask_act()
            one(V.reciprocal(deg[:, :], deg[:, :]))

            def counts(of):
                one(V.tensor_tensor_scan(cnt[:, :], cont[:, :], of, 0.0, ALU.mult, ALU.add))

            def carries(with_counts):
                V.memset(shT[:, 0:1], 0.0).then_inc(own.sem, own.add())
                V.tensor_copy(tail[:, 0:D], M[:, CE - 1, :]).then_inc(own.sem, own.add())
                one(V.tensor_copy(tail[:, D:D + 1], cnt[:, CE - 1:CE]))
                ask_pe()
                one(V.tensor_copy(tailT[:, :], psG[0:D + 1, 0:P]))
                one(V.tensor_tensor_scan(shT[:, 1:P + 1], fullT[:, :], tailT[:, :], 0.0, ALU.mult, ALU.add))
                ask_pe()
                one(V.tensor_copy(carry[:, :], psG[:, P:P + D + 1]))
                if with_counts:
                    one(V.scalar_tensor_tensor(cnt[:, :], pre[:, :], carry[:, D:D + 1], cnt[:, :], ALU.mult, ALU.add))

            def carried(cols, mask=pre, n=R):
                one(V.tensor_tensor(su[:, :, :], along(mask[:, cols]), down(carry[:, 0:D]), ALU.mult))
                one(V.tensor_tensor(M[:, cols, :], M[:, cols, :], su[:, :, :], ALU.add))

            def norm(units, factor=None, free=False, stores=False, keep=None):
                for h, x, u, out in units:
                    V.tensor_reduce(mu[:, h, :], x, X, ALU.add).then_inc(own.sem, own.add())
                dve.wait_ge(own.sem, own.now())
                for h, x, u, out in units:
                    V.scalar_tensor_tensor(u, along(mu[:, h, :]), -1.0 / D, x, ALU.mult, ALU.add
                                           ).then_inc(S["centered"], 1)
                for h, x, u, out in units:
                    dve.wait_ge(squared.sem, squared.up())
                    if free:
                        dve.sem_inc(S["in_free"], 1)
                    V.tensor_reduce(var[:, h, :], sq[:, h, :, :], X, ALU.add).then_inc(S["var_ready"], 1)
                for h, x, u, out in units:
                    dve.wait_ge(std_ready.sem, std_ready.up())
                    V.reciprocal(srs[:, h, :], std[:, h, :]).then_inc(own.sem, own.add())
                    if keep:
                        V.tensor_copy(keep(h), var[:, h, :]).then_inc(own.sem, own.add())
                dve.wait_ge(own.sem, own.now())
                for h, x, u, out in units:
                    if stores:
                        dve.wait_ge(st[h].sem, st[h].now())
                    if factor is None:
                        V.tensor_tensor(out, u, along(srs[:, h, :]), ALU.mult).then_inc(own.sem, own.add())
                    else:
                        V.scalar_tensor_tensor(out, u, factor, along(srs[:, h, :]), ALU.mult, ALU.mult
                                               ).then_inc(own.sem, own.add())
                dve.wait_ge(own.sem, own.now())

            NORM1, NORM2 = 3, 6
            DU = [du[:, h, :, :] for h in range(2)]
            DO = [do[:, h, :, :] for h in range(2)]
            pair = [(h, DU[h], DU[h], DO[h]) for h in range(2)]

            def wide(h, w):
                return din[:, h, 0:R * w].rearrange("p (c w) -> p c w", w=w)[:, :, 0:D]

            one(V.memset(t0[:, :], 1.0))
            counts(t0[:, :])
            carries(True)
            one(V.scalar_tensor_tensor(c2s[:, :], c2e[:, :], 1.0 / D, c2e[:, :], ALU.mult, ALU.mult))
            per = {own: 2 * NORM2 + 6 + NORM1, ld[0]: 2, ld[1]: 2, st[0]: 4, st[1]: 4, kept: 2,
                   squared: PER + 1, std_ready: PER + 1, act_done: 1}
            with loop(dve, NBLK, per) as i:
                for q in range(PER // 2):
                    for h in range(2):
                        dve.wait_ge(ld[h].sem, ld[h].up())
                    norm([(h, wide(h, XW), DU[h], DO[h]) for h in range(2)], factor=c2e[:, 0:1], free=True, stores=True)
                    for h in range(2):
                        V.tensor_tensor(dy[:, h, :, :], DO[h], along(deg[:, bass.ds((PER * i + 2 * q + h) * R, R)]), ALU.mult
                                        ).then_inc(S["out_ready"], 1)
                        st[h].n += 32
                dve.wait_ge(kept.sem, kept.up(2))
                cols = bass.ds(i * R, R)
                V.tensor_scalar(cib[:, :], dg[:, cols], 1.0, None, ALU.max).then_inc(own.sem, own.add())
                carried(cols)
                ask_act()
                V.reciprocal(cib[:, :], cib[:, :]).then_inc(own.sem, own.add())
                one(V.scalar_tensor_tensor(su[:, :, :], XS[:, cols, :], c2e[:, 0:1], M[:, cols, :], ALU.mult, ALU.add))
                norm([(0, su[:, :, :], su[:, :, :], XS[:, cols, :])])
                one(V.tensor_tensor(M[:, cols, :], XS[:, cols, :], along(cib[:, :]), ALU.mult))
                dve.sem_inc(S["rows_new"], 1)

            def taken(h, x):
                for g in range(4):
                    n = 4 if g == 3 else 8
                    dve.wait_ge(mm.sem, mm.up())
                    V.scalar_tensor_tensor(DU[h][:, 8 * g:8 * g + n, :],
                                           psO[g][:, 0:n * D].rearrange("p (c d) -> p c d", d=D), 0.0,
                                           x(g, n), ALU.max, ALU.add).then_inc(mm_used.sem, mm_used.add())

            with loop(dve, NBLK, {own: 2 * NORM2, mm: 16, mm_used: 16, ld[0]: 2, ld[1]: 2, st[0]: 2, st[1]: 2,
                                  squared: PER, std_ready: PER}) as i:
                for q in range(PER // 2):
                    for h in range(2):
                        dve.wait_ge(ld[h].sem, ld[h].up())
                        taken(h, lambda g, n: wide(h, D)[:, 8 * g:8 * g + n, :])
                    dve.wait_ge(mm_used.sem, mm_used.now())
                    dve.sem_inc(S["in_free"], 2)
                    norm(pair, stores=True)
                    for h in range(2):
                        st[h].n += 16
                    dve.sem_inc(S["out_ready"], 2)

            for h in range(2):
                dve.wait_ge(st[h].sem, st[h].now())
            V.tensor_copy(zbs, zs[:, :]).then_inc(own.sem, own.add())
            V.tensor_copy(zbd, zd[:, :]).then_inc(own.sem, own.add())
            V.memset(h1T, 1.0).then_inc(own.sem, own.add())
            one(V.tensor_scalar(t0[:, :], ew[:, :], 6.0, 0.5, ALU.is_lt, ALU.mult))
            one(V.tensor_scalar(t1[:, :], ew[:, :], 0.0, 6.0, ALU.max, ALU.min))
            one(V.tensor_scalar(t1[:, :], t1[:, :], -3.14159265358979 / 6, 3.14159265358979 / 2, ALU.mult, ALU.add))
            ask_act()
            one(V.scalar_tensor_tensor(t1[:, :], t1[:, :], 1.0, t0[:, :], ALU.add, ALU.mult))
            one(V.tensor_tensor(t1[:, :], t1[:, :], nv[:, :], ALU.mult))
            dve.sem_inc(S["mlp_free"], 1)
            dve.sem_inc(S["mlp_used"], 2)
            for h in range(2):
                fill[h].n = 2 * CE // 2 * 16
            ma, mg = views("mlp_a", "mlp_g")
            steps = [(h, f) for h in range(2) for f in range(D)]
            with loop(dve, NBLK, {own: 2 * D + 2 + 4 * R // 4, ma: 4 * R // 4, mg: R // 4, fill[0]: H, fill[1]: H}) as i:
                cols = bass.ds(i * R, R)
                V.tensor_tensor(ohs, down(iotaz[:, :]), along(zbs[:, cols], Z), ALU.is_equal).then_inc(own.sem, own.add())
                one(V.tensor_tensor(ohd, down(iotaz[:, :]), along(zbd[:, cols], Z), ALU.is_equal))
                dve.sem_inc(S["hots"], 1)
                for g in range(R // 4):
                    for h, f in steps[14 * g:14 * g + 14]:
                        half = bass.ds((2 * i + h) * H, H)
                        if f == 0:
                            dve.wait_ge(own.sem, own.now())
                            dve.wait_ge(fill[h].sem, fill[h].up(H))
                        V.tensor_tensor_scan(M[:, half, f], cont[:, half], ring[:, h, :, f],
                                             MG[:, bass.ds((2 * i + h) * H, 1), f], ALU.mult, ALU.add
                                             ).then_inc(own.sem, own.add())
                        if f == D - 1:
                            dve.wait_ge(own.sem, own.now())
                            dve.sem_inc(S["ring_free"], 1)
                    c4 = bass.ds(i * R + 4 * g, 4)
                    dve.wait_ge(ma.sem, ma.up(3 if g == 0 else 4))
                    one(V.tensor_tensor(prod, (psB, psC)[g % 2][:, 0:4 * G].rearrange("p (c g) -> p c g", g=G),
                                        ejs[g % 2], ALU.mult))
                    one(V.tensor_reduce(lg[:, :], prod, X, ALU.add))
                    dve.wait_ge(mg.sem, mg.up())
                    one(V.tensor_tensor(gsum, (psG, psT[1])[g % 2][:, 0:4 * D].rearrange(
                        "p (c d) -> p c d", d=D), along(lg[:, :]), ALU.add))
                    dve.sem_inc(S["mlp_used"], 1)
                    one(V.tensor_tensor(GX[:, c4, 0:D], gsum, along(t1[:, c4]), ALU.mult))
                ma.n += 1
                dve.sem_inc(S["mlp_free"], 1)
            V.tensor_copy(GX[:, :, D], nv[:, :]).then_inc(own.sem, own.add())
            one(V.tensor_copy(GX[:, :, D + 1].bitcast(I32), dstI[:, :]))
            dve.sem_inc(S["rec_ready"], 1)

            carries(False)
            one(V.tensor_scalar(t0[:, :], cnt[:, :], 1.0, None, ALU.max))
            ask_act()
            one(V.reciprocal(t0[:, :], t0[:, :]))
            one(V.tensor_scalar(t1[:, :], dg[:, :], 1.0, None, ALU.max))
            ask_act()
            one(V.reciprocal(t1[:, :], t1[:, :]))
            one(V.tensor_scalar(dg[:, :], dg[:, :], 1.0, None, ALU.min))
            one(V.tensor_tensor(t1[:, :], t1[:, :], dg[:, :], ALU.mult))

            def update_by_product():
                with loop(dve, NBLK, {own: 2 + 1 + NORM1, mm: 4, mm_used: 4, squared: 1, std_ready: 1}) as i:
                    cols = bass.ds(i * R, R)
                    carried(cols)
                    one(V.tensor_tensor(su[:, :, :], M[:, cols, :], along(t0[:, cols]), ALU.mult))
                    dve.sem_inc(S["h_ready"], 1)
                    taken(0, lambda g, n: XS[:, bass.ds(i * R + 8 * g, n), :])
                    dve.wait_ge(mm_used.sem, mm_used.now())
                    norm([(0, DU[0], DU[0], XS[:, cols, :])])
                    dve.sem_inc(S["rows_new"], 1)
            update_by_product()

            one(V.tensor_tensor(M, XS[:, :, :], along(end[:, :]), ALU.mult))
            one(V.tensor_scalar(t0[:, :], end[:, :], -1.0, 1.0, ALU.mult, ALU.add))
            for f in range(D):
                V.tensor_tensor_scan(M[:, ::-1, f], t0[:, ::-1], M[:, ::-1, f], 0.0, ALU.mult, ALU.add).then_inc(own.sem, own.add())
            dve.wait_ge(own.sem, own.now())
            V.memset(shT[:, P:P + 1], 0.0).then_inc(own.sem, own.add())
            one(V.tensor_copy(tail[:, 0:D], M[:, 0, :]))
            ask_pe()
            one(V.tensor_copy(tailT[:, :], psG[0:D + 1, 0:P]))
            one(V.tensor_tensor_scan(shT[:, 0:P][:, ::-1], restT[:, ::-1], tailT[:, ::-1], 0.0, ALU.mult, ALU.add))
            ask_pe()
            one(V.tensor_copy(carry[:, :], psG[:, P:P + D + 1]))
            with loop(dve, NBLK, {own: 3}) as i:
                cols = bass.ds(i * R, R)
                carried(cols, suf)
                one(V.tensor_tensor(M[:, cols, :], M[:, cols, :], along(t1[:, cols]), ALU.mult))
            dve.sem_inc(S["rec_ready"], 1)

            one(V.tensor_copy(va[0:SORT_P, :], vb[0:SORT_P, :].bitcast(I32)))
            one(V.memset(vb[96:P, :], 3.4028234e38))
            one(V.tensor_scalar(vb[0:SORT_P, :], va[0:SORT_P, :], float(HALF_NODES), float(65536 - HALF_NODES),
                                ALU.is_ge, ALU.mult))
            one(V.scalar_tensor_tensor(va[0:SORT_P, :], va[0:SORT_P, :], 256.0, vb[0:SORT_P, :], ALU.add, ALU.add))
            vi = vb[0:SORT_P, :].bitcast(I32)
            one(V.tensor_copy(vi, va[0:SORT_P, :]))
            one(V.tensor_scalar(vi, vi, 15, None, ALU.logical_shift_left))
            one(V.tensor_tensor(vi, vi, pos[0:SORT_P, :], ALU.bitwise_or))
            now = [vb, va]

            def compare(d):
                lo, hi = (now[0][:, :].rearrange("p (b two d) -> p b two d", two=2, d=d)[:, :, j, :] for j in range(2))
                a, b = (now[1][:, :].rearrange("p (b two d) -> p b two d", two=2, d=d)[:, :, j, :] for j in range(2))
                V.tensor_tensor(a, lo, hi, ALU.min).then_inc(own.sem, own.add())
                one(V.tensor_tensor(b, lo, hi, ALU.max))
                now.reverse()

            def turned():
                dve.sem_inc(S["ask_pe"], 1)
                dve.wait_ge(pe_done.sem, pe_done.up())
                one(V.tensor_copy(now[1][:, :], psT[0][:, 0:SORT_C]))
                now.reverse()

            def negate(m):
                v = now[0][:, :].rearrange("p (b two d) -> p b two d", two=2, d=1 << m)[:, :, 1, :]
                one(V.tensor_scalar(v, v, -1.0, None, ALU.mult))

            for m in range(1, 16):
                if m >= 9:
                    one(V.tensor_scalar(now[0][:, :], now[0][:, :], psgn[:, m - 8:m - 7], None, ALU.mult))
                elif m == 8:
                    negate(7)
                    one(V.tensor_scalar(now[0][:, :], now[0][:, :], psgn[:, 0:1], None, ALU.mult))
                else:
                    if m > 1:
                        negate(m - 1)
                    negate(m)
                if m > 8:
                    turned()
                    for b in range(m - 9, -1, -1):
                        compare(1 << b)
                    turned()
                for b in range(min(m, 8) - 1, -1, -1):
                    compare(1 << b)
            assert now[0] is vb
            dve.sem_inc(S["srt_ready"], 1)

            dve.wait_ge(S["srt_ld"], 16 * 3)
            dve.wait_ge(S["s_done"], 2)
            one(V.tensor_scalar(dstI[:, :], t0[:, :].bitcast(I32), 0x7FFF, None, ALU.bitwise_and))
            for t in (t0, keyn, cont):
                V.tensor_scalar(t[:, :].bitcast(I32), t[:, :].bitcast(I32), 15, None, ALU.logical_shift_right).then_inc(own.sem, own.add())
            dve.wait_ge(own.sem, own.now())
            V.tensor_copy(key[:, :], t0[:, :].bitcast(I32)).then_inc(own.sem, own.add())
            V.tensor_copy(dg[:, :], keyn[:, :].bitcast(I32)).then_inc(own.sem, own.add())
            one(V.tensor_copy(cnt[:, :], cont[:, :].bitcast(I32)))
            order(key[:, :], dg[:, :], cnt[:, :])
            one(V.tensor_scalar(t0[:, :], key[:, :], 65536.0, -float(65536 - HALF_NODES), ALU.is_ge, ALU.mult))
            one(V.scalar_tensor_tensor(key[:, :], key[:, :], -256.0, t0[:, :], ALU.add, ALU.add))
            one(V.tensor_copy(srcI[:, :], key[:, :]))
            writers(key[:, :])
            one(V.memset(t0[:, :], 1.0))
            counts(t0[:, :])

            with loop(dve, NBLK, {own: 2 * (4 + NORM2), ld[0]: 2, ld[1]: 2, st[0]: 4, st[1]: 4,
                                  squared: PER, std_ready: PER}) as i:
                for q in range(PER // 2):
                    for h in range(2):
                        dve.wait_ge(ld[h].sem, ld[h].up())
                        V.tensor_tensor(DU[h], wide(h, D), down(rows[:, 0, :]), ALU.add).then_inc(own.sem, own.add())
                    dve.wait_ge(own.sem, own.now())
                    dve.sem_inc(S["in_free"], 2)
                    norm(pair, stores=True, keep=lambda h: deg[:, bass.ds((PER * i + 2 * q + h) * R, R)])
                    for h in range(2):
                        st[h].n += 32
                    dve.sem_inc(S["out_ready"], 2)

            mid = DU[0].rearrange("p c d -> p (c d)")[:, 0:CN]
            one(V.tensor_scalar(mid, deg[:, :], D * EPS, None, ALU.add))
            one(V.reciprocal(mid, mid))
            one(V.tensor_tensor(deg[:, :], deg[:, :], mid, ALU.mult))
            one(V.tensor_scalar(deg[:, :], deg[:, :], EPS, None, ALU.add))
            ask_act()
            one(V.reciprocal(deg[:, :], deg[:, :]))

            def short3(i):
                for h in range(2):
                    dve.wait_ge(ld[h].sem, ld[h].up())
                    V.tensor_tensor(DU[h], along(deg[:, bass.ds((2 * i + h) * R, R)]), down(rows[:, 1, :]), ALU.mult
                                    ).then_inc(own.sem, own.add())
                dve.wait_ge(own.sem, own.now())
                for h in range(2):
                    V.scalar_tensor_tensor(DU[h], DU[h], 1.0, wide(h, D), ALU.add, ALU.mult).then_inc(own.sem, own.add())
                dve.wait_ge(own.sem, own.now())
                dve.sem_inc(S["in_free"], 2)
                for h in range(2):
                    V.tensor_tensor(DU[h], DU[h], down(rows[:, 2, :]), ALU.add).then_inc(own.sem, own.add())
                dve.wait_ge(own.sem, own.now())
                norm(pair, stores=True)
                for h in range(2):
                    st[h].n += 16
                dve.sem_inc(S["out_ready"], 2)

            for h in range(2):
                fill[h].n = 4 * CE // 2 * 16
            short = {ld[0]: 1, ld[1]: 1, st[0]: 1, st[1]: 1, squared: 2, std_ready: 2}
            with loop(dve, NBLK, {own: 2 * D + NORM2 + 6, fill[0]: H, fill[1]: H, **short}) as i:
                for h in range(2):
                    dve.wait_ge(fill[h].sem, fill[h].up(H))
                    scans(2 * i + h, lambda f: ring[:, h, :, f])
                    dve.sem_inc(S["scanned"], 1)
                short3(i)

            dve.wait_ge(kept.sem, kept.up(2 * CE // H))
            carries(True)
            one(V.tensor_copy(t0[:, :], cnt[:, :]))
            ask_act()
            one(V.reciprocal(t0[:, :], t0[:, :]))
            update_by_product()

            for h in range(2):
                assert fill[h].n == 5 * CE // 2 * 16
            with loop(dve, NBLK, {own: 2 + 2 * D + NORM2 + 6, fill[0]: H, fill[1]: H, **short}) as i:
                for h in range(2):
                    dve.wait_ge(fill[h].sem, fill[h].up(H))
                    cols = bass.ds((2 * i + h) * H, H)
                    one(V.tensor_tensor(M[:, cols, :], ring[:, h, :, 0:D], GX[:, cols, 0:D], ALU.mult))
                    dve.sem_inc(S["ring_free"], 1)
                    scans(2 * i + h, lambda f: M[:, cols, f])
                short3(i + NBLK)
            one(V.tensor_copy(nv[:, :], GX[:, :, D]))
            counts(nv[:, :])
            carries(True)
            one(V.tensor_scalar(t0[:, :], cnt[:, :], 1e-8, None, ALU.max))
            one(V.reciprocal(t0[:, :], t0[:, :]))

            with loop(dve, NBLK, {own: 2 + 2 + 3 + 2 * NORM1, squared: 2, std_ready: 2}) as i:
                cols = bass.ds(i * R, R)
                carried(cols)
                one(V.tensor_tensor(su[:, :, :], M[:, cols, :], along(t0[:, cols]), ALU.mult))
                one(V.tensor_tensor(su[:, :, :], su[:, :, :], XS[:, cols, :], ALU.add))
                norm([(0, su[:, :, :], su[:, :, :], su[:, :, :])])
                one(V.tensor_tensor(su[:, :, :], su[:, :, :], down(rows[:, 1, :]), ALU.mult))
                one(V.tensor_tensor(su[:, :, :], su[:, :, :], down(rows[:, 2, :]), ALU.add))
                one(V.tensor_tensor(su[:, :, :], su[:, :, :], XS[:, cols, :], ALU.add))
                norm([(0, su[:, :, :], su[:, :, :], XS[:, cols, :])])
                dve.sem_inc(S["rows_new"], 1)


def kernel(**inputs):
    import ml_dtypes
    import numpy as np
    from concourse import bacc
    from concourse.bass_utils import run_bass_kernel_spmd

    f = {k: np.asarray(v) for k, v in inputs.items()}
    f32 = np.float32

    def padded(a, rows, width):
        out = np.zeros((rows, width), a.dtype)
        out[:a.shape[0], :a.shape[1]] = a
        return out

    def edges(a):
        return np.concatenate([[-1], a, np.full(EP - E, NP - 1), [-1]]).astype(np.int32)

    def twice(w, b):
        out = np.zeros((97, 96), f32)
        out[0:D, 0:D] = w.T
        out[D:96, D:96] = w.T
        out[96, 0:D] = b
        out[96, D:96] = b
        return out

    xaux = np.zeros((NP, XW), f32)
    xaux[:N, 0:D] = f["x"]
    xaux[:N, D] = f["node_vec"]
    xaux[:N, D + 1] = f["node_type_119"].astype(np.int32).view(f32)
    place = np.arange(P)
    psgn = np.ones((P, 8), f32)
    psgn[:, 0] = 1 - 2 * (place & 1)
    for m in range(9, 16):
        now = (place >> (m - 8)) & 1 if m < 15 else 0
        psgn[:, m - 8] = (1 - 2 * now) * (1 - 2 * ((place >> (m - 9)) & 1))
    arrays = {
        "xaux": xaux,
        "src": edges(f["src"]), "dst": edges(f["dst"]),
        "ea48": padded(f["edge_attr_48"], EP, D), "ea40": padded(f["edge_attr_40"], EP, A_DIM),
        "ew": padded(f["edge_weight"][:, None], EP, 1)[:, 0],
        "iota": np.tile(np.arange(CN, dtype=np.int16), (P, 1)),
        "iotaz": np.tile(np.arange(Z), (P, 1)).astype(ml_dtypes.bfloat16),
        "ident": np.eye(P, dtype=f32), "identb": np.eye(P).astype(ml_dtypes.bfloat16),
        "w1b": twice(f["L1_gnn_W"], f["L1_gnn_b"]), "w2b": twice(f["L2_gnn_W"], f["L2_gnn_b"]),
        "wm1": np.ascontiguousarray(f["L3_gnn_W1"].T), "bm1": f["L3_gnn_b1"][:, None],
        "wm2": np.concatenate([f["L3_gnn_W2"].T, f["L3_gnn_b2"][None]]),
        "emb": padded(f["L3_gnn_emb"], Z, G), "embT": np.ascontiguousarray(padded(f["L3_gnn_emb"], Z, G).T),
        "adT": np.ascontiguousarray(f["L3_gnn_adaptW"].T),
        "psgn": psgn, "pos": np.arange(P * SORT_C, dtype=np.int32).reshape(P, SORT_C),
        "b2": f["L2_gnn_b"][None], "gamma": f["L3_gnn_gamma"][None], "beta": f["L3_gnn_beta"][None],
        "eps": f["L0_gnn_eps"][None],
    }
    nc = bacc.Bacc("TRN2", target_bir_lowering=False, num_devices=1)
    aps = {k: nc.dram_tensor(f"in_{k}", a.shape, mybir.dt.from_np(a.dtype), kind="ExternalInput").ap()
           for k, a in arrays.items()}
    out = nc.dram_tensor("out", [NP, D], F32, kind="ExternalOutput").ap()
    bass_gnn(nc, aps, out)
    r = run_bass_kernel_spmd(nc, [{f"in_{k}": a for k, a in arrays.items()}], core_ids=[0])
    return r.results[0]["out"][:N]
```

```python
from contextlib import ExitStack, contextmanager

import concourse.bass as bass
from concourse import mybir

P = 128
D = 48
N = 100000
CN = 784
NP = P * CN
E = 25000
CE = 196
EP = P * CE
R = 28
H = 14
NBLK = CE // R
DBLK = CN // R
PER = DBLK // NBLK
XW = 52
RW = 98
A_DIM = 40
EW = 91
Z = 120
G = 32
EPS = 1e-5
SORT_C = 256
SORT_P = EP // SORT_C
SKIP = float(1 << 20)
HALF_NODES = NP // 2
F32 = mybir.dt.float32
I32 = mybir.dt.int32
I16 = mybir.dt.int16
BF16 = mybir.dt.bfloat16


class Count:

    def __init__(self, sem, step=1):
        self.sem, self.step, self.n, self.turn = sem, step, 0, 0

    def add(self):
        self.n += self.step
        return self.step

    def up(self, times=1):
        self.n += self.step * times
        return self.now()

    def now(self):
        return self.turn + self.n


def sort_turns():
    now, turns = 0, []
    for m in range(1, 16):
        if m > 8:
            turns.append(now)
            now = (now + 1 + m - 8) % 2
            turns.append(now)
            now = (now + 1) % 2
        now = (now + min(m, 8)) % 2
    return turns, now


@contextmanager
def loop(eng, times, per):
    with eng.Fori(0, times) as i:
        before = {c: c.n for c in per}
        for c, k in per.items():
            c.turn = i * (k * c.step)
        yield i
        for c, k in per.items():
            assert c.n - before[c] == k * c.step, (c.sem, c.n - before[c], k * c.step)
            c.turn = 0
    for c, k in per.items():
        c.n = before[c] + times * k * c.step


def bass_gnn(nc, A, OUT):
    ALU, ACT, X = mybir.AluOpType, mybir.ActivationFunctionType, mybir.AxisListType.X
    ctx = ExitStack()
    with ctx:
        def sb(name, shape, dt=F32):
            return ctx.enter_context(nc.sbuf_tensor(name, shape, dt))

        def ps(name):
            return ctx.enter_context(nc.psum_tensor(name, [P, 512], F32))

        def sem(name):
            return ctx.enter_context(nc.semaphore(name))

        def dram(name, shape, dt=F32):
            return nc.dram_tensor(name, shape, dt, kind="Internal").ap()

        XA = dram("xa_table", [NP, XW])
        X1 = dram("x1_table", [NP, D])
        Y1 = dram("y1_table", [NP, D])
        X2 = dram("x2_table", [NP, D])
        X3 = dram("x3_table", [NP, D])
        X3C = dram("x3_copy", [NP, D])
        REC = dram("edge_records", [EP, RW])
        SRC_D = dram("src_by_dst", [EP + 2], I32)
        DST_D = dram("dst_by_dst", [EP + 2], I32)
        EW_D = dram("ew_by_dst", [EP])
        EA48_D = dram("ea48_by_dst", [EP, D])
        EA40_D = dram("ea40_by_dst", [A_DIM, CE, P])
        SRT = dram("sorted_src", [P * SORT_C + 2], I32)

        def blk(table, k, w=D):
            return table.rearrange("(p c) d -> p c d", p=P)[:, bass.ds(k * R, R), 0:w]

        MG = sb("MG", [P, 1 + CE, D])
        M = MG[:, 1:1 + CE, :]
        XS = sb("XS", [P, CE, D])
        GX = sb("GX", [P, CE, D + 2])
        ring = sb("ring", [P, 2, H, RW])
        idx = sb("idx", [P, 2, H], I32)
        sumb = sb("sumb", [P, 2, D * (H + 1)])
        din = sb("din", [P, 2, R * XW])
        du = sb("du", [P, 2, R, D])
        sq = sb("sq", [P, 2, R, D])
        do = sb("do", [P, 2, R, D])
        sub = sb("sub", [P, 2, D * (H + 1)])
        mask = sb("mask", [P, D, H + 1], BF16)
        hT = sb("hT", [97, 2, 512])
        mu = sb("mu", [P, 2, R])
        var = sb("var", [P, 2, R])
        std = sb("std", [P, 2, R])
        c2s = sb("c2s", [P, 1])
        srs = sb("srs", [P, 2, R])
        deg = sb("deg", [P, CN])
        srcI = sb("srcI", [P, CE], I32)
        dstI = sb("dstI", [P, CE], I32)
        dstS = sb("dstS", [P, CE], I32)
        key = sb("key", [P, CE])
        keyn = sb("keyn", [P, CE])
        cont = sb("cont", [P, CE])
        pre = sb("pre", [P, CE])
        suf = sb("suf", [P, CE])
        end = sb("end", [P, CE])
        cnt = sb("cnt", [P, CE])
        put = sb("put", [P, CE], I32)
        zs = sb("zs", [P, CE])
        zd = sb("zd", [P, CE])
        nv = sb("nv", [P, CE])
        dg = sb("dg", [P, CE])
        t0 = sb("t0", [P, CE])
        t1 = sb("t1", [P, CE])
        tail = sb("tail", [P, D + 1])
        carry = sb("carry", [P, D + 1])
        ident = sb("ident", [P, P])
        identb = sb("identb", [P, P], BF16)
        fullT = sb("fullT", [D + 1, P])
        tailT = sb("tailT", [D + 1, P])
        shT = sb("shT", [D + 1, P + 1])
        w1b = sb("w1b", [97, 96])
        w2b = sb("w2b", [97, 96])
        wm1 = sb("wm1", [A_DIM, D])
        bm1 = sb("bm1", [D, 1])
        wm2 = sb("wm2", [D + 1, D])
        logit = sb("logit", [Z, 3, Z], BF16)
        rows = sb("rows", [P, 3, D])
        c2e = sb("c2e", [P, 1])
        lneps = sb("lneps", [P, 1])
        psgn = sb("psgn", [P, 8])
        va = sb("va", [P, SORT_C])
        vb = sb("vb", [P, SORT_C])
        zero1 = sb("zero1", [P, 1])
        flag = sb("flag", [1, 2], I32)
        stage = sumb[:, :, 0:H * D].rearrange("p h (c d) -> p h c d", d=D)
        sums = sumb[:, :, :].rearrange("p h (d c) -> p h d c", d=D)
        su = sub[:, :, :].rearrange("p h w -> p (h w)")[:, 0:R * D].rearrange("p (c d) -> p c d", d=D)
        terms = sub[:, :, :].rearrange("p h (d c) -> p h d c", d=D)
        gflat = GX[:, :, :].rearrange("p c w -> p (c w)")
        iota = gflat[:, 0:CN // 2].bitcast(I16)
        ohc = gflat[:, 400:400 + 2 * CN].bitcast(BF16).rearrange("p (h c) -> p h c", h=4)
        ohp = gflat[:, 2000:2000 + 2 * P].bitcast(BF16).rearrange("p (h c) -> p h c", h=4)
        colf = gflat[:, 2300:2300 + CE]
        parf = gflat[:, 2500:2500 + CE]
        tmpf = gflat[:, 2700:2700 + CE]
        embT = gflat[0:G, 6000:6000 + Z]
        adT = gflat[0:G, 6200:6200 + G]
        dy = gflat[:, 3000:3000 + 2 * R * D].rearrange("p (h c d) -> p h c d", h=2, d=D)
        OH = (0, 1, 0, 1, 0, 1, 2)
        ohs, ohd = (t[:, :, :, :].rearrange("p h c d -> p (h c d)")[:, 0:3 * 2 * Z].bitcast(BF16).rearrange(
            "p (k c z) -> p k c z", k=3, z=Z) for t in (du, sq))
        zbs = du[:, :, :, :].rearrange("p h c d -> p (h c d)")[:, 1700:1700 + CE // 2].bitcast(BF16)
        zbd = du[:, :, :, :].rearrange("p h c d -> p (h c d)")[:, 1800:1800 + CE // 2].bitcast(BF16)
        pos = gflat[:, 7000:7000 + SORT_C].bitcast(I32)
        aez = gflat[0:G, 6800:6800 + Z]
        pair_f = gflat[0:Z, 6400:6400 + Z]
        part_f = gflat[0:Z, 6600:6600 + Z]
        dflat = din[:, :, :].rearrange("p h w -> p (h w)")
        eaG = dflat[0:A_DIM, 0:H * P]
        eaT = [dflat[0:A_DIM, k * 512:(k + 1) * 512] for k in (0, 1, 2, 3, 0, 1, 2)]
        doflat = do[:, :, :, :].rearrange("p h c d -> p (h c d)")
        h1T = doflat[0:D + 1, 512:1024]
        zT = doflat[0:Z, 0:256].bitcast(BF16)
        prod = sq[:, :, :, :].rearrange("p h c d -> p (h c d)")[:, 1700:1700 + 4 * Z].rearrange("p (c z) -> p c z", z=Z)
        gsum = doflat[:, 2400:2400 + 4 * D].rearrange("p (c d) -> p c d", d=D)
        lg = sb("lg", [P, 4])
        iotaz = sb("iotaz", [P, Z], BF16)
        restT = sb("restT", [D + 1, P])
        ew = t1[:, :]
        psT = [ps("psT0"), ps("psT1")]
        psA, psB, psC, psG = ps("psA"), ps("psB"), ps("psC"), ps("psG")
        psO = [ps("psO0"), ps("psO1"), psA, psB, psC, psG]

        S = {n: sem(n) for n in (
            "dve", "act", "pool",
            "look", "flag", "g_ld", "g_ask", "g_turned", "g_dve", "g_pool", "g_sorted", "g_places", "g_fill",
            "g_rows", "g_trans", "g_copied", "g_ea", "g_st", "g_free",
            "consts", "edges", "ea48", "init", "spread", "returned", "pool_turns", "pe_turns",
            "hot", "counted", "deg_done", "col_ready", "xa_ld0", "xa_ld1", "xa_done",
            "ld0", "ld1", "in_free", "out_ready", "st0", "st1", "short_done",
            "centered", "squared", "var_ready", "std_ready",
            "fill0", "fill1", "ring_free", "kept", "scanned", "xs_free", "sc0", "sc1", "stage_free",
            "rows_ready", "rows_new", "idx_ready", "s_done",
            "h_ready", "trans", "hT_ready", "mm", "mm_used", "ask_act", "act_done", "ask_pe", "pe_done",
            "mlp_ld0", "mlp_ld1", "mlp_ld2", "mlp_ld3", "mlp_free", "hots", "mlp_t", "mlp_a", "mlp_o", "mlp_g",
            "mlp_used",
            "rec_ready", "rec_st", "srt_ready", "srt_st", "srt_ld")}
        FROM_DMA = ("look", "g_ld", "g_fill", "g_st", "consts", "edges", "ea48", "xa_ld0", "xa_ld1", "ld0", "ld1",
                    "st0", "st1", "fill0", "fill1", "sc0", "sc1", "mlp_ld0", "mlp_ld1", "mlp_ld2", "mlp_ld3", "rec_st",
                    "srt_st", "srt_ld")

        def views(*names):
            return [Count(S[n], 16 if n in FROM_DMA else 1) for n in names]

        block = ctx.enter_context(nc.Block())

        @block.sync
        def _(sp):
            consts, edges, ea48, look = views("consts", "edges", "ea48", "look")
            for to, of in ((dstI[:, :], A["dst"][1:EP + 1]), (t0[:, :].bitcast(I32), A["dst"][2:EP + 2])):
                sp.dma_start(to, of.rearrange("(p c) -> p c", p=P)).then_inc(look.sem, look.add())
            for to, name in ((ident[:], "ident"), (iota, "iota"), (iotaz[:], "iotaz"), (identb[:], "identb"),
                             (w1b[:], "w1b"), (w2b[:], "w2b"), (wm1[:], "wm1"), (bm1[:], "bm1"), (wm2[:], "wm2"),
                             (embT, "embT"), (adT, "adT"), (psgn[:], "psgn"), (pos, "pos")):
                sp.dma_start(to, A[name]).then_inc(consts.sem, consts.add())
            for j, name in enumerate(("b2", "gamma", "beta")):
                sp.dma_start(rows[:, j, :], A[name].broadcast_to([P, D])).then_inc(consts.sem, consts.add())
            sp.dma_start(c2e[:, :], A["eps"].broadcast_to([P, 1])).then_inc(consts.sem, consts.add())

            def sort_edges():
                g_ld, g_sorted, g_rows, g_ea, g_st = views("g_ld", "g_sorted", "g_rows", "g_ea", "g_st")
                sp.dma_start(vb[0:SORT_P, :].bitcast(I32), A["dst"][1:EP + 1].rearrange("(p c) -> p c", p=SORT_P)
                             ).then_inc(g_ld.sem, g_ld.add())
                sp.wait_ge(g_sorted.sem, g_sorted.up())
                sp.dma_start(SRT[1:P * SORT_C + 1].rearrange("(p c) -> p c", p=P), vb[:, :].bitcast(I32)
                             ).then_inc(g_ld.sem, g_ld.add())
                sp.wait_ge(g_ld.sem, g_ld.now())
                sp.dma_start(srcI[:, :], SRT[1:EP + 1].rearrange("(p c) -> p c", p=P)).then_inc(g_ld.sem, g_ld.add())
                with loop(sp, CE // H, {g_rows: 1, g_ea: 1, g_st: 5}) as c:
                    cols = bass.ds(c * H, H)
                    sp.wait_ge(g_rows.sem, g_rows.up())
                    for of, table in ((A_DIM + D, SRC_D[1:EP + 1]), (A_DIM + D + 1, DST_D[1:EP + 1])):
                        sp.dma_start(table.rearrange("(p c) -> p c", p=P)[:, cols], ring[:, 0, :, of].bitcast(I32),
                                     allow_slow_non_contiguous=True).then_inc(g_st.sem, g_st.add())
                    sp.dma_start(EW_D.rearrange("(p c) -> p c", p=P)[:, cols], ring[:, 0, :, A_DIM + D + 2],
                                 allow_slow_non_contiguous=True).then_inc(g_st.sem, g_st.add())
                    sp.dma_start(EA48_D.rearrange("(p c) d -> p c d", p=P)[:, cols, :], ring[:, 0, :, 0:D]
                                 ).then_inc(g_st.sem, g_st.add())
                    sp.wait_ge(g_ea.sem, g_ea.up())
                    sp.dma_start(EA40_D[:, cols, :], eaG.rearrange("a (c p) -> a c p", p=P)
                                 ).then_inc(g_st.sem, g_st.add())
                    sp.wait_ge(g_st.sem, g_st.now())
                    sp.sem_inc(S["g_free"], 1)
                for table, name in ((SRC_D, "src"), (DST_D, "dst")):
                    for at in (0, EP + 1):
                        sp.dma_start(table[at:at + 1], A[name][at:at + 1]).then_inc(g_st.sem, g_st.add())
                sp.wait_ge(g_st.sem, g_st.now())

            def load_edges(src, dst, weight, ea):
                n, m = edges.n, ea48.n
                for to, of in ((srcI[:, :], src[1:EP + 1]), (dstI[:, :], dst[1:EP + 1]),
                               (t0[:, :].bitcast(I32), dst[2:EP + 2]), (cnt[:, :].bitcast(I32), dst[0:EP]),
                               (ew, weight)):
                    sp.dma_start(to, of.rearrange("(p c) -> p c", p=P)).then_inc(edges.sem, edges.add())
                sp.dma_start(vb[0:SORT_P, :].bitcast(I32), src[1:EP + 1].rearrange("(p c) -> p c", p=SORT_P)
                             ).then_inc(edges.sem, edges.add())
                sp.dma_start(M, ea.rearrange("(p c) d -> p c d", p=P)).then_inc(ea48.sem, ea48.add())
                edges.n, ea48.n = n, m

            sp.wait_ge(S["flag"], 1)
            unsorted = sp.value_load(flag[0:1, 0:1], min_val=0, max_val=1)
            with sp.If(unsorted != 0):
                sort_edges()
                load_edges(SRC_D, DST_D, EW_D, EA48_D)
            with sp.Else():
                load_edges(A["src"], A["dst"], A["ew"], A["ea48"])

            ld, st = views("ld0", "ld1"), views("st0", "st1")
            xld = views("xa_ld0", "xa_ld1")
            col_ready, = views("col_ready")

            def xa_load(h, k):
                sp.dma_start(din[:, h, :], blk(A["xaux"], k, XW).rearrange("p c d -> p (c d)")
                    ).then_inc(xld[h].sem, xld[h].add())

            def xa_store(h, k):
                sp.wait_ge(col_ready.sem, col_ready.up())
                sp.dma_start(blk(XA, k, XW).rearrange("p c d -> p (c d)"), din[:, h, :]
                    ).then_inc(st[h].sem, st[h].add())

            xa_load(0, 0)
            xa_load(1, 1)
            with loop(sp, DBLK // 2 - 1, {xld[0]: 1, xld[1]: 1, st[0]: 1, st[1]: 1, col_ready: 2}) as i:
                for h in range(2):
                    xa_store(h, 2 * i + h)
                for h in range(2):
                    sp.wait_ge(st[h].sem, st[h].now())
                    xa_load(h, 2 * i + 2 + h)
            for h in range(2):
                xa_store(h, DBLK - 2 + h)
            for h in range(2):
                sp.wait_ge(st[h].sem, st[h].now())
            sp.sem_inc(S["xa_done"], 1)

            srt_ready, srt_st, srt_ld = views("srt_ready", "srt_st", "srt_ld")
            sp.wait_ge(srt_ready.sem, srt_ready.up())
            sp.dma_start(SRT[1:P * SORT_C + 1].rearrange("(p c) -> p c", p=P), vb[:, :].bitcast(I32)
                ).then_inc(srt_st.sem, srt_st.add())
            sp.dma_start(SRT[0:1].rearrange("(p c) -> p c", p=1), zero1[0:1, 0:1].bitcast(I32)
                ).then_inc(srt_st.sem, srt_st.add())
            sp.wait_ge(srt_st.sem, srt_st.now())

            in_free, out_ready = views("in_free", "out_ready")

            def load(h, k, table, w):
                sp.wait_ge(in_free.sem, in_free.up())
                sp.dma_start(din[:, h, 0:R * w], blk(table, k, w).rearrange("p c d -> p (c d)")
                    ).then_inc(ld[h].sem, ld[h].add())

            def store(h, k, tables):
                sp.wait_ge(out_ready.sem, out_ready.up())
                for buf, table in tables:
                    sp.dma_start(blk(table, k), buf[:, h, :, :]).then_inc(st[h].sem, st[h].add())

            def dense(table, w, tables, before=None):
                if before:
                    before()
                for h in range(2):
                    load(h, h, table, w)
                with loop(sp, DBLK // 2 - 1, {ld[0]: 1, ld[1]: 1, in_free: 2, out_ready: 2,
                                              st[0]: len(tables), st[1]: len(tables)}) as i:
                    for h in range(2):
                        load(h, 2 * i + 2 + h, table, w)
                    for h in range(2):
                        store(h, 2 * i + h, tables)
                for h in range(2):
                    store(h, DBLK - 2 + h, tables)
                for h in range(2):
                    sp.wait_ge(st[h].sem, st[h].now())
                sp.sem_inc(S["short_done"], 1)

            dense(A["xaux"], XW, [(do, X1), (dy, Y1)])
            dense(X1, D, [(do, X2)])

            mld, (mfree,) = views("mlp_ld0", "mlp_ld1", "mlp_ld2", "mlp_ld3"), views("mlp_free")

            def edge_features(of):
                before = [m.n for m in mld + [mfree]]
                with loop(sp, NBLK, {mld[0]: 2, mld[1]: 2, mld[2]: 2, mld[3]: 1, mfree: R // 4}) as i:
                    for g in range(R // 4):
                        sp.wait_ge(mfree.sem, mfree.up())
                        sp.dma_start(eaT[g], of[:, bass.ds(i * (R // 4) + g, 1), :].rearrange("a g w -> a (g w)")
                                     ).then_inc(mld[g % 4].sem, mld[g % 4].add())
                for m, n in zip(mld + [mfree], before):
                    m.n = n
            with sp.If(unsorted != 0):
                edge_features(EA40_D.rearrange("a (g c) p -> a g (c p)", c=4))
            with sp.Else():
                edge_features(A["ea40T"])

            rec_ready, rec_st = views("rec_ready", "rec_st")
            recv = REC.rearrange("(p c) w -> p c w", p=P)
            sp.wait_ge(rec_ready.sem, rec_ready.up())
            sp.dma_start(recv[:, :, D:RW], GX[:, :, :]).then_inc(rec_st.sem, rec_st.add())
            sp.wait_ge(srt_ready.sem, srt_ready.up())
            for at, to in ((1, zs), (2, zd), (0, cnt)):
                sp.dma_start(to[:, :].bitcast(I32), SRT[at:at + EP].rearrange("(p c) -> p c", p=P)
                    ).then_inc(srt_ld.sem, srt_ld.add())
            with loop(sp, NBLK, {rec_ready: 1, rec_st: 1}) as i:
                cols = bass.ds(i * R, R)
                sp.wait_ge(rec_ready.sem, rec_ready.up())
                sp.dma_start(recv[:, cols, 0:D], M[:, cols, :]).then_inc(rec_st.sem, rec_st.add())
            s_done, = views("s_done")

            def scattered():
                sp.wait_ge(s_done.sem, s_done.up(2))
            dense(X2, D, [(do, X3), (do, X3C)], scattered)
            dense(X3C, D, [(do, OUT)])
            sp.wait_ge(s_done.sem, s_done.up(2))

        @block.gpsimd
        def _(pool):
            own, = views("pool")
            fill, sc = views("fill0", "fill1"), views("sc0", "sc1")
            ring_free, rows_ready = views("ring_free", "rows_ready")
            idx_ready, short_done, edges, rec_st = views("idx_ready", "short_done", "edges", "rec_st")
            last_row = pool.to_reg(NP - 1)

            def indices(h, c, of):
                nc.gpsimd.tensor_copy(idx[:, h, :], of[:, bass.ds(c * H, H)]).then_inc(own.sem, own.add())
                pool.wait_ge(own.sem, own.now())
                pool.sem_inc(S["pool_turns"], 1)

            def gather(table, w, of):
                with loop(pool, NBLK, {own: 2, ring_free: 2, fill[0]: H, fill[1]: H}) as i:
                    for h in range(2):
                        pool.wait_ge(ring_free.sem, ring_free.up())
                        indices(h, 2 * i + h, of)
                        for t in range(H):
                            pool.indirect_dma_start(
                                ring[:, h, t, 0:w], None, table,
                                bass.IndirectOffsetOnAxis(ap=idx[:, h, t:t + 1], axis=0)
                                    ).then_inc(fill[h].sem, fill[h].add())
                for h in range(2):
                    pool.wait_ge(fill[h].sem, fill[h].now())

            def scatter_turn(table, c, h, first):
                pool.wait_ge(rows_ready.sem, rows_ready.up())
                indices(h, c, put)
                for t in range(H):
                    pool.indirect_dma_start(
                        table, bass.IndirectOffsetOnAxis(ap=idx[:, h, t:t + 1], axis=0),
                        stage[:, h, t, :], None, bounds_check=last_row, oob_is_err=False
                            ).then_inc(sc[h].sem, sc[h].add())
                    if t == H // 2 and not first:
                        pool.wait_ge(sc[1 - h].sem, sc[1 - h].now())
                        pool.sem_inc(S["stage_free"], 1)

            def scatter(table):
                scatter_turn(table, 0, 0, True)
                scatter_turn(table, 1, 1, False)
                with loop(pool, NBLK - 1, {own: 2, rows_ready: 2, sc[0]: H, sc[1]: H}) as i:
                    scatter_turn(table, 2 * i + 2, 0, False)
                    scatter_turn(table, 2 * i + 3, 1, False)
                pool.wait_ge(sc[1].sem, sc[1].now())
                pool.sem_inc(S["stage_free"], 1)
                pool.sem_inc(S["s_done"], 1)

            def sort_edges():
                g_own, g_fill, g_free = views("g_pool", "g_fill", "g_free")
                pool.wait_ge(S["g_places"], 1)
                with loop(pool, CE // H, {g_own: 1, g_fill: H, g_free: 1}) as c:
                    nc.gpsimd.tensor_copy(idx[:, 0, :], srcI[:, bass.ds(c * H, H)]).then_inc(g_own.sem, g_own.add())
                    pool.wait_ge(g_own.sem, g_own.now())
                    pool.sem_inc(S["pool_turns"], 1)
                    for t in range(H):
                        pool.indirect_dma_start(
                            ring[:, 0, t, 0:EW], None, A["erec"],
                            bass.IndirectOffsetOnAxis(ap=idx[:, 0, t:t + 1], axis=0)).then_inc(g_fill.sem, g_fill.add())
                    pool.wait_ge(g_fill.sem, g_fill.now())
                    pool.sem_inc(S["g_rows"], 1)
                    pool.wait_ge(g_free.sem, g_free.up())

            pool.wait_ge(S["flag"], 1)
            unsorted = pool.value_load(flag[0:1, 0:1], min_val=0, max_val=1)
            with pool.If(unsorted != 0):
                sort_edges()
            pool.wait_ge(edges.sem, edges.up(6))
            gather(A["xaux"], XW, srcI)
            pool.wait_ge(S["xa_done"], 1)
            gather(XA, XW, dstI)
            pool.wait_ge(idx_ready.sem, idx_ready.up())
            pool.wait_ge(short_done.sem, short_done.up())
            scatter(Y1)
            gather(Y1, D, srcI)
            pool.wait_ge(short_done.sem, short_done.up())
            scatter(X2)
            pool.wait_ge(idx_ready.sem, idx_ready.up())
            gather(X2, D, srcI)
            pool.wait_ge(rec_st.sem, rec_st.up(1 + NBLK))
            pool.wait_ge(idx_ready.sem, idx_ready.up())
            gather(REC, RW, dstI)
            pool.wait_ge(short_done.sem, short_done.up())
            pool.wait_ge(idx_ready.sem, idx_ready.up())
            scatter(X3)
            gather(X3, D, dstS)
            pool.wait_ge(short_done.sem, short_done.up())
            scatter(OUT)

        @block.scalar
        def _(act):
            own, = views("act")
            fill = views("fill0", "fill1")
            spread, returned = views("spread", "returned")
            centered, var_ready, xs_free, rows_new, stage_free, scanned = views(
                "centered", "var_ready", "xs_free", "rows_new", "stage_free", "scanned")
            trans, ask = views("trans", "ask_act")
            act.wait_ge(S["init"], 1)
            act.wait_ge(S["consts"], 16 * 17)
            act.sem_inc(S["ring_free"], 2)
            act.sem_inc(S["stage_free"], 2)

            def before(c, h):
                nc.scalar.activation(terms[:, h, :, 0:1],
                                     MG[:, bass.ds(c * H, 1), :].rearrange("p c d -> p d c"), ACT.Copy
                                     ).then_inc(spread.sem, spread.add())
                nc.scalar.activation(mask[:, :, 1:H + 1],
                                     cont[:, bass.ds(c * H, H)].unsqueeze(1).broadcast_to([P, D, H]),
                                     ACT.Copy).then_inc(spread.sem, spread.add())

            def take_terms(c, h, uses=()):
                act.wait_ge(fill[h].sem, fill[h].up(H))
                for to, of in uses:
                    nc.scalar.activation(to, of, ACT.Copy).then_inc(own.sem, own.add())
                nc.scalar.activation(terms[:, h, :, 1:H + 1], ring[:, h, :, 0:D].rearrange("p c d -> p d c"), ACT.Copy
                                     ).then_inc(spread.sem, spread.add())
                act.wait_ge(own.sem, own.now())
                act.wait_ge(spread.sem, spread.now())
                act.sem_inc(S["ring_free"], 1)
                before(c, h)

            def give_back(c, h):
                act.wait_ge(scanned.sem, scanned.up())
                nc.scalar.activation(M[:, bass.ds(c * H, H), :],
                                     sums[:, h, :, 1:H + 1].rearrange("p d c -> p c d"), ACT.Copy
                                     ).then_inc(returned.sem, returned.add())
                act.wait_ge(returned.sem, returned.now())

            def take(h, uses):
                act.wait_ge(fill[h].sem, fill[h].up(H))
                for to, of in uses:
                    nc.scalar.activation(to, of, ACT.Copy).then_inc(own.sem, own.add())
                act.wait_ge(own.sem, own.now())
                act.sem_inc(S["ring_free"], 1)
                act.sem_inc(S["kept"], 1)

            def squares(units):
                for h, u in units:
                    act.wait_ge(centered.sem, centered.up())
                    nc.scalar.activation(sq[:, h, :, :], u, ACT.Square).then_inc(S["squared"], 1)

            def roots(units, scale=1.0 / D):
                for h, u in units:
                    act.wait_ge(var_ready.sem, var_ready.up())
                    nc.scalar.activation(std[:, h, :], var[:, h, :], ACT.Sqrt, bias=lneps[:, 0:1],
                                         scale=scale).then_inc(S["std_ready"], 1)

            def norm(units, scale=1.0 / D):
                squares(units)
                roots(units, scale)

            def evacuate(groups=range(4)):
                for g in groups:
                    w = 256 if g == 3 else 512
                    act.wait_ge(trans.sem, trans.up())
                    nc.scalar.activation(hT[0:96, g % 2, 0:w], psT[g % 2][0:96, 0:w], ACT.Copy
                                         ).then_inc(S["hT_ready"], 1)

            def to_stage(of, i):
                act.wait_ge(rows_new.sem, rows_new.up())
                for h in range(2):
                    act.wait_ge(stage_free.sem, stage_free.up())
                    nc.scalar.activation(stage[:, h, :, :], of[:, bass.ds((2 * i + h) * H, H), :], ACT.Copy
                                         ).then_inc(S["rows_ready"], 1)

            def function(of, what=ACT.Sqrt):
                act.wait_ge(ask.sem, ask.up())
                nc.scalar.activation(of, of, what).then_inc(S["act_done"], 1)

            pair = [(0, du[:, 0, :, :]), (1, du[:, 1, :, :])]

            xld = views("xa_ld0", "xa_ld1")

            def source_rows(c, h):
                cols = bass.ds(c * H, H)
                take(h, [(XS[:, cols, :], ring[:, h, :, 0:D]),
                         (zs[:, cols], ring[:, h, :, D + 1].bitcast(I32))])

            def degrees(k):
                for h in range(2):
                    act.wait_ge(xld[h].sem, xld[h].up())
                    nc.scalar.activation(din[:, h, :].rearrange("p (c w) -> p c w", w=XW)[:, :, D + 3],
                                         deg[:, bass.ds((k + h) * R, R)], ACT.Copy).then_inc(S["col_ready"], 1)

            with loop(act, 3, {own: 4, fill[0]: H, fill[1]: H}) as i:
                for h in range(2):
                    source_rows(2 * i + h, h)
            act.wait_ge(S["deg_done"], 1)
            with loop(act, 3, {own: 4, fill[0]: H, fill[1]: H, xld[0]: 4, xld[1]: 4}) as i:
                for h in range(2):
                    degrees(8 * i + 4 * h)
                    degrees(8 * i + 4 * h + 2)
                    source_rows(2 * i + 6 + h, h)
            for h in range(2):
                degrees(24 + 2 * h)
                source_rows(12 + h, h)
            function(deg[:, :])

            with loop(act, NBLK, {own: 8, fill[0]: H, fill[1]: H, xs_free: 2, centered: PER, var_ready: PER}) as i:
                for h in range(2):
                    norm(pair, c2s[:, 0:1])
                    act.wait_ge(xs_free.sem, xs_free.up())
                    cols = bass.ds((2 * i + h) * H, H)
                    take(h, [(XS[:, cols, :], ring[:, h, :, 0:D]),
                             (nv[:, cols], ring[:, h, :, D]),
                             (zd[:, cols], ring[:, h, :, D + 1].bitcast(I32)),
                             (dg[:, cols], ring[:, h, :, D + 3])])

            function(t0[:, :])
            with loop(act, NBLK, {centered: 1, var_ready: 1}) as i:
                norm([(0, su[:, :, :])])

            def short1(i, last=False):
                to_stage(M, i)
                for q in range(PER // 2):
                    ahead = not (last and q == PER // 2 - 1)
                    evacuate()
                    if ahead:
                        evacuate((0, 1))
                    squares(pair)
                    if ahead:
                        evacuate((2, 3))
                    roots(pair)
            evacuate()
            with loop(act, NBLK - 1, {stage_free: 2, rows_new: 1, centered: PER, var_ready: PER, trans: 4 * PER}) as i:
                short1(i)
            short1(NBLK - 1, True)

            function(t1[:, :], ACT.Sin)
            mt, = views("mlp_t")
            mfree = S["mlp_free"]

            def one_hots():
                act.wait_ge(mt.sem, mt.up())
                nc.scalar.activation(zT, psO[0][0:Z, 0:256].bitcast(BF16), ACT.Copy).then_inc(S["mlp_a"], 1)

            def factors(i, last=False):
                take_terms(2 * i, 0)
                for g in range(R // 4):
                    act.wait_ge(mt.sem, mt.up())
                    act.sem_inc(mfree, 1)
                    nc.scalar.activation(h1T[0:D, :], psA[0:D, :], ACT.Silu, bias=bm1[:, 0:1]).then_inc(S["mlp_a"], 1)
                    if not (last and g == R // 4 - 1):
                        one_hots()
                    if g == 2:
                        give_back(2 * i, 0)
                        take_terms(2 * i + 1, 1)
                give_back(2 * i + 1, 1)

            one_hots()
            with loop(act, NBLK - 1, {mt: 2 * R // 4, fill[0]: H, fill[1]: H, spread: 6, scanned: 2, returned: 2}) as i:
                factors(i)
            factors(NBLK - 1, True)

            function(t0[:, :])
            function(t1[:, :])
            def update():
                evacuate()
                norm(pair[:1])

            with loop(act, 4, {stage_free: 2, rows_new: 1, centered: 1, var_ready: 1, trans: 4}) as i:
                update()
                to_stage(XS, i)
            update()
            update()
            to_stage(XS, 4)
            update()
            to_stage(XS, 5)
            to_stage(XS, 6)

            with loop(act, NBLK, {own: 2, fill[0]: H, fill[1]: H, centered: PER, var_ready: PER}) as i:
                for h in range(2):
                    cols = bass.ds((2 * i + h) * H, H)
                    take(h, [(XS[:, cols, :], ring[:, h, :, 0:D])])
                for _ in range(PER // 2):
                    norm(pair)

            function(deg[:, :])

            with loop(act, NBLK, {own: 4, scanned: 2, spread: 6, returned: 2, fill[0]: H, fill[1]: H,
                                  centered: 2, var_ready: 2}) as i:
                norm(pair)
                for h in range(2):
                    cols = bass.ds((2 * i + h) * H, H)
                    take_terms(2 * i + h, h, [(GX[:, cols, 0:D + 1], ring[:, h, :, D:RW - 1]),
                                              (dstS[:, cols], ring[:, h, :, RW - 1].bitcast(I32))])
                    give_back(2 * i + h, h)

            function(t0[:, :])
            with loop(act, NBLK, {stage_free: 2, rows_new: 1, centered: 1, var_ready: 1, trans: 4}) as i:
                evacuate()
                norm(pair[:1])
                to_stage(XS, i)

            with loop(act, NBLK, {scanned: 2, spread: 4, returned: 2, centered: 2, var_ready: 2}) as i:
                norm(pair)
                for h in range(2):
                    before(2 * i + h, h)
                    give_back(2 * i + h, h)

            with loop(act, NBLK, {stage_free: 2, rows_new: 1, centered: 2, var_ready: 2}) as i:
                norm([(0, su[:, :, :])])
                norm([(0, su[:, :, :])])
                to_stage(XS, i)

        @block.tensor
        def _(pe):
            T = nc.tensor
            hot, ask, h_ready, hT_ready, mm_used = views("hot", "ask_pe", "h_ready", "hT_ready", "mm_used")
            ld = views("ld0", "ld1")
            pe.wait_ge(S["consts"], 16 * 17)
            pe.wait_ge(S["init"], 1)

            def flip():
                pe.wait_ge(ask.sem, ask.up())
                T.transpose(psG[0:D + 1, 0:P], tail[:, :], ident[:, :]).then_inc(S["pe_done"], 1)

            def flip_back(at):
                pe.wait_ge(ask.sem, ask.up())
                T.transpose(psG[:, P:P + D + 1], shT[:, at:at + P], ident[0:D + 1, 0:D + 1]).then_inc(S["pe_done"], 1)

            def product(blocks, weights):
                def turn(k):
                    rows_of, h = blocks[k // 4]
                    g = k % 4
                    if g == 0 and h is not None:
                        pe.wait_ge(ld[h].sem, ld[h].up())
                    for j in range(2 if g == 3 else 4):
                        last = T.transpose(psT[g % 2][0:96, j * P:(j + 1) * P],
                                           rows_of[:, (4 * g + j) * 96:(4 * g + j + 1) * 96], ident[:, :])
                    last.then_inc(S["trans"], 1)

                turn(0)
                turn(1)
                for k in range(4 * len(blocks)):
                    g = k % 4
                    pe.wait_ge(hT_ready.sem, hT_ready.up())
                    used = mm_used.up()
                    if k < 2:
                        pe.wait_ge(mm_used.sem, used)
                    elif k >= 6:
                        pe.wait_ge(mm_used.sem, used - 4)
                    for j in range(2 if g == 3 else 4):
                        last = T.matmul(psO[k % 6][:, j * 96:(j + 1) * 96], hT[0:97, g % 2, j * P:(j + 1) * P],
                                        weights[:, :], start=True, stop=True)
                    last.then_inc(S["mm"], 1)
                    if k + 2 < 4 * len(blocks):
                        turn(k + 2)

            def sort_edges():
                g_ask, g_rows, g_copied = views("g_ask", "g_rows", "g_copied")
                for n in sort_turns()[0]:
                    pe.wait_ge(g_ask.sem, g_ask.up())
                    for h in range(2):
                        last = T.transpose(psT[0][:, h * P:(h + 1) * P], (vb, va)[n][:, h * P:(h + 1) * P], ident[:, :])
                    last.then_inc(S["g_turned"], 1)
                with loop(pe, CE // H, {g_rows: 1, g_copied: H}) as c:
                    pe.wait_ge(g_rows.sem, g_rows.up())
                    pe.sem_inc(S["pe_turns"], 1)
                    for t in range(H):
                        pe.wait_ge(g_copied.sem, g_copied.up())
                        pe.sem_inc(S["pe_turns"], 1)
                        T.transpose(psT[0][0:A_DIM, 0:P], ring[:, 0, t, D:D + A_DIM], ident[:, :]
                                    ).then_inc(S["g_trans"], 1)

            flip()
            pe.wait_ge(S["flag"], 1)
            unsorted = pe.value_load(flag[0:1, 0:1], min_val=0, max_val=1)
            with pe.If(unsorted != 0):
                sort_edges()
            T.matmul(psG[0:G, 0:Z], adT, embT, start=True, stop=True).then_inc(S["pe_done"], 1)
            pe.wait_ge(ask.sem, ask.up())
            T.matmul(psG[0:Z, 0:Z], embT, aez, start=True, stop=True).then_inc(S["pe_done"], 1)
            flip()
            flip()

            pe.sem_inc(S["counted"], 4)

            def count_edges(g, start, stop):
                pe.wait_ge(hot.sem, hot.up())
                for c in range(2):
                    last = T.matmul((psA, psB)[c][:, 0:CN // 2], ohp[:, g, :],
                                    ohc[:, g, c * (CN // 2):(c + 1) * (CN // 2)],
                                    start=start, stop=stop, skip_group_check=True)
                last.then_inc(S["counted"], 1)
            for g in range(4):
                count_edges(g, g == 0, False)
            with loop(pe, CE // 4 - 2, {hot: 4}) as i:
                for g in range(4):
                    count_edges(g, False, False)
            for g in range(4):
                count_edges(g, False, g == 3)

            for n in sort_turns()[0]:
                pe.wait_ge(ask.sem, ask.up())
                for h in range(2):
                    last = T.transpose(psT[0][:, h * P:(h + 1) * P], (vb, va)[n][:, h * P:(h + 1) * P], ident[:, :])
                last.then_inc(S["pe_done"], 1)

            flip()
            flip_back(0)
            for h in range(2):
                ld[h].n = 16 * DBLK // 2
            with loop(pe, NBLK, {ld[0]: PER // 2, ld[1]: PER // 2, hT_ready: 4 * PER, mm_used: 4 * PER}) as i:
                for _ in range(PER // 2):
                    product([(din[:, h, :], h) for h in range(2)], w1b)

            hots, ma, mused = views("hots", "mlp_a", "mlp_used")
            mld = views("mlp_ld0", "mlp_ld1", "mlp_ld2", "mlp_ld3")

            def one_hots(g):
                pe.wait_ge(hots.sem, hots.up())
                pe.sem_inc(S["pe_turns"], 1)
                for j in range(4):
                    last = T.transpose(psO[0][0:Z, 0:256].bitcast(BF16)[:, j * P:(j + 1) * P],
                                       ohs[:, OH[g], j, :], identb[:, :])
                last.then_inc(S["mlp_t"], 1)

            def factors(last_block=False):
                for g in range(R // 4):
                    bank = (psB, psC, psB, psC, psB, psC, psO[1])[g]
                    pe.wait_ge(ma.sem, ma.up())
                    pe.wait_ge(mused.sem, mused.up())
                    pe.sem_inc(S["pe_turns"], 1)
                    for j in range(4):
                        for part in range(3):
                            last = T.matmul(bank[:, j * Z:(j + 1) * Z], zT[:, j * P:(j + 1) * P], logit[:, part, :],
                                            start=part == 0, stop=part == 2)
                    last.then_inc(S["mlp_o"], 1)
                    pe.wait_ge(mld[g % 4].sem, mld[g % 4].up())
                    pe.sem_inc(S["pe_turns"], 1)
                    T.matmul(psA[0:D, :], wm1[:, :], eaT[g], start=True, stop=True).then_inc(S["mlp_t"], 1)
                    if not (last_block and g == R // 4 - 1):
                        one_hots((g + 1) % (R // 4))
                    pe.wait_ge(ma.sem, ma.up())
                    for j in range(4):
                        last = T.matmul((psG, psT[1], psG, psT[1], psG, psT[1], psT[0])[g][:, j * D:(j + 1) * D],
                                        h1T[:, j * P:(j + 1) * P], wm2[:, :], start=True, stop=True)
                    last.then_inc(S["mlp_g"], 1)

            one_hots(0)
            with loop(pe, NBLK - 1, {hots: R // 4, mld[0]: 2, mld[1]: 2, mld[2]: 2, mld[3]: 1, ma: 2 * R // 4,
                                     mused: R // 4}) as i:
                factors()
            factors(True)

            flip()
            flip_back(0)
            su_rows = su[:, :, :].rearrange("p c d -> p (c d)")

            def products(weights):
                with loop(pe, NBLK, {h_ready: 1, hT_ready: 4, mm_used: 4}) as i:
                    pe.wait_ge(h_ready.sem, h_ready.up())
                    product([(su_rows, None)], weights)
            products(w1b)
            flip()
            flip_back(1)
            flip()
            flip()
            flip_back(0)
            products(w2b)
            flip()
            flip_back(0)

        @block.vector
        def _(dve):
            V = nc.vector
            own, = views("dve")

            def one(instruction):
                instruction.then_inc(own.sem, own.add())
                dve.wait_ge(own.sem, own.now())

            def along(t, w=D):
                return t.unsqueeze(2).broadcast_to([P, t.shape[1], w])

            def down(t, n=R):
                return t.unsqueeze(1).broadcast_to([P, n, t.shape[1]])

            act_done, pe_done = views("act_done", "pe_done")
            ld, st, xld = views("ld0", "ld1"), views("st0", "st1"), views("xa_ld0", "xa_ld1")
            squared, std_ready, kept, mm, counted = views("squared", "std_ready", "kept", "mm", "counted")
            mm_used, spread, returned = views("mm_used", "spread", "returned")
            fill = views("fill0", "fill1")

            def ask_act():
                dve.sem_inc(S["ask_act"], 1)
                dve.wait_ge(act_done.sem, act_done.up())

            def ask_pe():
                dve.sem_inc(S["ask_pe"], 1)
                dve.wait_ge(pe_done.sem, pe_done.up())

            V.memset(hT[:, :, :], 1.0).then_inc(own.sem, own.add())
            V.memset(lneps[:, :], EPS).then_inc(own.sem, own.add())
            V.memset(zero1[:, :], 0.0).then_inc(own.sem, own.add())
            V.memset(mask[:, :, 0:1], 0.0).then_inc(own.sem, own.add())
            V.memset(MG[:, 0:1, :], 0.0).then_inc(own.sem, own.add())
            dve.wait_ge(S["consts"], 16 * 17)
            one(V.tensor_scalar(c2e[:, :], c2e[:, :], 2.0, None, ALU.add))
            one(V.tensor_scalar(rows[:, 0, :], rows[:, 0, :], 0.0, None, ALU.max))
            dve.sem_inc(S["init"], 1)
            dve.sem_inc(mm_used.sem, mm_used.up(2))
            dve.sem_inc(S["in_free"], 2)
            dve.wait_ge(S["look"], 32)
            V.tensor_copy(key[:, :], dstI[:, :]).then_inc(own.sem, own.add())
            one(V.tensor_copy(keyn[:, :], t0[:, :].bitcast(I32)))
            one(V.tensor_tensor(end[:, :], key[:, :], keyn[:, :], ALU.is_gt))
            one(V.tensor_reduce(carry[:, 0:1], end[:, :], X, ALU.add))
            one(V.tensor_copy(tail[:, :], carry[:, 0:1].broadcast_to([P, D + 1])))
            ask_pe()
            one(V.tensor_reduce(carry[0:1, 1:2], psG[0:1, 0:P], X, ALU.add))
            one(V.tensor_scalar(carry[0:1, 1:2], carry[0:1, 1:2], 1.5, None, ALU.is_gt))
            one(V.tensor_copy(flag[:, 0:1], carry[0:1, 1:2]))
            dve.sem_inc(S["flag"], 1)

            def sort(own, turn):
                def one(instruction):
                    instruction.then_inc(own.sem, own.add())
                    dve.wait_ge(own.sem, own.now())

                one(V.tensor_copy(va[0:SORT_P, :], vb[0:SORT_P, :].bitcast(I32)))
                one(V.memset(vb[96:P, :], 3.4028234e38))
                one(V.tensor_scalar(vb[0:SORT_P, :], va[0:SORT_P, :], float(HALF_NODES), float(65536 - HALF_NODES),
                                    ALU.is_ge, ALU.mult))
                one(V.scalar_tensor_tensor(va[0:SORT_P, :], va[0:SORT_P, :], 256.0, vb[0:SORT_P, :], ALU.add, ALU.add))
                vi = vb[0:SORT_P, :].bitcast(I32)
                one(V.tensor_copy(vi, va[0:SORT_P, :]))
                one(V.tensor_scalar(vi, vi, 15, None, ALU.logical_shift_left))
                one(V.tensor_tensor(vi, vi, pos[0:SORT_P, :], ALU.bitwise_or))
                now = [vb, va]

                def compare(d):
                    (lo, hi), (a, b) = ([v[:, :].rearrange("p (b two d) -> p b two d", two=2, d=d)[:, :, j, :]
                                         for j in range(2)] for v in now)
                    V.tensor_tensor(a, lo, hi, ALU.min).then_inc(own.sem, own.add())
                    one(V.tensor_tensor(b, lo, hi, ALU.max))
                    now.reverse()

                def turned():
                    turn()
                    one(V.tensor_copy(now[1][:, :], psT[0][:, 0:SORT_C]))
                    now.reverse()

                def negate(m):
                    v = now[0][:, :].rearrange("p (b two d) -> p b two d", two=2, d=1 << m)[:, :, 1, :]
                    one(V.tensor_scalar(v, v, -1.0, None, ALU.mult))

                for m in range(1, 16):
                    if m >= 9:
                        one(V.tensor_scalar(now[0][:, :], now[0][:, :], psgn[:, m - 8:m - 7], None, ALU.mult))
                    elif m == 8:
                        negate(7)
                        one(V.tensor_scalar(now[0][:, :], now[0][:, :], psgn[:, 0:1], None, ALU.mult))
                    else:
                        if m > 1:
                            negate(m - 1)
                        negate(m)
                    if m > 8:
                        turned()
                        for b in range(m - 9, -1, -1):
                            compare(1 << b)
                        turned()
                    for b in range(min(m, 8) - 1, -1, -1):
                        compare(1 << b)
                assert now[0] is vb

            def sort_edges():
                g_own, g_turned, g_trans, g_copied = views("g_dve", "g_turned", "g_trans", "g_copied")

                def turn():
                    dve.sem_inc(S["g_ask"], 1)
                    dve.wait_ge(g_turned.sem, g_turned.up())

                dve.wait_ge(S["g_ld"], 16)
                sort(g_own, turn)
                dve.sem_inc(S["g_sorted"], 1)
                dve.wait_ge(S["g_ld"], 48)
                V.tensor_scalar(srcI[:, :], srcI[:, :], 0x7FFF, None, ALU.bitwise_and).then_inc(g_own.sem, g_own.add())
                dve.wait_ge(g_own.sem, g_own.now())
                dve.sem_inc(S["g_places"], 1)
                dve.sem_inc(g_copied.sem, g_copied.up())
                with loop(dve, CE // H, {g_trans: H, g_copied: H}) as c:
                    for t in range(H):
                        dve.wait_ge(g_trans.sem, g_trans.up())
                        V.tensor_copy(eaG[:, t * P:(t + 1) * P], psT[0][0:A_DIM, 0:P]
                            ).then_inc(g_copied.sem, g_copied.add())
                    dve.wait_ge(g_copied.sem, g_copied.now())
                    dve.sem_inc(S["g_ea"], 1)

            unsorted = dve.value_load(flag[0:1, 0:1], min_val=0, max_val=1)
            with dve.If(unsorted != 0):
                sort_edges()
            dve.wait_ge(pe_done.sem, pe_done.up())
            one(V.tensor_copy(aez, psG[0:G, 0:Z]))
            ask_pe()
            one(V.tensor_copy(pair_f, psG[0:Z, 0:Z]))
            for part in range(3):
                one(V.tensor_copy(logit[:, part, :], pair_f))
                if part < 2:
                    one(V.tensor_copy(part_f, logit[:, part, :]))
                    one(V.tensor_tensor(pair_f, pair_f, part_f, ALU.subtract))

            def flipped(to, column):
                one(V.tensor_copy(tail[:, :], column.broadcast_to([P, D + 1])))
                ask_pe()
                one(V.tensor_copy(to[:, :], psG[0:D + 1, 0:P]))

            def order(key, after, before):
                V.tensor_tensor(end[:, :], key, after, ALU.not_equal).then_inc(own.sem, own.add())
                one(V.tensor_tensor(cont[:, :], key, before, ALU.is_equal))
                V.tensor_scalar(carry[:, 0:1], end[:, CE - 1:CE], -1.0, 1.0, ALU.mult, ALU.add
                    ).then_inc(own.sem, own.add())
                one(V.tensor_scalar(pre[:, :], key, key[:, 0:1], cont[:, 0:1], ALU.is_equal, ALU.mult))
                one(V.tensor_scalar(suf[:, :], key, key[:, CE - 1:CE], carry[:, 0:1], ALU.is_equal, ALU.mult))
                flipped(fullT, pre[:, CE - 1:CE])

            def writers(node):
                one(V.tensor_scalar(t0[:, :], end[:, :], -SKIP, SKIP, ALU.mult, ALU.add))
                one(V.tensor_tensor(t0[:, :], t0[:, :], node, ALU.add))
                one(V.tensor_copy(put[:, :], t0[:, :]))
                dve.sem_inc(S["idx_ready"], 1)

            dve.wait_ge(S["edges"], 16 * 6)
            V.tensor_copy(key[:, :], dstI[:, :]).then_inc(own.sem, own.add())
            V.tensor_copy(keyn[:, :], t0[:, :].bitcast(I32)).then_inc(own.sem, own.add())
            one(V.tensor_copy(dg[:, :], cnt[:, :].bitcast(I32)))
            order(key[:, :], keyn[:, :], dg[:, :])
            flipped(restT, suf[:, 0:1])
            writers(key[:, :])

            one(V.tensor_copy(colf, srcI[:, :]))
            one(V.tensor_scalar(tmpf, colf, 1.0 / CN, None, ALU.mult))
            one(V.tensor_copy(keyn[:, :].bitcast(I32), tmpf))
            one(V.tensor_copy(parf, keyn[:, :].bitcast(I32)))
            one(V.scalar_tensor_tensor(colf, parf, -float(CN), colf, ALU.mult, ALU.add))
            one(V.tensor_scalar(tmpf, colf, 0.0, None, ALU.is_lt))
            V.tensor_tensor(parf, parf, tmpf, ALU.subtract).then_inc(own.sem, own.add())
            one(V.scalar_tensor_tensor(colf, tmpf, float(CN), colf, ALU.mult, ALU.add))
            one(V.tensor_scalar(tmpf, colf, float(CN), None, ALU.is_ge))
            V.tensor_tensor(parf, parf, tmpf, ALU.add).then_inc(own.sem, own.add())
            one(V.scalar_tensor_tensor(colf, tmpf, -float(CN), colf, ALU.mult, ALU.add))
            with loop(dve, CE // R, {counted: R}) as i:
                for t in range(R):
                    g = t % 4
                    dve.wait_ge(counted.sem, counted.up())
                    V.tensor_scalar(ohp[:, g, :], iota[:, 0:P], parf[:, bass.ds(i * R + t, 1)], None, ALU.is_equal)
                    V.tensor_scalar(ohc[:, g, :], iota[:, :], colf[:, bass.ds(i * R + t, 1)], None, ALU.is_equal
                                    ).then_inc(S["hot"], 1)
            dve.wait_ge(counted.sem, counted.up(4))
            V.tensor_copy(deg[:, 0:CN // 2], psA[:, 0:CN // 2]).then_inc(own.sem, own.add())
            one(V.tensor_copy(deg[:, CN // 2:CN], psB[:, 0:CN // 2]))
            dve.sem_inc(S["deg_done"], 1)

            mask_row, terms_row, sums_row = (t.rearrange("p d c -> p (d c)") for t in (
                mask[:, :, :], terms[:, :, :, :].rearrange("p h d c -> p (h d) c"),
                sums[:, :, :, :].rearrange("p h d c -> p (h d) c")))

            def scan(h):
                part = slice(h * D * (H + 1), (h + 1) * D * (H + 1))
                return V.tensor_tensor_scan(sums_row[:, part], mask_row, terms_row[:, part], 0.0, ALU.mult, ALU.add)

            def summed(h, parts=3):
                dve.wait_ge(spread.sem, spread.up(parts))
                scan(h).then_inc(S["scanned"], 1)

            sort(own, ask_pe)
            dve.sem_inc(S["srt_ready"], 1)

            dve.wait_ge(S["ea48"], 16)
            with loop(dve, 2 * NBLK, {own: 6, kept: 1}) as i:
                dve.wait_ge(kept.sem, kept.up())
                cols = bass.ds(i * H, H)
                V.tensor_tensor(terms[:, 0, :, 1:H + 1].rearrange("p d c -> p c d"), M[:, cols, :], XS[:, cols, :],
                                ALU.add
                                ).then_inc(own.sem, own.add())
                V.tensor_copy(mask[:, :, 1:H + 1], cont[:, cols].unsqueeze(1).broadcast_to([P, D, H])
                              ).then_inc(own.sem, own.add())
                one(V.tensor_copy(terms[:, 0, :, 0:1], MG[:, bass.ds(i * H, 1), :].rearrange("p c d -> p d c")))
                one(V.tensor_scalar(terms[:, 0, :, 1:H + 1], terms[:, 0, :, 1:H + 1], 0.0, None, ALU.max))
                one(scan(0))
                dve.sem_inc(S["xs_free"], 1)
                one(V.tensor_copy(M[:, cols, :], sums[:, 0, :, 1:H + 1].rearrange("p d c -> p c d")))
            for h in range(2):
                st[h].n = 16 * DBLK // 2
                dve.wait_ge(st[h].sem, st[h].now())
            one(V.tensor_scalar(deg[:, :], deg[:, :], 1.0, None, ALU.max))
            ask_act()
            one(V.reciprocal(deg[:, :], deg[:, :]))

            def counts(of):
                one(V.tensor_tensor_scan(cnt[:, :], cont[:, :], of, 0.0, ALU.mult, ALU.add))

            def carries(with_counts):
                V.memset(shT[:, 0:1], 0.0).then_inc(own.sem, own.add())
                V.tensor_copy(tail[:, 0:D], M[:, CE - 1, :]).then_inc(own.sem, own.add())
                one(V.tensor_copy(tail[:, D:D + 1], cnt[:, CE - 1:CE]))
                ask_pe()
                one(V.tensor_copy(tailT[:, :], psG[0:D + 1, 0:P]))
                one(V.tensor_tensor_scan(shT[:, 1:P + 1], fullT[:, :], tailT[:, :], 0.0, ALU.mult, ALU.add))
                ask_pe()
                one(V.tensor_copy(carry[:, :], psG[:, P:P + D + 1]))
                if with_counts:
                    one(V.scalar_tensor_tensor(cnt[:, :], pre[:, :], carry[:, D:D + 1], cnt[:, :], ALU.mult, ALU.add))

            def carried(cols, mask=pre, n=R):
                one(V.tensor_tensor(su[:, :, :], along(mask[:, cols]), down(carry[:, 0:D]), ALU.mult))
                one(V.tensor_tensor(M[:, cols, :], M[:, cols, :], su[:, :, :], ALU.add))

            def norm(units, factor=None, free=False, stores=False, keep=None):
                for h, x, u, out in units:
                    V.tensor_reduce(mu[:, h, :], x, X, ALU.add).then_inc(own.sem, own.add())
                dve.wait_ge(own.sem, own.now())
                for h, x, u, out in units:
                    V.scalar_tensor_tensor(u, along(mu[:, h, :]), -1.0 / D, x, ALU.mult, ALU.add
                                           ).then_inc(S["centered"], 1)
                for h, x, u, out in units:
                    dve.wait_ge(squared.sem, squared.up())
                    if free:
                        dve.sem_inc(S["in_free"], 1)
                    V.tensor_reduce(var[:, h, :], sq[:, h, :, :], X, ALU.add).then_inc(S["var_ready"], 1)
                for h, x, u, out in units:
                    dve.wait_ge(std_ready.sem, std_ready.up())
                    V.reciprocal(srs[:, h, :], std[:, h, :]).then_inc(own.sem, own.add())
                    if keep:
                        V.tensor_copy(keep(h), var[:, h, :]).then_inc(own.sem, own.add())
                dve.wait_ge(own.sem, own.now())
                for h, x, u, out in units:
                    if stores:
                        dve.wait_ge(st[h].sem, st[h].now())
                    if factor is None:
                        V.tensor_tensor(out, u, along(srs[:, h, :]), ALU.mult).then_inc(own.sem, own.add())
                    else:
                        V.scalar_tensor_tensor(out, u, factor, along(srs[:, h, :]), ALU.mult, ALU.mult
                                               ).then_inc(own.sem, own.add())
                dve.wait_ge(own.sem, own.now())

            NORM1, NORM2 = 3, 6
            DU = [du[:, h, :, :] for h in range(2)]
            DO = [do[:, h, :, :] for h in range(2)]
            pair = [(h, DU[h], DU[h], DO[h]) for h in range(2)]

            def wide(h, w):
                return din[:, h, 0:R * w].rearrange("p (c w) -> p c w", w=w)[:, :, 0:D]

            one(V.memset(t0[:, :], 1.0))
            counts(t0[:, :])
            carries(True)
            one(V.scalar_tensor_tensor(c2s[:, :], c2e[:, :], 1.0 / D, c2e[:, :], ALU.mult, ALU.mult))
            with loop(dve, NBLK, {own: 2 * NORM2, ld[0]: 2, ld[1]: 2, st[0]: 4, st[1]: 4,
                                  squared: PER, std_ready: PER}) as i:
                for q in range(PER // 2):
                    for h in range(2):
                        dve.wait_ge(ld[h].sem, ld[h].up())
                    norm([(h, wide(h, XW), DU[h], DO[h]) for h in range(2)], factor=c2e[:, 0:1], free=True, stores=True)
                    for h in range(2):
                        V.tensor_tensor(dy[:, h, :, :], DO[h],
                                        along(deg[:, bass.ds((PER * i + 2 * q + h) * R, R)]), ALU.mult
                                        ).then_inc(S["out_ready"], 1)
                        st[h].n += 32

            dve.wait_ge(kept.sem, kept.up(2 * NBLK))
            one(V.tensor_scalar(t0[:, :], dg[:, :], 1.0, None, ALU.max))
            ask_act()
            one(V.reciprocal(t0[:, :], t0[:, :]))
            with loop(dve, NBLK, {own: 4 + NORM1, squared: 1, std_ready: 1}) as i:
                cols = bass.ds(i * R, R)
                carried(cols)
                one(V.scalar_tensor_tensor(su[:, :, :], XS[:, cols, :], c2e[:, 0:1], M[:, cols, :], ALU.mult, ALU.add))
                norm([(0, su[:, :, :], su[:, :, :], XS[:, cols, :])])
                one(V.tensor_tensor(M[:, cols, :], XS[:, cols, :], along(t0[:, cols]), ALU.mult))
                dve.sem_inc(S["rows_new"], 1)

            def taken(h, x):
                for g in range(4):
                    n = 4 if g == 3 else 8
                    dve.wait_ge(mm.sem, mm.up())
                    V.scalar_tensor_tensor(DU[h][:, 8 * g:8 * g + n, :],
                                           psO[(4 * h + g) % 6][:, 0:n * D].rearrange("p (c d) -> p c d", d=D), 0.0,
                                           x(g, n), ALU.max, ALU.add).then_inc(mm_used.sem, mm_used.add())

            with loop(dve, NBLK, {own: 2 * NORM2, mm: 16, mm_used: 16, ld[0]: 2, ld[1]: 2, st[0]: 2, st[1]: 2,
                                  squared: PER, std_ready: PER}) as i:
                for q in range(PER // 2):
                    for h in range(2):
                        dve.wait_ge(ld[h].sem, ld[h].up())
                        taken(h, lambda g, n: wide(h, D)[:, 8 * g:8 * g + n, :])
                        dve.wait_ge(mm_used.sem, mm_used.now())
                        dve.sem_inc(S["in_free"], 1)
                    norm(pair, stores=True)
                    for h in range(2):
                        st[h].n += 16
                    dve.sem_inc(S["out_ready"], 2)

            for h in range(2):
                dve.wait_ge(st[h].sem, st[h].now())
            V.tensor_copy(zbs, zs[:, :]).then_inc(own.sem, own.add())
            V.tensor_copy(zbd, zd[:, :]).then_inc(own.sem, own.add())
            V.memset(h1T, 1.0).then_inc(own.sem, own.add())
            one(V.tensor_scalar(t0[:, :], ew[:, :], 6.0, 0.5, ALU.is_lt, ALU.mult))
            one(V.tensor_scalar(t1[:, :], ew[:, :], 0.0, 6.0, ALU.max, ALU.min))
            one(V.tensor_scalar(t1[:, :], t1[:, :], -3.14159265358979 / 6, 3.14159265358979 / 2, ALU.mult, ALU.add))
            ask_act()
            one(V.scalar_tensor_tensor(t1[:, :], t1[:, :], 1.0, t0[:, :], ALU.add, ALU.mult))
            one(V.tensor_tensor(t1[:, :], t1[:, :], nv[:, :], ALU.mult))
            dve.sem_inc(S["mlp_free"], 3)
            dve.sem_inc(S["mlp_used"], 2)
            mo, mg = views("mlp_o", "mlp_g")

            def one_hots(slot, g):
                for oh, types in ((ohs, zbs), (ohd, zbd)):
                    V.tensor_tensor(oh[:, OH[g], :, :], down(iotaz[:, :], 4), along(types[:, bass.ds(slot, 4)], Z),
                                    ALU.is_equal).then_inc(own.sem, own.add())
                dve.wait_ge(own.sem, own.now())
                dve.sem_inc(S["hots"], 1)

            def factors(i, last=False):
                for g in range(R // 4):
                    if not (last and g == R // 4 - 1):
                        one_hots(i * R + 4 * (g + 1), (g + 1) % (R // 4))
                    if g in (0, 4):
                        summed(g // 4)
                    c4 = bass.ds(i * R + 4 * g, 4)
                    dve.wait_ge(mo.sem, mo.up())
                    one(V.tensor_tensor(prod, (psB, psC, psB, psC, psB, psC, psO[1])[g][:, 0:4 * Z].rearrange(
                        "p (c z) -> p c z", z=Z), ohd[:, OH[g], :, :], ALU.mult))
                    one(V.tensor_reduce(lg[:, :], prod, X, ALU.add))
                    dve.wait_ge(mg.sem, mg.up())
                    one(V.tensor_tensor(gsum, (psG, psT[1], psG, psT[1], psG, psT[1], psT[0])[g][:, 0:4 * D].rearrange(
                        "p (c d) -> p c d", d=D), along(lg[:, :]), ALU.add))
                    dve.sem_inc(S["mlp_used"], 1)
                    one(V.tensor_tensor(GX[:, c4, 0:D], gsum, along(t1[:, c4]), ALU.mult))

            one_hots(0, 0)
            with loop(dve, NBLK - 1, {own: 6 * R // 4, mo: R // 4, mg: R // 4, spread: 6}) as i:
                factors(i)
            factors(NBLK - 1, True)
            dve.wait_ge(returned.sem, returned.up(2 * NBLK))
            V.tensor_copy(GX[:, :, D], nv[:, :]).then_inc(own.sem, own.add())
            one(V.tensor_copy(GX[:, :, D + 1].bitcast(I32), dstI[:, :]))
            dve.sem_inc(S["rec_ready"], 1)

            carries(False)
            one(V.tensor_scalar(t0[:, :], cnt[:, :], 1.0, None, ALU.max))
            dve.sem_inc(S["srt_ready"], 1)
            ask_act()
            one(V.reciprocal(t0[:, :], t0[:, :]))
            one(V.tensor_scalar(t1[:, :], dg[:, :], 1.0, None, ALU.max))
            ask_act()
            one(V.reciprocal(t1[:, :], t1[:, :]))
            one(V.tensor_scalar(dg[:, :], dg[:, :], 1.0, None, ALU.min))
            one(V.tensor_tensor(t1[:, :], t1[:, :], dg[:, :], ALU.mult))

            def update_by_product():
                with loop(dve, NBLK, {own: 2 + 1 + NORM1, mm: 4, mm_used: 4, squared: 1, std_ready: 1}) as i:
                    cols = bass.ds(i * R, R)
                    carried(cols)
                    one(V.tensor_tensor(su[:, :, :], M[:, cols, :], along(t0[:, cols]), ALU.mult))
                    dve.sem_inc(S["h_ready"], 1)
                    taken(0, lambda g, n: XS[:, bass.ds(i * R + 8 * g, n), :])
                    dve.wait_ge(mm_used.sem, mm_used.now())
                    norm([(0, DU[0], DU[0], XS[:, cols, :])])
                    dve.sem_inc(S["rows_new"], 1)
            update_by_product()

            one(V.tensor_tensor(M, XS[:, :, :], along(end[:, :]), ALU.mult))

            dve.wait_ge(S["srt_ld"], 16 * 3)
            V.tensor_copy(dstS[:, :], zs[:, :].bitcast(I32)).then_inc(own.sem, own.add())
            one(V.tensor_scalar(zs[:, :].bitcast(I32), zs[:, :].bitcast(I32), 15, None, ALU.logical_shift_right))
            one(V.tensor_copy(zs[:, :], zs[:, :].bitcast(I32)))
            one(V.tensor_scalar(keyn[:, :], zs[:, :], 65536.0, -float(65536 - HALF_NODES), ALU.is_ge, ALU.mult))
            one(V.scalar_tensor_tensor(key[:, :], zs[:, :], -256.0, keyn[:, :], ALU.add, ALU.add))
            one(V.tensor_copy(srcI[:, :], key[:, :]))
            dve.sem_inc(S["idx_ready"], 1)

            one(V.tensor_scalar(t0[:, :], end[:, :], -1.0, 1.0, ALU.mult, ALU.add))
            for f in range(D):
                V.tensor_tensor_scan(M[:, ::-1, f], t0[:, ::-1], M[:, ::-1, f], 0.0, ALU.mult, ALU.add
                    ).then_inc(own.sem, own.add())
            dve.wait_ge(own.sem, own.now())
            V.memset(shT[:, P:P + 1], 0.0).then_inc(own.sem, own.add())
            one(V.tensor_copy(tail[:, 0:D], M[:, 0, :]))
            ask_pe()
            one(V.tensor_copy(tailT[:, :], psG[0:D + 1, 0:P]))
            one(V.tensor_tensor_scan(shT[:, 0:P][:, ::-1], restT[:, ::-1], tailT[:, ::-1], 0.0, ALU.mult, ALU.add))
            ask_pe()
            one(V.tensor_copy(carry[:, :], psG[:, P:P + D + 1]))
            with loop(dve, NBLK, {own: 3}) as i:
                cols = bass.ds(i * R, R)
                carried(cols, suf)
                one(V.tensor_tensor(M[:, cols, :], M[:, cols, :], along(t1[:, cols]), ALU.mult))
                dve.sem_inc(S["rec_ready"], 1)

            dve.wait_ge(S["srt_ld"], 16 * 3)
            one(V.tensor_scalar(dstI[:, :], dstS[:, :], 0x7FFF, None, ALU.bitwise_and))
            dve.sem_inc(S["idx_ready"], 1)
            for t in (zd, cnt):
                V.tensor_scalar(t[:, :].bitcast(I32), t[:, :].bitcast(I32), 15, None, ALU.logical_shift_right
                    ).then_inc(own.sem, own.add())
            dve.wait_ge(own.sem, own.now())
            V.tensor_copy(keyn[:, :], zd[:, :].bitcast(I32)).then_inc(own.sem, own.add())
            one(V.tensor_copy(dg[:, :], cnt[:, :].bitcast(I32)))
            order(zs[:, :], keyn[:, :], dg[:, :])
            dve.wait_ge(S["s_done"], 2)
            writers(key[:, :])
            one(V.memset(t0[:, :], 1.0))
            counts(t0[:, :])

            with loop(dve, NBLK, {own: 2 * (4 + NORM2), ld[0]: 2, ld[1]: 2, st[0]: 4, st[1]: 4,
                                  squared: PER, std_ready: PER}) as i:
                for q in range(PER // 2):
                    for h in range(2):
                        dve.wait_ge(ld[h].sem, ld[h].up())
                        V.tensor_tensor(DU[h], wide(h, D), down(rows[:, 0, :]), ALU.add).then_inc(own.sem, own.add())
                    dve.wait_ge(own.sem, own.now())
                    dve.sem_inc(S["in_free"], 2)
                    norm(pair, stores=True, keep=lambda h: deg[:, bass.ds((PER * i + 2 * q + h) * R, R)])
                    for h in range(2):
                        st[h].n += 32
                    dve.sem_inc(S["out_ready"], 2)

            mid = DU[0].rearrange("p c d -> p (c d)")[:, 0:CN]
            one(V.tensor_scalar(mid, deg[:, :], D * EPS, None, ALU.add))
            one(V.reciprocal(mid, mid))
            one(V.tensor_tensor(deg[:, :], deg[:, :], mid, ALU.mult))
            one(V.tensor_scalar(deg[:, :], deg[:, :], EPS, None, ALU.add))
            ask_act()
            one(V.reciprocal(deg[:, :], deg[:, :]))

            def short3(i):
                for h in range(2):
                    dve.wait_ge(ld[h].sem, ld[h].up())
                    V.tensor_tensor(DU[h], along(deg[:, bass.ds((2 * i + h) * R, R)]), down(rows[:, 1, :]), ALU.mult
                                    ).then_inc(own.sem, own.add())
                dve.wait_ge(own.sem, own.now())
                for h in range(2):
                    V.scalar_tensor_tensor(DU[h], DU[h], 1.0, wide(h, D), ALU.add, ALU.mult
                        ).then_inc(own.sem, own.add())
                dve.wait_ge(own.sem, own.now())
                dve.sem_inc(S["in_free"], 2)
                for h in range(2):
                    V.tensor_tensor(DU[h], DU[h], down(rows[:, 2, :]), ALU.add).then_inc(own.sem, own.add())
                dve.wait_ge(own.sem, own.now())
                norm(pair, stores=True)
                for h in range(2):
                    st[h].n += 16
                dve.sem_inc(S["out_ready"], 2)

            short = {ld[0]: 1, ld[1]: 1, st[0]: 1, st[1]: 1, squared: 2, std_ready: 2}
            with loop(dve, NBLK, {own: NORM2 + 6, spread: 6, **short}) as i:
                short3(i)
                summed(0)
                summed(1)
            dve.wait_ge(returned.sem, returned.up(2 * NBLK))

            dve.wait_ge(kept.sem, kept.up(CE // H))
            carries(True)
            one(V.tensor_copy(t0[:, :], cnt[:, :]))
            ask_act()
            one(V.reciprocal(t0[:, :], t0[:, :]))
            update_by_product()

            for h in range(2):
                fill[h].n = 5 * CE // 2 * 16
            with loop(dve, NBLK, {own: 2 + NORM2 + 6, fill[0]: H, fill[1]: H, spread: 4, **short}) as i:
                short3(i + NBLK)
                for h in range(2):
                    dve.wait_ge(fill[h].sem, fill[h].up(H))
                    one(V.tensor_tensor(terms[:, h, :, 1:H + 1].rearrange("p d c -> p c d"), ring[:, h, :, 0:D],
                                        GX[:, bass.ds((2 * i + h) * H, H), 0:D], ALU.mult))
                    dve.sem_inc(S["ring_free"], 1)
                    summed(h, 2)
            dve.wait_ge(returned.sem, returned.up(2 * NBLK))
            one(V.tensor_copy(nv[:, :], GX[:, :, D]))
            counts(nv[:, :])
            carries(True)
            one(V.tensor_scalar(t0[:, :], cnt[:, :], 1e-8, None, ALU.max))
            one(V.reciprocal(t0[:, :], t0[:, :]))

            with loop(dve, NBLK, {own: 2 + 2 + 3 + 2 * NORM1, squared: 2, std_ready: 2}) as i:
                cols = bass.ds(i * R, R)
                carried(cols)
                one(V.tensor_tensor(su[:, :, :], M[:, cols, :], along(t0[:, cols]), ALU.mult))
                one(V.tensor_tensor(su[:, :, :], su[:, :, :], XS[:, cols, :], ALU.add))
                norm([(0, su[:, :, :], su[:, :, :], su[:, :, :])])
                one(V.tensor_tensor(su[:, :, :], su[:, :, :], down(rows[:, 1, :]), ALU.mult))
                one(V.tensor_tensor(su[:, :, :], su[:, :, :], down(rows[:, 2, :]), ALU.add))
                one(V.tensor_tensor(su[:, :, :], su[:, :, :], XS[:, cols, :], ALU.add))
                norm([(0, su[:, :, :], su[:, :, :], XS[:, cols, :])])
                dve.sem_inc(S["rows_new"], 1)


def kernel(**inputs):
    import ml_dtypes
    import numpy as np
    from concourse import bacc
    from concourse.bass_utils import run_bass_kernel_spmd

    f = {k: np.asarray(v) for k, v in inputs.items()}
    f32 = np.float32

    def padded(a, rows, width):
        out = np.zeros((rows, width), a.dtype)
        out[:a.shape[0], :a.shape[1]] = a
        return out

    def edges(a):
        return np.concatenate([[-1], a, np.full(EP - E, NP - 1), [-1]]).astype(np.int32)

    def twice(w, b):
        out = np.zeros((97, 96), f32)
        out[0:D, 0:D] = w.T
        out[D:96, D:96] = w.T
        out[96, 0:D] = b
        out[96, D:96] = b
        return out

    xaux = np.zeros((NP, XW), f32)
    xaux[:N, 0:D] = f["x"]
    xaux[:N, D] = f["node_vec"]
    xaux[:N, D + 1] = f["node_type_119"].astype(np.int32).view(f32)
    erec = np.zeros((EP, EW), f32)
    erec[:E, 0:D] = f["edge_attr_48"]
    erec[:E, D:D + A_DIM] = f["edge_attr_40"]
    erec[:, D + A_DIM] = edges(f["src"])[1:EP + 1].view(f32)
    erec[:, D + A_DIM + 1] = edges(f["dst"])[1:EP + 1].view(f32)
    erec[:E, D + A_DIM + 2] = f["edge_weight"]
    place = np.arange(P)
    psgn = np.ones((P, 8), f32)
    psgn[:, 0] = 1 - 2 * (place & 1)
    for m in range(9, 16):
        now = (place >> (m - 8)) & 1 if m < 15 else 0
        psgn[:, m - 8] = (1 - 2 * now) * (1 - 2 * ((place >> (m - 9)) & 1))
    arrays = {
        "xaux": xaux,
        "erec": erec, "src": edges(f["src"]), "dst": edges(f["dst"]),
        "ea48": padded(f["edge_attr_48"], EP, D), "ea40T": np.ascontiguousarray(
            padded(f["edge_attr_40"], EP, A_DIM).reshape(P, CE // 4, 4, A_DIM).transpose(3, 1, 2, 0)
        ).reshape(A_DIM, CE // 4, 4 * P),
        "ew": padded(f["edge_weight"][:, None], EP, 1)[:, 0],
        "iota": np.tile(np.arange(CN, dtype=np.int16), (P, 1)),
        "iotaz": np.tile(np.arange(Z), (P, 1)).astype(ml_dtypes.bfloat16),
        "ident": np.eye(P, dtype=f32), "identb": np.eye(P).astype(ml_dtypes.bfloat16),
        "w1b": twice(f["L1_gnn_W"], f["L1_gnn_b"]), "w2b": twice(f["L2_gnn_W"], f["L2_gnn_b"]),
        "wm1": np.ascontiguousarray(f["L3_gnn_W1"].T), "bm1": f["L3_gnn_b1"][:, None],
        "wm2": np.concatenate([f["L3_gnn_W2"].T, f["L3_gnn_b2"][None]]),
        "embT": np.ascontiguousarray(padded(f["L3_gnn_emb"], Z, G).T),
        "adT": np.ascontiguousarray(f["L3_gnn_adaptW"].T),
        "psgn": psgn, "pos": np.arange(P * SORT_C, dtype=np.int32).reshape(P, SORT_C),
        "b2": f["L2_gnn_b"][None], "gamma": f["L3_gnn_gamma"][None], "beta": f["L3_gnn_beta"][None],
        "eps": f["L0_gnn_eps"][None],
    }
    nc = bacc.Bacc("TRN2", target_bir_lowering=False, num_devices=1)
    aps = {k: nc.dram_tensor(f"in_{k}", a.shape, mybir.dt.from_np(a.dtype), kind="ExternalInput").ap()
           for k, a in arrays.items()}
    out = nc.dram_tensor("out", [NP, D], F32, kind="ExternalOutput").ap()
    bass_gnn(nc, aps, out)
    r = run_bass_kernel_spmd(nc, [{f"in_{k}": a for k, a in arrays.items()}], core_ids=[0])
    return r.results[0]["out"][:N]
```
